# Optimizing a Trainium2 kernel written in Bass

```python
import numpy as np
import jax
import jax.numpy as jnp

def _softmax(x, axis=-1):
    return jax.nn.softmax(x, axis=axis)

def _gelu(x):
    return jax.nn.gelu(x, approximate=True)

def _silu(x):
    return jax.nn.silu(x)

def _sigmoid(x):
    return jax.nn.sigmoid(x)

def _layernorm(x, axis=-1, eps=1e-05):
    m = jnp.mean(x, axis=axis, keepdims=True)
    v = jnp.var(x, axis=axis, keepdims=True)
    return (x - m) / jnp.sqrt(v + eps)

def _scatter_add(tgt, idx, src, axis=0):
    return tgt.at[idx].add(src)

def _segment_sum(src, seg, n):
    return jax.ops.segment_sum(src, seg, n)
kernel_name = 'mk_conv_attn_hybrid_d2_conv_nchw256_r2_608108'

def setup_inputs(seed: int=0):
    np.random.seed(seed)
    _w = jnp.asarray

    def _rec_inputs():
        import jax
        import jax.numpy as jnp
        _gk = jax.random.key(seed)
        x = 7.22e-05 + 1 * jax.random.normal(jax.random.fold_in(_gk, 1), (8, 128, 32, 32), jnp.float32)
        return x
    x = _rec_inputs()

    def _L0_conv_setup():
        import jax, jax.numpy as jnp
        import numpy as np
        key = jax.random.key(seed)
        ks = jax.random.split(key, 4)
        B, C, H, W = (8, 128, 32, 32)
        Cq = C // 8
        x = jax.random.normal(ks[0], (B, C, H, W), dtype=jnp.float32)
        wq = jax.random.normal(ks[1], (Cq, C), dtype=jnp.float32) * (1.0 / np.sqrt(C))
        bq = jnp.zeros((Cq,), dtype=jnp.float32)
        wk = jax.random.normal(ks[2], (Cq, C), dtype=jnp.float32) * (1.0 / np.sqrt(C))
        bk = jnp.zeros((Cq,), dtype=jnp.float32)
        wv = jax.random.normal(ks[3], (C, C), dtype=jnp.float32) * (1.0 / np.sqrt(C))
        bv = jnp.zeros((C,), dtype=jnp.float32)
        return {'x': x, 'wq': wq, 'bq': bq, 'wk': wk, 'bk': bk, 'wv': wv, 'bv': bv}
    _L0_conv_all = _L0_conv_setup()
    _L0_conv_in = {k: v for k, v in _L0_conv_all.items() if k in ('wq', 'bq', 'wk', 'bk', 'wv', 'bv')}
    del _L0_conv_all

    def _L1_attn_setup():
        import jax, jax.numpy as jnp
        import numpy as np
        DIM = 128
        H_GLOBAL = 8
        H_LOCAL = 4
        WINDOW = 5
        HALF = WINDOW // 2
        B, S = (4, 1024)
        EPS = 1e-05

        def layer_norm(x, g, b):
            mu = jnp.mean(x, axis=-1, keepdims=True)
            var = jnp.mean(jnp.square(x - mu), axis=-1, keepdims=True)
            return (x - mu) * jax.lax.rsqrt(var + EPS) * g + b

        def qkv_proj(x, in_w, in_b):
            qkv = x @ in_w.T + in_b
            return jnp.split(qkv, 3, axis=-1)

        def global_mha(x, in_w, in_b, out_w, out_b, nh):
            Bq, Sq, D = x.shape
            hd = D // nh
            q, k, v = qkv_proj(x, in_w, in_b)
            q = q.reshape(Bq, Sq, nh, hd)
            k = k.reshape(Bq, Sq, nh, hd)
            v = v.reshape(Bq, Sq, nh, hd)
            scores = jnp.einsum('bqhd,bkhd->bhqk', q, k) / np.sqrt(hd).astype(np.float32)
            attn = jax.nn.softmax(scores, axis=-1)
            o = jnp.einsum('bhqk,bkhd->bqhd', attn, v).reshape(Bq, Sq, D)
            return o @ out_w.T + out_b

        def local_mha(x, in_w, in_b, out_w, out_b, nh):
            Bq, Sq, D = x.shape
            hd = D // nh
            q, k, v = qkv_proj(x, in_w, in_b)
            kp = jnp.pad(k, ((0, 0), (HALF, HALF), (0, 0)))
            vp = jnp.pad(v, ((0, 0), (HALF, HALF), (0, 0)))
            k_win = jnp.stack([kp[:, j:j + Sq] for j in range(WINDOW)], axis=2)
            v_win = jnp.stack([vp[:, j:j + Sq] for j in range(WINDOW)], axis=2)
            q = q.reshape(Bq, Sq, nh, hd)
            k_win = k_win.reshape(Bq, Sq, WINDOW, nh, hd)
            v_win = v_win.reshape(Bq, Sq, WINDOW, nh, hd)
            scores = jnp.einsum('bshd,bswhd->bshw', q, k_win) / np.sqrt(hd).astype(np.float32)
            idx = jnp.arange(Sq)[:, None] + jnp.arange(-HALF, HALF + 1)[None, :]
            valid = (idx >= 0) & (idx < Sq)
            scores = jnp.where(valid[None, :, None, :], scores, -jnp.inf)
            attn = jax.nn.softmax(scores, axis=-1)
            o = jnp.einsum('bshw,bswhd->bshd', attn, v_win).reshape(Bq, Sq, D)
            return o @ out_w.T + out_b
        key = jax.random.key(seed)
        ks = jax.random.split(key, 8)
        sc = 0.02
        d = DIM
        return {'x': jax.random.normal(ks[0], (B, S, d), jnp.float32), 'g_in_w': jax.random.normal(ks[1], (3 * d, d), jnp.float32) * sc, 'g_in_b': jnp.zeros((3 * d,), jnp.float32), 'g_out_w': jax.random.normal(ks[2], (d, d), jnp.float32) * sc, 'g_out_b': jnp.zeros((d,), jnp.float32), 't_in_w': jax.random.normal(ks[3], (3 * d, d), jnp.float32) * sc, 't_in_b': jnp.zeros((3 * d,), jnp.float32), 't_out_w': jax.random.normal(ks[4], (d, d), jnp.float32) * sc, 't_out_b': jnp.zeros((d,), jnp.float32), 'fus_w1': jax.random.normal(ks[5], (2 * d, 2 * d), jnp.float32) * sc, 'fus_b1': jnp.zeros((2 * d,), jnp.float32), 'fus_w2': jax.random.normal(ks[6], (d, 2 * d), jnp.float32) * sc, 'fus_b2': jnp.zeros((d,), jnp.float32), 'ffn_w1': jax.random.normal(ks[7], (2 * d, d), jnp.float32) * sc, 'ffn_b1': jnp.zeros((2 * d,), jnp.float32), 'ffn_w2': jax.random.normal(jax.random.fold_in(key, 9), (d, 2 * d), jnp.float32) * sc, 'ffn_b2': jnp.zeros((d,), jnp.float32), 'gn_g': jnp.ones((d,), jnp.float32), 'gn_b': jnp.zeros((d,), jnp.float32), 'fn_g': jnp.ones((d,), jnp.float32), 'fn_b': jnp.zeros((d,), jnp.float32)}
    _L1_attn_all = _L1_attn_setup()
    _L1_attn_in = {k: v for k, v in _L1_attn_all.items() if k in ('g_in_w', 'g_in_b', 'g_out_w', 'g_out_b', 't_in_w', 't_in_b', 't_out_w', 't_out_b', 'fus_w1', 'fus_b1', 'fus_w2', 'fus_b2', 'ffn_w1', 'ffn_b1', 'ffn_w2', 'ffn_b2', 'gn_g', 'gn_b', 'fn_g', 'fn_b')}
    del _L1_attn_all

    def _L1_ffn_setup():
        import math
        import jax, jax.numpy as jnp
        import numpy as np
        CAPACITY_FACTOR = 1.25
        key = jax.random.key(seed)
        ks = jax.random.split(key, 5)
        B, L, D, F, E = (8, 4096, 128, 512, 8)
        h = jax.random.normal(ks[0], (B, L, D), dtype=jnp.float32)
        gate_w = jax.random.normal(ks[1], (D, E), dtype=jnp.float32) * 0.02
        gate_b = jnp.zeros((E,), dtype=jnp.float32)
        w1 = jax.random.normal(ks[2], (E, D, F), dtype=jnp.float32) * (1.0 / math.sqrt(D))
        b1 = jnp.zeros((E, F), dtype=jnp.float32)
        w2 = jax.random.normal(ks[3], (E, F, D), dtype=jnp.float32) * (1.0 / math.sqrt(F))
        b2 = jnp.zeros((E, D), dtype=jnp.float32)
        return {'h': h, 'gate_w': gate_w, 'gate_b': gate_b, 'w1': w1, 'b1': b1, 'w2': w2, 'b2': b2}
    _L1_ffn_all = _L1_ffn_setup()
    _L1_ffn_in = {k: v for k, v in _L1_ffn_all.items() if k in ('gate_w', 'gate_b', 'w1', 'b1', 'w2', 'b2')}
    del _L1_ffn_all
    return {'x': x, 'L0_conv_wq': _L0_conv_in['wq'], 'L0_conv_bq': _L0_conv_in['bq'], 'L0_conv_wk': _L0_conv_in['wk'], 'L0_conv_bk': _L0_conv_in['bk'], 'L0_conv_wv': _L0_conv_in['wv'], 'L0_conv_bv': _L0_conv_in['bv'], 'L1_attn_g_in_w': _L1_attn_in['g_in_w'], 'L1_attn_g_in_b': _L1_attn_in['g_in_b'], 'L1_attn_g_out_w': _L1_attn_in['g_out_w'], 'L1_attn_g_out_b': _L1_attn_in['g_out_b'], 'L1_attn_t_in_w': _L1_attn_in['t_in_w'], 'L1_attn_t_in_b': _L1_attn_in['t_in_b'], 'L1_attn_t_out_w': _L1_attn_in['t_out_w'], 'L1_attn_t_out_b': _L1_attn_in['t_out_b'], 'L1_attn_fus_w1': _L1_attn_in['fus_w1'], 'L1_attn_fus_b1': _L1_attn_in['fus_b1'], 'L1_attn_fus_w2': _L1_attn_in['fus_w2'], 'L1_attn_fus_b2': _L1_attn_in['fus_b2'], 'L1_attn_ffn_w1': _L1_attn_in['ffn_w1'], 'L1_attn_ffn_b1': _L1_attn_in['ffn_b1'], 'L1_attn_ffn_w2': _L1_attn_in['ffn_w2'], 'L1_attn_ffn_b2': _L1_attn_in['ffn_b2'], 'L1_attn_gn_g': _L1_attn_in['gn_g'], 'L1_attn_gn_b': _L1_attn_in['gn_b'], 'L1_attn_fn_g': _L1_attn_in['fn_g'], 'L1_attn_fn_b': _L1_attn_in['fn_b'], 'L1_ffn_gate_w': _L1_ffn_in['gate_w'], 'L1_ffn_gate_b': _L1_ffn_in['gate_b'], 'L1_ffn_w1': _L1_ffn_in['w1'], 'L1_ffn_b1': _L1_ffn_in['b1'], 'L1_ffn_w2': _L1_ffn_in['w2'], 'L1_ffn_b2': _L1_ffn_in['b2']}

def reference(x, L0_conv_wq, L0_conv_bq, L0_conv_wk, L0_conv_bk, L0_conv_wv, L0_conv_bv, L1_attn_g_in_w, L1_attn_g_in_b, L1_attn_g_out_w, L1_attn_g_out_b, L1_attn_t_in_w, L1_attn_t_in_b, L1_attn_t_out_w, L1_attn_t_out_b, L1_attn_fus_w1, L1_attn_fus_b1, L1_attn_fus_w2, L1_attn_fus_b2, L1_attn_ffn_w1, L1_attn_ffn_b1, L1_attn_ffn_w2, L1_attn_ffn_b2, L1_attn_gn_g, L1_attn_gn_b, L1_attn_fn_g, L1_attn_fn_b, L1_ffn_gate_w, L1_ffn_gate_b, L1_ffn_w1, L1_ffn_b1, L1_ffn_w2, L1_ffn_b2):
    import jax
    import jax.numpy as jnp

    def _L0_conv_ref(x, wq, bq, wk, bk, wv, bv):
        import jax, jax.numpy as jnp
        import numpy as np
        B, C, H, W = x.shape
        N = H * W
        xf = x.reshape(B, C, N)
        q = jnp.einsum('bcn,dc->bnd', xf, wq) + bq
        k = jnp.einsum('bcn,dc->bdn', xf, wk) + bk[:, None]
        v = jnp.einsum('bcn,dc->bdn', xf, wv) + bv[:, None]
        energy = jnp.einsum('bnd,bdm->bnm', q, k)
        attn = jax.nn.softmax(energy, axis=-1)
        out = jnp.einsum('bcj,bij->bci', v, attn).reshape(B, C, H, W)
        return x + out

    def _L1_attn_ref(x, g_in_w, g_in_b, g_out_w, g_out_b, t_in_w, t_in_b, t_out_w, t_out_b, fus_w1, fus_b1, fus_w2, fus_b2, ffn_w1, ffn_b1, ffn_w2, ffn_b2, gn_g, gn_b, fn_g, fn_b):
        import jax, jax.numpy as jnp
        import numpy as np
        DIM = 128
        H_GLOBAL = 8
        H_LOCAL = 4
        WINDOW = 5
        HALF = WINDOW // 2
        B, S = (4, 1024)
        EPS = 1e-05

        def layer_norm(x, g, b):
            mu = jnp.mean(x, axis=-1, keepdims=True)
            var = jnp.mean(jnp.square(x - mu), axis=-1, keepdims=True)
            return (x - mu) * jax.lax.rsqrt(var + EPS) * g + b

        def qkv_proj(x, in_w, in_b):
            qkv = x @ in_w.T + in_b
            return jnp.split(qkv, 3, axis=-1)

        def global_mha(x, in_w, in_b, out_w, out_b, nh):
            Bq, Sq, D = x.shape
            hd = D // nh
            q, k, v = qkv_proj(x, in_w, in_b)
            q = q.reshape(Bq, Sq, nh, hd)
            k = k.reshape(Bq, Sq, nh, hd)
            v = v.reshape(Bq, Sq, nh, hd)
            scores = jnp.einsum('bqhd,bkhd->bhqk', q, k) / np.sqrt(hd).astype(np.float32)
            attn = jax.nn.softmax(scores, axis=-1)
            o = jnp.einsum('bhqk,bkhd->bqhd', attn, v).reshape(Bq, Sq, D)
            return o @ out_w.T + out_b

        def local_mha(x, in_w, in_b, out_w, out_b, nh):
            Bq, Sq, D = x.shape
            hd = D // nh
            q, k, v = qkv_proj(x, in_w, in_b)
            kp = jnp.pad(k, ((0, 0), (HALF, HALF), (0, 0)))
            vp = jnp.pad(v, ((0, 0), (HALF, HALF), (0, 0)))
            k_win = jnp.stack([kp[:, j:j + Sq] for j in range(WINDOW)], axis=2)
            v_win = jnp.stack([vp[:, j:j + Sq] for j in range(WINDOW)], axis=2)
            q = q.reshape(Bq, Sq, nh, hd)
            k_win = k_win.reshape(Bq, Sq, WINDOW, nh, hd)
            v_win = v_win.reshape(Bq, Sq, WINDOW, nh, hd)
            scores = jnp.einsum('bshd,bswhd->bshw', q, k_win) / np.sqrt(hd).astype(np.float32)
            idx = jnp.arange(Sq)[:, None] + jnp.arange(-HALF, HALF + 1)[None, :]
            valid = (idx >= 0) & (idx < Sq)
            scores = jnp.where(valid[None, :, None, :], scores, -jnp.inf)
            attn = jax.nn.softmax(scores, axis=-1)
            o = jnp.einsum('bshw,bswhd->bshd', attn, v_win).reshape(Bq, Sq, D)
            return o @ out_w.T + out_b
        x_global = global_mha(x, g_in_w, g_in_b, g_out_w, g_out_b, H_GLOBAL)
        x_local = local_mha(x, t_in_w, t_in_b, t_out_w, t_out_b, H_LOCAL)
        x_comb = jnp.concatenate([x_global, x_local], axis=-1)
        x_fused = jax.nn.silu(x_comb @ fus_w1.T + fus_b1) @ fus_w2.T + fus_b2
        x = layer_norm(x + x_fused, gn_g, gn_b)
        x_ffn = jax.nn.silu(x @ ffn_w1.T + ffn_b1) @ ffn_w2.T + ffn_b2
        x = layer_norm(x + x_ffn, fn_g, fn_b)
        return x

    def _L1_ffn_ref(h, gate_w, gate_b, w1, b1, w2, b2):
        import math
        import jax, jax.numpy as jnp
        import numpy as np
        CAPACITY_FACTOR = 1.25
        B, L, D = h.shape
        E = gate_w.shape[1]
        T = B * L
        C = max(1, math.ceil(CAPACITY_FACTOR * T / E))
        x = h.reshape(T, D)
        logits = x @ gate_w + gate_b
        probs = jax.nn.softmax(logits, axis=-1)
        idx = jnp.argmax(probs, axis=-1)
        prb = jnp.take_along_axis(probs, idx[:, None], axis=1)[:, 0]
        one_hot = jax.nn.one_hot(idx, E, dtype=jnp.float32)
        pos = (jnp.cumsum(one_hot, axis=0) * one_hot).sum(-1).astype(jnp.int32) - 1
        kept = pos < C
        pos_safe = jnp.where(kept, pos, C)
        buf = jnp.zeros((E, C, D), dtype=h.dtype).at[idx, pos_safe].set(x, mode='drop')
        hmid = jax.nn.relu(jnp.einsum('ecd,edf->ecf', buf, w1) + b1[:, None, :])
        ybuf = jnp.einsum('ecf,efd->ecd', hmid, w2) + b2[:, None, :]
        pos_g = jnp.minimum(pos, C - 1)
        y_tok = ybuf[idx, pos_g] * (prb * kept)[:, None]
        y = y_tok.reshape(B, L, D)
        y = jnp.nan_to_num(y, nan=0.0, posinf=10000.0, neginf=-10000.0)
        return y

    def _gn(v, G=32, eps=1e-05):
        B_, C_, H_, W_ = v.shape
        g = v.reshape(B_, G, C_ // G, H_, W_)
        m = jnp.mean(g, axis=(2, 3, 4), keepdims=True)
        s = jnp.var(g, axis=(2, 3, 4), keepdims=True)
        return ((g - m) / jnp.sqrt(s + eps)).reshape(v.shape)

    def _ln_c(v, eps=1e-06):
        m = jnp.mean(v, axis=1, keepdims=True)
        s = jnp.var(v, axis=1, keepdims=True)
        return (v - m) / jnp.sqrt(s + eps)

    def _ln_t(v, eps=1e-05):
        m = jnp.mean(v, axis=-1, keepdims=True)
        s = jnp.var(v, axis=-1, keepdims=True)
        return (v - m) / jnp.sqrt(s + eps)

    def _to_tokens(v):
        B_, C_, H_, W_ = v.shape
        return v.reshape(B_, C_, H_ * W_).transpose(0, 2, 1)

    def _from_tokens(t, like):
        B_, C_, H_, W_ = like.shape
        return t.transpose(0, 2, 1).reshape(B_, C_, H_, W_)
    x = _L0_conv_ref(x, L0_conv_wq, L0_conv_bq, L0_conv_wk, L0_conv_bk, L0_conv_wv, L0_conv_bv)
    t = _to_tokens(x)
    t = t + _L1_attn_ref(_ln_t(t), L1_attn_g_in_w, L1_attn_g_in_b, L1_attn_g_out_w, L1_attn_g_out_b, L1_attn_t_in_w, L1_attn_t_in_b, L1_attn_t_out_w, L1_attn_t_out_b, L1_attn_fus_w1, L1_attn_fus_b1, L1_attn_fus_w2, L1_attn_fus_b2, L1_attn_ffn_w1, L1_attn_ffn_b1, L1_attn_ffn_w2, L1_attn_ffn_b2, L1_attn_gn_g, L1_attn_gn_b, L1_attn_fn_g, L1_attn_fn_b)
    t = t + _L1_ffn_ref(_ln_t(t), L1_ffn_gate_w, L1_ffn_gate_b, L1_ffn_w1, L1_ffn_b1, L1_ffn_w2, L1_ffn_b2)
    x = _from_tokens(t, x)
    return x

_drawn_inputs = setup_inputs


def setup_inputs(seed=0):
    import zlib

    import numpy as np

    out = dict(_drawn_inputs(seed))
    spreads = {'L0_conv_bq': (0.0, 0.1),
     'L0_conv_bk': (0.0, 2.0),
     'L0_conv_bv': (0.0, 0.1),
     'L1_attn_g_in_b': (0.0, 0.8),
     'L1_attn_g_out_b': (0.0, 0.8),
     'L1_attn_t_in_b': (0.0, 0.8),
     'L1_attn_t_out_b': (0.0, 0.8),
     'L1_attn_fus_b1': (0.0, 0.8),
     'L1_attn_fus_b2': (0.0, 0.578),
     'L1_attn_ffn_b1': (0.0, 0.8),
     'L1_attn_ffn_b2': (0.0, 0.1),
     'L1_attn_gn_g': (1.0, 0.2),
     'L1_attn_gn_b': (0.0, 0.1),
     'L1_attn_fn_g': (1.0, 0.2),
     'L1_attn_fn_b': (0.0, 0.1),
     'L1_ffn_gate_b': (0.0, 0.1),
     'L1_ffn_b1': (0.0, 0.8),
     'L1_ffn_b2': (0.0, 0.8)}
    factors = {'L1_attn_g_in_w': 8.0,
     'L1_attn_g_out_w': 8.0,
     'L1_attn_t_in_w': 8.0,
     'L1_attn_t_out_w': 8.0,
     'L1_attn_fus_w1': 8.0,
     'L1_attn_fus_w2': 6.638,
     'L1_attn_ffn_w1': 3.091,
     'L1_attn_ffn_w2': 2.887}
    for name, (base, spread) in spreads.items():
        noise = np.random.default_rng([zlib.crc32(name.encode()), seed]).standard_normal(out[name].shape)
        drawn = base * np.exp(spread * noise) if base else spread * noise
        out[name] = jnp.asarray(drawn.astype(out[name].dtype))
    for name, factor in factors.items():
        out[name] = (out[name] * factor).astype(out[name].dtype)
    return out
```

```python
from contextlib import ExitStack

import numpy as np

import concourse.bass as bass
from concourse import mybir

F32 = mybir.dt.float32
BF16 = mybir.dt.bfloat16
U32 = mybir.dt.uint32
ALU = mybir.AluOpType
ACT = mybir.ActivationFunctionType
AX = mybir.AxisListType

P = 128
B = 8
N = 1024
C = 128
NT = N // P
HT = NT // 2
HN = N // 2
D = 16
HEADS = C // D
QH = 4
CG = 32
QUADS = HEADS // QH
LH = 4
LD = C // LH
WIN = 5
PAD = WIN // 2
EPS = 1e-5
Q_PART = [0, 0, 1, 0, 2, 1]
K_PART = [0, 1, 0, 2, 0, 1]
TERMS = len(Q_PART)
KROWS = TERMS * D
KM = KROWS + 3
GROUPS = 2 * NT
TILES = GROUPS * QH
E = 8
CAP = (5 * B * N) // (4 * E)
CT = CAP // P
FF = 512
FC = FF // P
ROW = C + 4
NOWHERE = 1.0e6
STEP_UP = 20000.0
MAX_F32 = 3.4028234663852886e38
FAR = 64.0
ONEHOT_STEP = 6
ROUTE_STEPS = 23
NORM_STEPS = HT + 3
SCRATCH_LOADS = 2 * B + E * CT // NT
XT_CHUNKS = [(0, 512), (512, 512), (1024, 256)]
MASKED = -1.0e30

HEAD_USES = (
    [("x_tokens", h) for h in range(2)] + [("conv_qk", h) for h in range(2)]
    + [("conv_v", h) for h in range(2)] + [("conv_max", t) for t in range(2 * NT)] + [("conv_guard",)]
    + [u for h in range(2) for u in
       [("conv_exp", h, j) for j in range(NT)] + [("conv_pv", i) for i in range(HT * h, HT * h + HT)]]
    + [("a_channels", h) for h in range(2)]
    + [u for w in range(2) for u in
       [("global_qk", w, h) for h in range(2)] + [("local_qkv", i) for i in range(HT * w, HT * w + HT)]]
)
HEAD_BANK = {u: n % 2 for n, u in enumerate(HEAD_USES)}
HEAD_TURN = {u: n // 2 for n, u in enumerate(HEAD_USES)}
HEAD_TURNS = [(len(HEAD_USES) + 1) // 2, len(HEAD_USES) // 2]
TAIL_USES = (
    [("o_tokens", q, h) for q in range(QUADS) for h in range(2)]
    + [("o_channels", w, h) for w in range(2) for h in range(2)]
    + [("fuse1", m, h) for h in range(2) for m in range(2)] + [("fuse2", h) for h in range(2)]
    + [("x1_channels", h) for h in range(2)]
    + [("ffn1", m, h) for h in range(2) for m in range(2)] + [("ffn2", h) for h in range(2)]
    + [("n2_channels", h) for h in range(2)] + [("logits",), ("ranks",)]
)
TAIL_TURN = {u: n for n, u in enumerate(TAIL_USES)}
TAIL_TURNS = len(TAIL_USES)


def head_a_steps():
    s = [("x_tokens", 0), ("x_tokens", 1), ("conv_qk", 0), ("conv_qk", 1), ("split", 0), ("conv_stacks",)]
    s += [("conv_v", 0), ("conv_v", 1), 20]
    return s + [("conv_max", t) for t in range(2 * NT)] + [3, ("conv_guard",)]


def head_b_steps():
    s = []
    for h in range(2):
        s += [("conv_exp", h, j) for j in range(NT)] + [1]
        s += [("conv_pv", i) for i in range(HT * h, HT * h + HT)]
        s += [("stats_t", h), 2, ("norm_t", h)]
    s += [("keep",), 3, ("a_channels", 0), ("a_channels", 1), 2]
    for w in range(2):
        s += [("global_qk", w, 0), ("global_qk", w, 1), ("split", 1 + w)]
        s += [("local_qkv", i) for i in range(HT * w, HT * w + HT)]
    return s


def local_steps():
    s = []
    for g in range(NT // 2):
        s += [("local_dot", g), 5, ("local_max", g), 1, ("local_sum", g), 5, ("local_out", g)]
    return s


def tail_a_steps():
    s = [("o_tokens", q, h) for q in range(QUADS) for h in range(2)]
    return s + [("o_channels", w, h) for w in range(2) for h in range(2)]


def tail_b_steps():
    s = [("recall",)]
    s += [("fuse1", m, h) for h in range(2) for m in range(2)] + [1, ("fuse2", 0), ("fuse2", 1)]
    s += [("stats_u", 0), 2, ("norm_u", 0), ("stats_u", 1), 2, ("norm_u", 1), 6]
    s += [("x1_channels", 0), 4, ("x1_channels", 1)]
    s += [("ffn1", m, h) for h in range(2) for m in range(2)] + [1, ("ffn2", 0), ("ffn2", 1)]
    s += [("stats_v", 0), 2, ("norm_v", 0), ("stats_v", 1), 2, ("norm_v", 1), 8]
    s += [("stats_t2", 0), 2, ("norm_t2", 0), 4, ("stats_t2", 1), 2, ("norm_t2", 1), 2]
    return s + [("n2_channels", 0), ("n2_channels", 1), 2, ("logits",), 4, ("ranks",), 4, ("route",)]


def quad_steps(quad, next_quad, has_next):
    s, done = [], 0
    ahead = 1 if next_quad == 0 else 0
    for n in range(TILES):
        while has_next and done < TILES and n >= 8 and done < (n - 8) * TILES / 48:
            s.append((ahead, ("max_tile", next_quad, done)))
            done += 1
        s.append((0, ("score_tile", quad, n)))
        if n % QH == QH - 1 and n >= QH:
            s.append((0, ("pv_group", quad, n // QH - 1)))
            if n // QH - 1 == NT - 1:
                s.append((0, ("o_copy", quad, 0)))
    if has_next:
        s.append((ahead, ("guard", next_quad)))
    s += [(0, ("pv_group", quad, GROUPS - 1)), (0, ("o_copy", quad, 1))]
    return s


def weave(main, *chains):
    placed = []
    for c, (ahead, first, last, chain) in enumerate(chains):
        steps = sum(not isinstance(x, int) for x in chain)
        room = max(0.0, last - first - sum(x for x in chain if isinstance(x, int)))
        at = float(first)
        for x in chain:
            if isinstance(x, int):
                at += x
            else:
                placed.append((at, c, (ahead, x)))
                at += room / steps
    placed.sort(key=lambda x: x[0])
    out, k = [], 0
    for n, step in enumerate(main):
        while k < len(placed) and placed[k][0] <= n:
            out.append(placed[k][2])
            k += 1
        out.append(step)
    return out + [x for _, _, x in placed[k:]]


def plain(chain, ahead=0):
    return [(ahead, x) for x in chain if not isinstance(x, int)]


def first_steps():
    s = plain([("load_x",)] + head_a_steps()) + plain([("load_x",)], 1) + plain(head_b_steps())
    s += plain([("global_stacks", 0), ("global_stacks", 1), ("global_v", 0), ("global_v", 1)])
    main = plain([("max_tile", 0, t) for t in range(TILES)] + [("guard", 0)])
    return s + weave(main, (1, 0, TILES, head_a_steps()))


def iteration_steps(has_tail, has_a, has_b):
    seg0 = quad_steps(0, 1, True)
    seg1 = quad_steps(1, 0, has_b)
    chains = [(0, 14, len(seg0), local_steps())]
    if has_tail:
        chains.append((-1, 0, 10, tail_a_steps()))
    if has_b:
        chains.append((1, 0, len(seg0), head_b_steps()))
    out = plain([("load_x",)], 2) if has_a else []
    out += weave(seg0, *chains)
    if has_b:
        out += [(1, ("global_stacks", 0))]
    chains = []
    if has_tail:
        chains.append((-1, 0, len(seg1), tail_b_steps()))
    if has_a:
        chains.append((2, 0, len(seg1), head_a_steps()))
    out += weave(seg1, *chains)
    if has_b:
        out += [(1, ("global_stacks", 1)), (1, ("global_v", 0)), (1, ("global_v", 1))]
    return out


def last_steps():
    return plain(tail_a_steps() + tail_b_steps())


def hybrid_kernel(nc, x, wq, bq, wk, bk, wv, bv, g_in_w, g_in_b, g_out_w, g_out_b, t_in_w, t_in_b, t_out_w,
                  t_out_b, fus_w1, fus_b1, fus_w2, fus_b2, ffn_w1, ffn_b1, ffn_w2, ffn_b2, gn_g, gn_b, fn_g,
                  fn_b, gate_w, gate_b, w1, b1, w2, b2, out):
    x_b = x.rearrange("b c h w -> b c (h w)")
    out_b = out.rearrange("b c h w -> b c (h w)")

    parts_d = nc.dram_tensor("parts_d", [B, 3, 3, C, N], BF16).ap()
    kv_d = nc.dram_tensor("kv_d", [B, N + 2 * PAD, 2 * C], F32)
    kv_a = kv_d.ap()
    ql_d = nc.dram_tensor("ql_d", [B, N, C], F32).ap()
    kept_d = nc.dram_tensor("kept_d", [B, 2, P, NT, C], F32).ap()
    t2_d = nc.dram_tensor("t2_d", [B * N, C], F32).ap()
    rows_d = nc.dram_tensor("rows_d", [E * CAP, ROW], F32).ap()

    ctx = ExitStack()
    with ctx:
        def sb(name, shape, dt=F32):
            return ctx.enter_context(nc.sbuf_tensor(name, shape, dt))

        def sem(name):
            return ctx.enter_context(nc.semaphore(name))

        bank = [ctx.enter_context(nc.psum_tensor(f"bank{i}", [P, HN], F32)) for i in range(8)]
        head_ps = bank[0:2]
        max_ps = bank[2:4]
        score_ps = bank[4:6]
        o_ps = bank[6]
        tail_ps = bank[7]

        ident = sb("ident", [P, P])
        identb = sb("identb", [P, P], BF16)
        ones = sb("ones", [P, P])
        tri = sb("tri", [P, P])
        lmask = sb("lmask", [P, NT, WIN, LH])
        experts = sb("experts", [P, E])
        half_pow = sb("half_pow", [P, NT])
        cqkT = sb("cqkT", [P, 2 * D])
        cvw = sb("cvw", [P, C])
        gT = sb("gT", [P, 3, C])
        lT = sb("lT", [P, 3 * C])
        fgT = sb("fgT", [P, 2 * C])
        flT = sb("flT", [P, 2 * C])
        f2T = sb("f2T", [P, 2, C])
        n1T = sb("n1T", [P, 2 * C])
        n2wT = sb("n2wT", [P, 2, C])
        gate = sb("gate", [P, E])
        cols = sb("cols", [P, 16])
        hcols = sb("hcols", [P, 16])
        b1c = sb("b1c", [P, E * FC])
        bc = sb("bc", [P, 10, C])
        gate_bc = sb("gate_bc", [P, E])
        BC = {n: i for i, n in enumerate(["bv", "gv", "lq", "lk", "lv", "fus_b2", "gn_g", "gn_b", "ffn_b2", "fn_g"])}
        fnb_bc = sb("fnb_bc", [P, C])

        x_cm = sb("x_cm", [P, N])
        split_x = sb("split_x", [P, N])
        parts = sb("parts", [P, 3, N], BF16)
        cq_stack = sb("cq_stack", [P, N], BF16)
        ck_stack = sb("ck_stack", [P, N], BF16)
        cprob = sb("cprob", [P, NT, HN])
        cv_tok = sb("cv_tok", [P, NT, C + 1])
        t_tok = sb("t_tok", [P, NT, C])
        a_tok = sb("a_tok", [P, NT, C])
        a_cm = sb("a_cm", [P, N])
        cmax = sb("cmax", [P, NT, 2])
        cneg = sb("cneg", [P, NT])
        crest = sb("crest", [P, NT])
        cneg_parts = sb("cneg_parts", [P, 3, NT], BF16)
        cneg_rows = sb("cneg_rows", [3 * NT, P], BF16)
        crecip = sb("crecip", [P, NT])
        stats = sb("stats", [P, HT, 6])
        mv = sb("mv", [P, HT, 3])
        rstd = sb("rstd", [P, HT])
        lqkv = sb("lqkv", [P, 2, 3 * C])

        q_stack = [sb(f"q_stack{q}", [P, QH, N], BF16) for q in range(QUADS)]
        k_stack = [sb(f"k_stack{q}", [P, QH, N], BF16) for q in range(QUADS)]
        v_tok = sb("v_tok", [P, NT, HEADS, CG])
        prob = sb("prob", [P, 2, QH, HN])
        gmax = sb("gmax", [P, QH, NT, 2])
        gneg = sb("gneg", [P, QH * NT])
        grest = sb("grest", [P, QH * NT])
        gneg_parts = sb("gneg_parts", [P, 3, QH * NT], BF16)
        gneg_rows = sb("gneg_rows", [3 * QH * NT, P], BF16)
        o_raw = sb("o_raw", [P, QUADS, 2, HN])
        og_tok = sb("og_tok", [P, NT, QUADS, QH, D])
        grecip = sb("grecip", [P, HT, QH])
        kv_win = sb("kv_win", [P, 2, WIN, 2 * C])
        ql_tok = sb("ql_tok", [P, 2, C])
        lprod = sb("lprod", [P, 2, WIN, C])
        ls = sb("ls", [P, 2, WIN, LH])
        lmx = sb("lmx", [P, 2, LH])
        lsum = sb("lsum", [P, 2, LH])
        ol_tok = sb("ol_tok", [P, NT, C])

        t_old = sb("t_old", [P, NT, C])
        a_old = sb("a_old", [P, NT, C])
        y_cm = sb("y_cm", [P, 2, N])
        hid = sb("hid", [P, 2, N])
        tanh_t = sb("tanh_t", [P, HN])
        half_t = sb("half_t", [P, HN])
        x1 = sb("x1", [P, NT, C])
        stats2 = sb("stats2", [P, HT, 6])
        mv2 = sb("mv2", [P, HT, 3])
        rstd2 = sb("rstd2", [P, HT])
        rows = sb("rows", [P, NT, ROW])
        lg = sb("lg", [P, NT, E])
        lgm = sb("lgm", [P, NT])
        lge = sb("lge", [P, NT, E])
        cand = sb("cand", [P, NT, E])
        idx = sb("idx", [P, NT])
        onehot = sb("onehot", [P, NT, E])
        cum = sb("cum", [P, NT + 1, E])
        rank = sb("rank", [P, NT])
        over = sb("over", [P, NT])
        slot = sb("slot", [P, NT], U32)
        token_no = sb("token_no", [P, NT])

        rows_e = cprob[:, :, :].rearrange("p a b -> p (a b)")[:, 0:CT * ROW].rearrange("p (t r) -> p t r", r=ROW)
        stk = [q_stack[0], q_stack[1], k_stack[0], k_stack[1]]
        hid_e = [s[:, :, :].rearrange("p a b -> p (a b)").bitcast(F32)[:, 0:CAP] for s in stk]
        x_e = prob[:, :, :, :].rearrange("p a b c -> p (a b c)")[:, 0:CAP]
        y_e = v_tok[:, :, :, :].rearrange("p a b c -> p (a b c)")[:, 0:CAP].rearrange("p (t c) -> p t c", c=C)
        w1_e = x_cm[:, 0:FF]
        w2_e = x_cm[:, FF:2 * FF].rearrange("p (f c) -> p f c", c=C)
        b2_e = t_tok
        b1_e = sb("b1_e", [P, FC])
        prob_e = sb("prob_e", [P, CT])
        token_e = sb("token_e", [P, CT], U32)
        odd_e = hid[:, :, :].rearrange("p a b -> p (a b)")[:, 0:3 * HN].rearrange("p (k n) -> p k n", k=3).bitcast(U32)
        huge = sb("huge", [P, 3])
        zero_rows = lprod[0:PAD, 0, 0:2, :].rearrange("p a c -> p (a c)")
        nat = cprob[:, :, :].rearrange("p a b -> p (a b)")
        fin_tok = [a_tok, t_old]
        fin_cm = [hid[:, 0, :], hid[:, 1, :]]

        consts_made = sem("consts_made")
        const_step = sem("const_step")
        const_dve = sem("const_dve")
        weights_in = sem("weights_in")
        weights_filled = sem("weights_filled")
        weights_used = sem("weights_used")
        scratch_zeroed = sem("scratch_zeroed")
        x_in = sem("x_in")
        kept = sem("kept")
        recalled = sem("recalled")
        head_full = [sem(f"head_full{k}") for k in range(2)]
        head_free = [sem(f"head_free{k}") for k in range(2)]
        split_step = sem("split_step")
        split_out = sem("split_out")
        cstacks_in = sem("cstacks_in")
        cguard_step = sem("cguard_step")
        cguard_in = sem("cguard_in")
        cpv_made = sem("cpv_made")
        crecip_made = sem("crecip_made")
        norm_step = sem("norm_step")
        norm_rstd = sem("norm_rstd")
        a_made = sem("a_made")
        lqkv_out = [sem(f"lqkv_out{k}") for k in range(2)]
        gstacks_in = [sem(f"gstacks_in{q}") for q in range(QUADS)]
        max_full = sem("max_full")
        max_free = sem("max_free")
        guard_step = sem("guard_step")
        guard_in = [sem(f"guard_in{q}") for q in range(QUADS)]
        score_full = sem("score_full")
        exp_made = sem("exp_made")
        pv_made = sem("pv_made")
        o_copied = sem("o_copied")
        grecip_made = sem("grecip_made")
        kv_in = sem("kv_in")
        lprod_made = sem("lprod_made")
        local_step = sem("local_step")
        lexp_made = sem("lexp_made")
        lpv_made = sem("lpv_made")
        ol_made = sem("ol_made")
        tail_full = sem("tail_full")
        tail_free = sem("tail_free")
        hid_made = sem("hid_made")
        bias_added = sem("bias_added")
        norm2_step = sem("norm2_step")
        norm2_rstd = sem("norm2_rstd")
        u_normed = sem("u_normed")
        affine_step = sem("affine_step")
        x1_made = sem("x1_made")
        x1_bias = sem("x1_bias")
        t2_made = sem("t2_made")
        t2_out = sem("t2_out")
        n2_made = sem("n2_made")
        route_step = sem("route_step")
        lexpert = sem("lexpert")
        routed = sem("routed")
        rows_out = sem("rows_out")
        erows_in = sem("erows_in")
        ew1_in = sem("ew1_in")
        ew2_in = sem("ew2_in")
        eb2_in = sem("eb2_in")
        ext_full = sem("ext_full")
        ext_free = sem("ext_free")
        eh_full = sem("eh_full")
        eh_free = sem("eh_free")
        ey_full = sem("ey_full")
        ey_free = sem("ey_free")
        etaken = sem("etaken")
        ey_step = sem("ey_step")
        eb1_made = sem("eb1_made")
        ey_odd = [sem(f"ey_odd{c}") for c in range(3)]
        ey_pass = [[sem(f"ey_pass{c}{k}") for k in range(2)] for c in range(3)]
        ey_made = [sem(f"ey_made{c}") for c in range(3)]
        ey_out = sem("ey_out")
        fin_in = [sem(f"fin_in{k}") for k in range(2)]
        fin_full = [sem(f"fin_full{k}") for k in range(2)]
        fin_made = [sem(f"fin_made{k}") for k in range(2)]
        fin_out = [sem(f"fin_out{k}") for k in range(2)]

        def after(eng, s, count):
            if not isinstance(count, int) or count > 0:
                eng.wait_ge(s, count)

        def head_fill(pe, b, use):
            k = HEAD_BANK[use]
            after(pe, head_free[k], b * HEAD_TURNS[k] + HEAD_TURN[use])
            return head_ps[k], head_full[k]

        def head_read(eng, b, use):
            k = HEAD_BANK[use]
            after(eng, head_full[k], b * HEAD_TURNS[k] + HEAD_TURN[use] + 1)
            return head_ps[k], head_free[k]

        def head_done(eng, b, *uses):
            for use in uses:
                k = HEAD_BANK[use]
                after(eng, head_free[k], b * HEAD_TURNS[k] + HEAD_TURN[use] + 1)

        def tail_done(eng, b, use):
            after(eng, tail_free, tail_count(b, use) + 1)

        def tail_count(b, use):
            if use[0] == "global_v":
                return (0 if isinstance(b, int) and b == 0 else (b - 1) * (TAIL_TURNS + 2) + 2) + use[1]
            last = isinstance(b, int) and b == B - 1
            return b * (TAIL_TURNS + 2) + (2 if last else 4) + TAIL_TURN[use]

        def max_bank(quad, n):
            return (quad * (TILES + 1) + n) % 2

        def walk(eng, steps):
            def take(order, i):
                for ahead, (name, *args) in order:
                    if name in steps:
                        steps[name](i + ahead if ahead else i, *args)
            take(first_steps(), 0)
            take(iteration_steps(False, True, True), 0)
            with eng.Fori(1, B - 2) as i:
                take(iteration_steps(True, True, True), i)
            take(iteration_steps(True, False, True), B - 2)
            take(iteration_steps(True, False, False), B - 1)
            take(last_steps(), B - 1)

        BIAS_ROWS = ["conv", "gq", "gk", "go", "to", "fus0", "fus1", "ffn0", "ffn1"]
        COL = {n: i for i, n in enumerate(BIAS_ROWS)}
        NAT = [("cqk", None, 2 * D), ("cv", wv, P)]
        NAT += [(f"g{i}", g_in_w[i * C:(i + 1) * C, :], P) for i in range(3)]
        NAT += [(f"l{i}", t_in_w[i * C:(i + 1) * C, :], P) for i in range(3)]
        NAT += [(f"f1{m}{k}", fus_w1[m * C:(m + 1) * C, k * C:(k + 1) * C], P) for m in range(2) for k in range(2)]
        NAT += [(f"f2{k}", fus_w2[:, k * C:(k + 1) * C], P) for k in range(2)]
        NAT += [(f"n1{m}", ffn_w1[m * C:(m + 1) * C, :], P) for m in range(2)]
        NAT += [(f"n2{k}", ffn_w2[:, k * C:(k + 1) * C], P) for k in range(2)]
        NAT += [("bias", None, len(BIAS_ROWS)), ("b1", b1.rearrange("e (f p) -> (e f) p", p=P), E * FC)]
        WO = {"g": len(NAT), "t": len(NAT) + 1}
        f1T = [hid[:, k, 0:2 * C] for k in range(2)]
        TARGET = {"cqk": cqkT[:, :], "cv": cvw[:, :]}
        for i in range(3):
            TARGET[f"g{i}"] = gT[:, i, :]
            TARGET[f"l{i}"] = lT[:, i * C:(i + 1) * C]
        for m in range(2):
            for k in range(2):
                TARGET[f"f1{m}{k}"] = f1T[k][:, m * C:(m + 1) * C]
            TARGET[f"f2{m}"] = f2T[:, m, :]
            TARGET[f"n1{m}"] = n1T[:, m * C:(m + 1) * C]
            TARGET[f"n2{m}"] = n2wT[:, m, :]
        TARGET["bias"] = cols[:, 0:len(BIAS_ROWS)]
        TARGET["b1"] = b1c[:, :]
        WEIGHT_LOADS = len(NAT) - 2 + 2 + 11 + 3 + len(BC) + 2

        block = ctx.enter_context(nc.Block())

        @block.sync
        def _(sp):
            def n_at(i, rows_=P, first=0):
                return nat[first:first + rows_, i * C:(i + 1) * C]

            loads = []
            for i, (name, src, r) in enumerate(NAT):
                if name == "cqk":
                    loads += [(n_at(i, D), wq), (n_at(i, D, D), wk)]
                elif name == "bias":
                    row = lambda k: nat[COL[k]:COL[k] + 1, i * C:(i + 1) * C]
                    one = lambda v, lo, hi: v[lo:hi].rearrange("(a n) -> a n", a=1)
                    loads += [(row("conv")[:, 0:D], one(bq, 0, D)), (row("conv")[:, D:2 * D], one(bk, 0, D))]
                    loads += [(row("conv")[:, 2 * D:C], one(g_in_b, 0, C - 2 * D))]
                    loads += [(row("gq"), one(g_in_b, 0, C)), (row("gk"), one(g_in_b, C, 2 * C))]
                    loads += [(row("go"), one(g_out_b, 0, C)), (row("to"), one(t_out_b, 0, C))]
                    loads += [(row(f"fus{m}"), one(fus_b1, m * C, (m + 1) * C)) for m in range(2)]
                    loads += [(row(f"ffn{m}"), one(ffn_b1, m * C, (m + 1) * C)) for m in range(2)]
                else:
                    loads.append((n_at(i, r), src))
            loads += [(n_at(WO["g"]), g_out_w), (n_at(WO["t"]), t_out_w), (gate[:, :], gate_w)]
            wide = {"bv": bv, "gv": g_in_b[2 * C:3 * C], "lq": t_in_b[0:C], "lk": t_in_b[C:2 * C],
                    "lv": t_in_b[2 * C:3 * C], "fus_b2": fus_b2, "gn_g": gn_g, "gn_b": gn_b, "ffn_b2": ffn_b2,
                    "fn_g": fn_g}
            loads += [(bc[:, BC[k], :], v.partition_broadcast(P)) for k, v in wide.items()]
            loads += [(fnb_bc[:, :], fn_b.partition_broadcast(P)), (gate_bc[:, :], gate_b.partition_broadcast(P))]
            assert len(loads) == WEIGHT_LOADS, len(loads)
            for dst, src in loads:
                sp.dma_start(dst, src).then_inc(weights_in, 16)

            sp.wait_ge(consts_made, 2)
            for b in range(B):
                sp.dma_start(kv_a[b, 0:PAD, :], zero_rows).then_inc(scratch_zeroed, 16)
                sp.dma_start(kv_a[b, N + PAD:N + 2 * PAD, :], zero_rows).then_inc(scratch_zeroed, 16)
            for e in range(E * CT // NT):
                sp.dma_start(rows_d[e * NT * P:(e + 1) * NT * P, :].rearrange("(t p) r -> p t r", p=P),
                             rows[:, :, :]).then_inc(scratch_zeroed, 16)

            def load_x(b):
                if not (isinstance(b, int) and b == 0):
                    k = HEAD_BANK["conv_v", 1]
                    after(sp, head_full[k], (b - 1) * HEAD_TURNS[k] + HEAD_TURN["conv_v", 1] + 1)
                sp.dma_start(x_cm[:, :], x_b[b]).then_inc(x_in, 16)

            def keep(b):
                after(sp, a_made, (b + 1) * 2)
                sp.dma_start(kept_d[b, 0], t_tok[:, :, :]).then_inc(kept, 16)
                sp.dma_start(kept_d[b, 1], a_tok[:, :, :]).then_inc(kept, 16)

            def recall(b):
                after(sp, kept, (b + 1) * 32)
                sp.dma_start(t_old[:, :, :], kept_d[b, 0]).then_inc(recalled, 16)
                sp.dma_start(a_old[:, :, :], kept_d[b, 1]).then_inc(recalled, 16)

            def split(b, w):
                rows_ = 2 * D if w == 0 else C
                after(sp, split_step, b * 9 + 3 * w + 3)
                sp.dma_start(parts_d[b, w].rearrange("s c n -> c s n")[0:rows_], parts[0:rows_, :, :])\
                  .then_inc(split_out, 16)

            def conv_stacks(b):
                if not (isinstance(b, int) and b == 0):
                    head_read(sp, b - 1, ("conv_exp", 1, NT - 1))
                after(sp, split_out, b * 48 + 16)
                for r in range(TERMS):
                    sp.dma_start(cq_stack[D * r:D * r + D, :], parts_d[b, 0, Q_PART[r], 0:D, :])\
                      .then_inc(cstacks_in, 16)
                    sp.dma_start(ck_stack[D * r:D * r + D, :], parts_d[b, 0, K_PART[r], D:2 * D, :])\
                      .then_inc(cstacks_in, 16)

            def conv_guard(b):
                head_done(sp, b, ("conv_guard",))
                for s in range(3):
                    dst = cq_stack[KROWS + s:KROWS + s + 1, :].rearrange("a (t p) -> a t p", p=P)
                    sp.dma_start(dst, cneg_rows[s * NT:s * NT + NT, :]).then_inc(cguard_in, 16)

            def local_qkv(b, i):
                head_done(sp, b, ("local_qkv", i))
                sp.dma_start(ql_d[b, i * P:(i + 1) * P, :], lqkv[:, i % 2, 0:C]).then_inc(lqkv_out[i % 2], 16)
                sp.dma_start(kv_a[b, PAD + i * P:PAD + (i + 1) * P, :], lqkv[:, i % 2, C:3 * C])\
                  .then_inc(lqkv_out[i % 2], 16)

            def global_stacks(b, quad):
                stored = b * 48 + 48 if isinstance(b, int) else sp.to_reg(b * 48 + 48)
                if not (isinstance(b, int) and b == 0):
                    after(sp, score_full, (b - 1) * 2 * TILES + (quad + 1) * TILES)
                after(sp, split_out, stored)
                for r in range(TERMS):
                    for w, st, part in ((1, q_stack[quad], Q_PART[r]), (2, k_stack[quad], K_PART[r])):
                        src = parts_d[b, w, part].rearrange("(h d) n -> d h n", d=D)
                        sp.dma_start(st[D * r:D * r + D, :, :], src[:, quad * QH:(quad + 1) * QH, :])\
                          .then_inc(gstacks_in[quad], 16)

            def guard(b, quad):
                after(sp, max_free, b * 2 * (TILES + 1) + (quad + 1) * (TILES + 1))
                for s in range(3):
                    dst = q_stack[quad][KROWS + s:KROWS + s + 1, :, :].rearrange("a h (t p) -> a (h t) p", p=P)
                    sp.dma_start(dst, gneg_rows[s * QH * NT:(s + 1) * QH * NT, :]).then_inc(guard_in[quad], 16)

            def local_dot(b, g):
                if not (isinstance(b, int) and b == 0 and g == 0):
                    after(sp, lpv_made, b * 4 + g)
                for out_ in lqkv_out:
                    after(sp, out_, (b + 1) * HT * 32)
                after(sp, scratch_zeroed, SCRATCH_LOADS * 16)
                win = bass.AP(kv_d, (b * (N + 2 * PAD) + 2 * g * P) * 2 * C,
                              [[2 * C, P], [P * 2 * C, 2], [1, WIN * 2 * C]])
                sp.dma_start(kv_win[:, :, :, :].rearrange("p i w c -> p i (w c)"), win).then_inc(kv_in, 16)
                sp.dma_start(ql_tok[:, :, :],
                             ql_d[b, 2 * g * P:(2 * g + 2) * P, :].rearrange("(i p) c -> p i c", p=P))\
                  .then_inc(kv_in, 16)

            def norm_t2(b, h):
                if h == 1:
                    after(sp, t2_made, (b + 1) * 2)
                    sp.dma_start(t2_d.rearrange("(b t p) c -> b p t c", t=NT, p=P)[b], x1[:, :, :])\
                        .then_inc(t2_out, 16)

            walk(sp, dict(load_x=load_x, keep=keep, recall=recall, split=split, conv_stacks=conv_stacks,
                          conv_guard=conv_guard, local_qkv=local_qkv, global_stacks=global_stacks, guard=guard,
                          local_dot=local_dot, norm_t2=norm_t2))

            sp.wait_ge(rows_out, B * NT * 16)
            rows_v = rows_d.rearrange("(e t p) r -> e p t r", t=CT, p=P)
            with sp.Fori(0, E) as e:
                sp.wait_ge(ext_full, e * 3)
                sp.wait_ge(etaken, e)
                sp.dma_start(rows_e, rows_v[e]).then_inc(erows_in, 16)
                sp.wait_ge(eh_full, e * FC * 3)
                sp.dma_start(w1_e, w1[e]).then_inc(ew1_in, 16)
                sp.wait_ge(ey_full, e * 3)
                sp.dma_start(w2_e, w2.rearrange("e (f p) c -> e p f c", p=P)[e]).then_inc(ew2_in, 16)
                sp.wait_ge(ey_free, e * 3)
                sp.dma_start(b2_e[:, 0, :], b2[e].partition_broadcast(P)).then_inc(eb2_in, 16)

            sp.wait_ge(ey_out, E * CT * 16)
            t2_v = t2_d.rearrange("(b k t p) c -> b k p t c", k=2, t=HT, p=P)
            with sp.Fori(0, B) as b:
                for k in range(2):
                    sp.wait_ge(fin_full[k], b)
                    sp.dma_start(fin_tok[k][:, 0:HT, :], t2_v[b, k]).then_inc(fin_in[k], 16)
                for k in range(2):
                    sp.wait_ge(fin_made[k], b + 1)
                    sp.dma_start(out_b[b, :, k * HN:(k + 1) * HN], fin_cm[k][:, 0:HN]).then_inc(fin_out[k], 16)
            for k in range(2):
                sp.wait_ge(fin_out[k], B * 16)

        @block.gpsimd
        def _(pool):
            last_slot = pool.to_reg(E * CAP - 1)
            last_token = pool.to_reg(B * N - 1)
            made = [0]

            def made_here(ins):
                made[0] += 1
                ins.then_inc(const_step, 1)
                pool.wait_ge(const_step, made[0])

            made_here(pool.memset(rows[:, :, :], 0.0))
            made_here(pool.memset(lprod[:, :, :, :], 0.0))
            pool.memset(rows[:, :, C + 1:C + 2], NOWHERE).then_inc(consts_made, 1)
            pool.memset(half_pow[:, :], -0.5).then_inc(consts_made, 1)
            for m in (ident, identb, tri):
                made_here(pool.memset(m[:, :], 1.0 if m is tri else 0.0))
            made_here(pool.memset(ones[:, :], 1.0))
            for m in (ident, identb):
                made_here(pool.affine_select(out=m[:, :], in_=m[:, :], compare_op=ALU.not_equal, fill=1.0,
                                             base=0, pattern=[[-1, P]], channel_multiplier=1))
            made_here(pool.affine_select(out=tri[:, :], in_=tri[:, :], compare_op=ALU.is_ge, fill=0.0,
                                         base=0, pattern=[[1, P]], channel_multiplier=-1))
            made_here(pool.memset(lmask[:, :, :, :], 0.0))
            made_here(pool.affine_select(out=lmask[:, 0, :, :], in_=lmask[:, 0, :, :], compare_op=ALU.is_ge,
                                         fill=MASKED, base=-PAD, pattern=[[1, WIN], [0, LH]], channel_multiplier=1))
            made_here(pool.affine_select(out=lmask[:, NT - 1, :, :], in_=lmask[:, NT - 1, :, :],
                                         compare_op=ALU.is_ge, fill=MASKED, base=P - 1 + PAD,
                                         pattern=[[-1, WIN], [0, LH]], channel_multiplier=-1))
            made_here(pool.iota(experts[:, :], pattern=[[1, E]], base=0, channel_multiplier=0,
                                allow_small_or_imprecise_dtypes=True))
            made_here(pool.iota(token_no[:, :], pattern=[[P, NT]], base=0, channel_multiplier=1,
                                allow_small_or_imprecise_dtypes=True))
            made_here(pool.memset(cum[:, :, :], 0.0))
            made_here(pool.memset(cv_tok[:, :, C:C + 1], 1.0))
            made_here(pool.memset(v_tok[:, :, :, :], 0.0))
            made_here(pool.memset(v_tok[:, :, :, D:D + 1], 1.0))
            made_here(pool.memset(huge[:, 0:1], 0.0))
            made_here(pool.memset(huge[:, 1:2], 10000.0))
            made_here(pool.memset(huge[:, 2:3], -10000.0))
            for s in (ck_stack[KROWS:KM, :], k_stack[0][KROWS:KM, :, :], k_stack[1][KROWS:KM, :, :]):
                made_here(pool.memset(s, 1.0))
            pool.memset(stats[:, 0, 0:1], 0.0).then_inc(consts_made, 1)

            def rms(b, in_, out_, step_sem, step, made_sem):
                after(pool, step_sem, step)
                pool.tensor_tensor(out_, in_, half_pow[:, 0:HT], ALU.pow).then_inc(made_sem, 1)

            def stats_t(b, h):
                rms(b, mv[:, :, 1], rstd[:, :], norm_step, b * 2 * NORM_STEPS + (h + 1) * NORM_STEPS, norm_rstd)

            def tail_rms(b, k):
                rms(b, mv2[:, :, 1], rstd2[:, :], norm2_step, b * 6 * NORM_STEPS + (k + 1) * NORM_STEPS, norm2_rstd)

            def wide(i, n=HT):
                return (bc[:, i, :] if isinstance(i, int) else i)[:, None, :].to_broadcast([P, n, C])

            def stats_u(b, h):
                tail_rms(b, h)

            def stats_v(b, h):
                tail_rms(b, 2 + h)

            def stats_t2(b, h):
                tail_rms(b, 4 + h)

            def local_dot(b, g):
                after(pool, kv_in, b * 128 + 32 * (g + 1))
                if not (isinstance(b, int) and b == 0 and g == 0):
                    after(pool, ol_made, b * 4 + g)
                for i in range(2):
                    m = pool.tensor_tensor(lprod[:, i, :, :], ql_tok[:, i, None, :].to_broadcast([P, WIN, C]),
                                           kv_win[:, i, :, 0:C], ALU.mult)
                m.then_inc(lprod_made, 1)

            def local_sum(b, g):
                after(pool, local_step, b * 28 + 7 * g + 7)
                for i in range(2):
                    m = pool.tensor_tensor(
                        lprod[:, i, :, :].rearrange("p w (h d) -> p w h d", d=LD),
                        ls[:, i, :, :, None].to_broadcast([P, WIN, LH, LD]),
                        kv_win[:, i, :, C:2 * C].rearrange("p w (h d) -> p w h d", d=LD), ALU.mult)
                m.then_inc(lpv_made, 1)

            def fuse1(b, m, h):
                if m == 0 and h == 0:
                    after(pool, recalled, (b + 1) * 32)
                    pool.tensor_tensor(a_old[:, :, :], a_old[:, :, :], wide(BC["fus_b2"], NT), ALU.add)\
                        .then_inc(bias_added, 1)

            def norm_u(b, h):
                t = slice(HT * h, HT * h + HT)
                after(pool, u_normed, b * 4 + h + 1)
                pool.tensor_tensor(x1[:, t, :], x1[:, t, :], wide(BC["gn_g"]), ALU.mult).then_inc(affine_step, 1)
                after(pool, affine_step, b * 6 + h * 1 + 1)
                pool.tensor_tensor(x1[:, t, :], x1[:, t, :], wide(BC["gn_b"]), ALU.add).then_inc(x1_made, 1)
                after(pool, x1_made, b * 2 + h + 1)
                tail_done(pool, b, ("fuse2", 1))
                pool.tensor_tensor(a_old[:, t, :], x1[:, t, :], wide(BC["ffn_b2"]), ALU.add).then_inc(x1_bias, 1)

            def norm_v(b, h):
                t = slice(HT * h, HT * h + HT)
                after(pool, u_normed, b * 4 + 2 + h + 1)
                pool.tensor_tensor(x1[:, t, :], x1[:, t, :], wide(BC["fn_g"]), ALU.mult).then_inc(affine_step, 1)
                after(pool, affine_step, b * 6 + 2 + 2 * h + 1)
                pool.tensor_tensor(x1[:, t, :], x1[:, t, :], wide(fnb_bc[:, :]), ALU.add).then_inc(affine_step, 1)
                after(pool, affine_step, b * 6 + 2 + 2 * h + 2)
                pool.tensor_tensor(x1[:, t, :], x1[:, t, :], t_old[:, t, :], ALU.add).then_inc(t2_made, 1)

            def route(b):
                pool.wait_ge(scratch_zeroed, SCRATCH_LOADS * 16)
                after(pool, routed, b + 1)
                for i in range(NT):
                    pool.indirect_dma_start(rows_d, bass.IndirectOffsetOnAxis(ap=slot[:, i:i + 1], axis=0),
                                            rows[:, i, :], None, bounds_check=last_slot, oob_is_err=False)\
                        .then_inc(rows_out, 16)

            walk(pool, dict(stats_t=stats_t, local_dot=local_dot, local_sum=local_sum, fuse1=fuse1, stats_u=stats_u,
                            norm_u=norm_u, stats_v=stats_v, norm_v=norm_v, stats_t2=stats_t2, route=route))

            with pool.Fori(1, E + 1) as nth:
                for i in range(CT):
                    c = i * P // HN
                    if i * P % HN == 0:
                        pool.wait_ge(t2_out, B * 16)
                        pool.wait_ge(ey_made[c], nth)
                    pool.indirect_dma_start(t2_d, bass.IndirectOffsetOnAxis(ap=token_e[:, i:i + 1], axis=0),
                                            y_e[:, i, :], None, bounds_check=last_token, oob_is_err=False,
                                            compute_op=ALU.add).then_inc(ey_out, 16)

        @block.tensor
        def _(pe):
            mm = nc.tensor.matmul

            def turn(dst, src, n=P, identity=None):
                return nc.tensor.transpose(dst, src, ident[0:n, 0:n] if identity is None else identity)

            pe.wait_ge(consts_made, 3)
            pe.wait_ge(weights_in, WEIGHT_LOADS * 16)
            for i, (name, _, r) in enumerate(NAT):
                if i >= 2:
                    pe.wait_ge(weights_used, i - 1)
                turn(bank[i % 2][:, 0:r], nat[0:r, i * C:(i + 1) * C], r).then_inc(weights_filled, 1)
            n = len(NAT)
            pe.wait_ge(weights_used, n)
            for k, w in enumerate("gt"):
                mm(bank[2 + k][:, 0:2 * C], nat[:, WO[w] * C:(WO[w] + 1) * C], f1T[k], start=True, stop=True)\
                    .then_inc(weights_filled, 1)
            for m in range(2):
                for k, name in enumerate(("go", "to")):
                    last = mm(bank[4][:, m:m + 1], f1T[k][:, m * C:(m + 1) * C], cols[:, COL[name]:COL[name] + 1],
                              start=(k == 0), stop=(k == 1))
            last.then_inc(weights_filled, 1)
            pe.wait_ge(weights_used, n + 5)

            def x_tokens(b, h):
                ps, full = head_fill(pe, b, ("x_tokens", h))
                after(pe, x_in, (b + 1) * 16)
                for i in range(HT):
                    last = turn(ps[:, i * C:(i + 1) * C], x_cm[:, (HT * h + i) * P:(HT * h + i + 1) * P])
                last.then_inc(full, 1)

            def conv_qk(b, h):
                ps, full = head_fill(pe, b, ("conv_qk", h))
                mm(ps[0:2 * D, :], cqkT[:, :], x_cm[:, h * HN:(h + 1) * HN], start=True, stop=True).then_inc(full, 1)

            def conv_v(b, h):
                ps, full = head_fill(pe, b, ("conv_v", h))
                for i in range(HT):
                    last = mm(ps[:, i * C:(i + 1) * C], x_cm[:, (HT * h + i) * P:(HT * h + i + 1) * P], cvw[:, :],
                              start=True, stop=True)
                last.then_inc(full, 1)

            def conv_max(b, t):
                ps, full = head_fill(pe, b, ("conv_max", t))
                if t == 0:
                    after(pe, cstacks_in, (b + 1) * 12 * 16)
                i, j = t // 2, t % 2
                mm(ps[:, :], cq_stack[0:KROWS, i * P:(i + 1) * P], ck_stack[0:KROWS, j * HN:(j + 1) * HN],
                   start=True, stop=True).then_inc(full, 1)

            def conv_guard(b):
                ps, full = head_fill(pe, b, ("conv_guard",))
                after(pe, cguard_step, b * 6 + 6)
                turn(ps[:, :].bitcast(BF16)[0:3 * NT, 0:P], cneg_parts[:, :, :].rearrange("p s t -> p (s t)"),
                     identity=identb[:, :]).then_inc(full, 1)

            def conv_exp(b, h, j):
                ps, full = head_fill(pe, b, ("conv_exp", h, j))
                if h == 0 and j == 0:
                    after(pe, cguard_in, (b + 1) * 48)
                mm(ps[:, :], ck_stack[0:KM, j * P:(j + 1) * P], cq_stack[0:KM, h * HN:(h + 1) * HN],
                   start=True, stop=True).then_inc(full, 1)

            def conv_pv(b, i):
                ps, full = head_fill(pe, b, ("conv_pv", i))
                if i % HT == 0:
                    head_done(pe, b, ("conv_exp", i // HT, NT - 2), ("conv_exp", i // HT, NT - 1))
                if i == 0:
                    head_done(pe, b, ("conv_v", 0), ("conv_v", 1))
                for j in range(NT):
                    last = mm(ps[:, 0:C + 1], cprob[:, j, (i % HT) * P:(i % HT + 1) * P], cv_tok[:, j, :],
                              start=(j == 0), stop=(j == NT - 1))
                last.then_inc(full, 1)

            def a_channels(b, h):
                ps, full = head_fill(pe, b, ("a_channels", h))
                after(pe, a_made, b * 2 + h + 1)
                for i in range(HT):
                    last = turn(ps[:, i * P:(i + 1) * P], a_tok[:, HT * h + i, :])
                last.then_inc(full, 1)

            def global_qk(b, w, h):
                ps, full = head_fill(pe, b, ("global_qk", w, h))
                head_done(pe, b, ("a_channels", h))
                mm(ps[:, :], gT[:, w, :], a_cm[:, h * HN:(h + 1) * HN], start=True, stop=True).then_inc(full, 1)

            def local_qkv(b, i):
                ps, full = head_fill(pe, b, ("local_qkv", i))
                mm(ps[:, 0:3 * C], a_cm[:, i * P:(i + 1) * P], lT[:, :], start=True, stop=True).then_inc(full, 1)

            def global_v(b, h):
                tail_fill_at(b, ("global_v", h))
                for i in range(HT):
                    last = mm(tail_ps[:, i * C:(i + 1) * C], a_cm[:, (HT * h + i) * P:(HT * h + i + 1) * P],
                              gT[:, 2, :], start=True, stop=True)
                last.then_inc(tail_full, 1)

            def max_fill(b, quad, n):
                if not (isinstance(b, int) and b == 0 and quad == 0 and n < 2):
                    after(pe, max_free, b * 2 * (TILES + 1) + quad * (TILES + 1) + n - 1)

            def max_tile(b, quad, n):
                max_fill(b, quad, n)
                if n == 0:
                    after(pe, gstacks_in[quad], (b + 1) * 12 * 16)
                h, i, j = n // (2 * NT), n // 2 % NT, n % 2
                mm(max_ps[max_bank(quad, n)][:, :], q_stack[quad][0:KROWS, h, i * P:(i + 1) * P],
                   k_stack[quad][0:KROWS, h, j * HN:(j + 1) * HN], start=True, stop=True).then_inc(max_full, 1)

            def guard(b, quad):
                max_fill(b, quad, TILES)
                after(pe, guard_step, b * 12 + quad * 6 + 6)
                turn(max_ps[max_bank(quad, TILES)][:, :].bitcast(BF16)[0:3 * QH * NT, 0:P],
                     gneg_parts[:, :, :].rearrange("p s t -> p (s t)"), identity=identb[:, :]).then_inc(max_full, 1)

            def score_tile(b, quad, n):
                u = b * 2 * TILES + quad * TILES + n
                if not (isinstance(b, int) and b == 0 and quad == 0 and n < 2):
                    after(pe, exp_made, u - 1)
                if n == 0:
                    after(pe, guard_in[quad], (b + 1) * 48)
                g, h = n // QH, n % QH
                half, j = g // NT, g % NT
                mm(score_ps[n % 2][:, :], k_stack[quad][0:KM, h, j * P:(j + 1) * P],
                   q_stack[quad][0:KM, h, half * HN:(half + 1) * HN], start=True, stop=True).then_inc(score_full, 1)

            def pv_group(b, quad, g):
                half, j = g // NT, g % NT
                after(pe, exp_made, b * 2 * TILES + quad * TILES + g * QH + QH)
                if j == 0:
                    after(pe, o_copied, b * 4 + quad * 2 + half)
                if quad == 0 and g == 0:
                    tail_done(pe, b, ("global_v", 1))
                for h in range(QH):
                    last = mm(o_ps[CG * h:CG * (h + 1), :], v_tok[:, j, quad * QH + h, :], prob[:, g % 2, h, :],
                              start=(j == 0), stop=(j == NT - 1))
                last.then_inc(pv_made, 1)

            def o_tokens(b, quad, h):
                tail_fill_at(b, ("o_tokens", quad, h))
                after(pe, o_copied, b * 4 + quad * 2 + h + 1)
                for i in range(HT):
                    last = turn(tail_ps[:, i * P:(i + 1) * P], o_raw[:, quad, h, i * P:(i + 1) * P])
                last.then_inc(tail_full, 1)

            def tail_fill_at(b, use):
                after(pe, tail_free, tail_count(b, use))

            def o_channels(b, w, h):
                tail_fill_at(b, ("o_channels", w, h))
                if w == 1 and h == 0:
                    after(pe, ol_made, (b + 1) * 4)
                for i in range(HT):
                    t = HT * h + i
                    src = og_tok[:, t, :, :, :].rearrange("p q h d -> p (q h d)") if w == 0 else ol_tok[:, t, :]
                    last = turn(tail_ps[:, i * P:(i + 1) * P], src)
                last.then_inc(tail_full, 1)

            def fuse1(b, m, h):
                tail_fill_at(b, ("fuse1", m, h))
                for k, w in enumerate((fgT, flT)):
                    last = mm(tail_ps[:, :], w[:, m * C:(m + 1) * C], y_cm[:, k, h * HN:(h + 1) * HN],
                              start=(k == 0), stop=(k == 1))
                last.then_inc(tail_full, 1)

            def second(b, use, h, w, count):
                tail_fill_at(b, use)
                after(pe, hid_made, count)
                for i in range(HT):
                    t = HT * h + i
                    for k in range(2):
                        last = mm(tail_ps[:, i * C:(i + 1) * C], hid[:, k, t * P:(t + 1) * P], w[:, k, :],
                                  start=(k == 0), stop=(k == 1))
                last.then_inc(tail_full, 1)

            def fuse2(b, h):
                second(b, ("fuse2", h), h, f2T, b * 8 + 2 * h + 2)

            def ffn2(b, h):
                second(b, ("ffn2", h), h, n2wT, b * 8 + 4 + 2 * h + 2)

            def x1_channels(b, h):
                tail_fill_at(b, ("x1_channels", h))
                after(pe, x1_made, b * 2 + h + 1)
                for i in range(HT):
                    last = turn(tail_ps[:, i * P:(i + 1) * P], x1[:, HT * h + i, :])
                last.then_inc(tail_full, 1)

            def ffn1(b, m, h):
                tail_fill_at(b, ("ffn1", m, h))
                mm(tail_ps[:, :], n1T[:, m * C:(m + 1) * C], y_cm[:, 0, h * HN:(h + 1) * HN],
                   start=True, stop=True).then_inc(tail_full, 1)

            def n2_channels(b, h):
                tail_fill_at(b, ("n2_channels", h))
                after(pe, n2_made, b * 2 + h + 1)
                for i in range(HT):
                    last = turn(tail_ps[:, i * P:(i + 1) * P], rows[:, HT * h + i, 0:C])
                last.then_inc(tail_full, 1)

            def logits(b):
                tail_fill_at(b, ("logits",))
                for i in range(NT):
                    last = mm(tail_ps[:, i * E:(i + 1) * E], y_cm[:, 1, i * P:(i + 1) * P], gate[:, :],
                              start=True, stop=True)
                last.then_inc(tail_full, 1)

            def ranks(b):
                tail_fill_at(b, ("ranks",))
                after(pe, route_step, b * ROUTE_STEPS + ONEHOT_STEP)
                oh = onehot[:, :, :].rearrange("p t e -> p (t e)")
                mm(tail_ps[:, 0:NT * E], tri[:, :], oh, start=True, stop=True)
                mm(tail_ps[:, NT * E:2 * NT * E], ones[:, :], oh, start=True, stop=True).then_inc(tail_full, 1)

            walk(pe, dict(x_tokens=x_tokens, conv_qk=conv_qk, conv_v=conv_v, conv_max=conv_max,
                          conv_guard=conv_guard, conv_exp=conv_exp, conv_pv=conv_pv, a_channels=a_channels,
                          global_qk=global_qk, local_qkv=local_qkv, global_v=global_v, max_tile=max_tile,
                          guard=guard, score_tile=score_tile, pv_group=pv_group, o_tokens=o_tokens,
                          o_channels=o_channels, fuse1=fuse1, fuse2=fuse2, x1_channels=x1_channels, ffn1=ffn1,
                          ffn2=ffn2, n2_channels=n2_channels, logits=logits, ranks=ranks))

            after(pe, tail_free, B * (TAIL_TURNS + 2))
            with pe.Fori(0, E) as e:
                pe.wait_ge(erows_in, e * 16 + 16)
                for c, (lo, n) in enumerate(XT_CHUNKS):
                    if c != 1:
                        pe.wait_ge(ext_free, e * 3 + c // 2)
                    for i in range(n // P):
                        last = turn(bank[c % 2][:, i * P:(i + 1) * P], rows_e[:, lo // P + i, 0:C])
                    last.then_inc(ext_full, 1)
                pe.wait_ge(ew1_in, e * 16 + 16)
                for f in range(FC):
                    for c, (lo, n) in enumerate(XT_CHUNKS):
                        u = f * 3 + c
                        if f == 0:
                            pe.wait_ge(ext_free, e * 3 + c + 1)
                        if u >= 4:
                            pe.wait_ge(eh_free, e * FC * 3 + u - 3)
                        elif u == 0:
                            pe.wait_ge(eh_free, e * FC * 3)
                        mm(bank[2 + u % 4][:, 0:n], w1_e[:, f * P:(f + 1) * P], x_e[:, lo:lo + n],
                           start=True, stop=True).then_inc(eh_full, 1)
                pe.wait_ge(ew2_in, e * 16 + 16)
                pe.wait_ge(eh_free, (e + 1) * FC * 3)
                for c, (lo, n) in enumerate(XT_CHUNKS):
                    if c == 2:
                        pe.wait_ge(ey_free, e * 3 + 1)
                    elif c == 0:
                        pe.wait_ge(ey_free, e * 3)
                    for i in range(n // P):
                        for f in range(FC):
                            last = mm(bank[6 + c % 2][:, i * C:(i + 1) * C], hid_e[f][:, lo + i * P:lo + (i + 1) * P],
                                      w2_e[:, f, :], start=(f == 0), stop=(f == FC - 1))
                    last.then_inc(ey_full, 1)

            pe.wait_ge(ey_free, E * 3)
            with pe.Fori(0, B) as b:
                for k in range(2):
                    pe.wait_ge(fin_in[k], b * 16 + 16)
                    pe.wait_ge(fin_made[k], b)
                    for i in range(HT):
                        last = turn(bank[k][:, i * P:(i + 1) * P], fin_tok[k][:, i, :])
                    last.then_inc(fin_full[k], 1)

        @block.scalar
        def _(act):
            def to(dst, src, **kw):
                return nc.scalar.activation(dst, src, ACT.Identity if kw else ACT.Copy, **kw)

            act.wait_ge(weights_used, len(NAT) + 5)

            def x_tokens(b, h):
                ps, free = head_read(act, b, ("x_tokens", h))
                if h == 0 and not (isinstance(b, int) and b == 0):
                    after(act, kept, b * 32)
                to(t_tok[:, HT * h:HT * h + HT, :], ps[:, :].rearrange("p (t c) -> p t c", c=C))\
                    .then_inc(free, 1)

            def split_load(b, use, w, h, rows_, bias, scale):
                ps, free = head_read(act, b, use)
                if h == 0:
                    after(act, split_out, b * 48 + 16 * w)
                n = slice(h * HN, (h + 1) * HN)
                to(parts[0:rows_, 0, n], ps[0:rows_, :], bias=bias, scale=scale)
                to(split_x[0:rows_, n], ps[0:rows_, :], bias=bias, scale=scale)\
                    .then_inc(free, 1)

            def conv_qk(b, h):
                split_load(b, ("conv_qk", h), 0, h, 2 * D, cols[0:2 * D, COL["conv"]:COL["conv"] + 1], 1.0)

            def global_qk(b, w, h):
                if w == 0:
                    split_load(b, ("global_qk", w, h), 1, h, C, hcols[:, 0:1], 0.25)
                else:
                    split_load(b, ("global_qk", w, h), 2, h, C, cols[:, COL["gk"]:COL["gk"] + 1], 1.0)

            def conv_guard(b):
                ps, free = head_read(act, b, ("conv_guard",))
                after(act, cguard_in, b * 48)
                to(cneg_rows[:, :], ps[:, :].bitcast(BF16)[0:3 * NT, 0:P]).then_inc(free, 1)

            def conv_exp(b, h, j):
                ps, free = head_read(act, b, ("conv_exp", h, j))
                if j == 0 and not (isinstance(b, int) and b == 0 and h == 0):
                    k = HEAD_BANK["conv_pv", NT - 1 if h == 0 else HT - 1]
                    n = HEAD_TURN["conv_pv", NT - 1 if h == 0 else HT - 1]
                    after(act, head_full[k], (b - 1 if h == 0 else b) * HEAD_TURNS[k] + n + 1)
                nc.scalar.activation(cprob[:, j, :], ps[:, :], ACT.Exp).then_inc(free, 1)

            def a_channels(b, h):
                ps, free = head_read(act, b, ("a_channels", h))
                if h == 0 and not (isinstance(b, int) and b == 0):
                    tail_done(act, b - 1, ("global_v", 1))
                to(a_cm[:, h * HN:(h + 1) * HN], ps[:, :]).then_inc(free, 1)

            def score_tile(b, quad, n):
                after(act, score_full, b * 2 * TILES + quad * TILES + n + 1)
                g, h = n // QH, n % QH
                if h == 0 and not (isinstance(b, int) and b == 0 and quad == 0 and g < 2):
                    after(act, pv_made, b * 2 * GROUPS + quad * GROUPS + g - 1)
                nc.scalar.activation(prob[:, g % 2, h, :], score_ps[n % 2][:, :], ACT.Exp).then_inc(exp_made, 1)

            def o_copy(b, quad, h):
                after(act, pv_made, b * 2 * GROUPS + quad * GROUPS + (h + 1) * NT)
                if not (isinstance(b, int) and b == 0):
                    tail_done(act, b - 1, ("o_tokens", quad, h))
                to(o_raw[:, quad, h, :], o_ps[:, :]).then_inc(o_copied, 1)

            def local_max(b, g):
                after(act, local_step, b * 28 + 7 * g + 4)
                nc.scalar.activation(ls[:, :, :, :], ls[:, :, :, :], ACT.Exp, scale=float(1.0 / np.sqrt(LD)))\
                    .then_inc(lexp_made, 1)

            def tail_wait(b, use):
                after(act, tail_full, tail_count(b, use) + 1)

            def o_channels(b, w, h):
                tail_wait(b, ("o_channels", w, h))
                to(y_cm[:, w, h * HN:(h + 1) * HN], tail_ps[:, :]).then_inc(tail_free, 1)

            def silu(b, use, count, bias):
                tail_wait(b, use)
                if not (isinstance(b, int) and b == 0 and count == 0):
                    after(act, hid_made, b * 8 + count)
                nc.scalar.activation(tanh_t[:, :], tail_ps[:, :], ACT.Tanh, bias=bias, scale=0.5)
                to(half_t[:, :], tail_ps[:, :], bias=bias, scale=0.5).then_inc(tail_free, 1)

            def fuse1(b, m, h):
                silu(b, ("fuse1", m, h), 2 * h + m, hcols[:, 1 + m:2 + m])

            def ffn1(b, m, h):
                silu(b, ("ffn1", m, h), 4 + 2 * h + m, hcols[:, 3 + m:4 + m])

            def x1_channels(b, h):
                tail_wait(b, ("x1_channels", h))
                to(y_cm[:, 0, h * HN:(h + 1) * HN], tail_ps[:, :]).then_inc(tail_free, 1)

            def n2_channels(b, h):
                tail_wait(b, ("n2_channels", h))
                to(y_cm[:, 1, h * HN:(h + 1) * HN], tail_ps[:, :]).then_inc(tail_free, 1)

            def ranks(b):
                after(act, route_step, b * ROUTE_STEPS + 2)
                nc.scalar.activation(lge[:, :, :], lg[:, :, :], ACT.Exp).then_inc(lexpert, 1)

            walk(act, dict(x_tokens=x_tokens, conv_qk=conv_qk, conv_guard=conv_guard, conv_exp=conv_exp,
                           a_channels=a_channels, global_qk=global_qk, score_tile=score_tile, o_copy=o_copy,
                           local_max=local_max, o_channels=o_channels, fuse1=fuse1, x1_channels=x1_channels, ffn1=ffn1,
                           n2_channels=n2_channels, ranks=ranks))

            with act.Fori(0, E) as e:
                act.wait_ge(eh_free, e * FC * 3)
                to(b1_e[:, :], b1c[:, bass.ds(e * FC, FC)]).then_inc(eb1_made, 1)
                for c, (lo, n) in enumerate(XT_CHUNKS):
                    act.wait_ge(ext_full, e * 3 + c + 1)
                    if c == 0:
                        act.wait_ge(eh_full, e * FC * 3)
                    to(x_e[:, lo:lo + n], bank[c % 2][:, 0:n]).then_inc(ext_free, 1)
                for f in range(FC):
                    for c, (lo, n) in enumerate(XT_CHUNKS):
                        u = f * 3 + c
                        act.wait_ge(eh_full, e * FC * 3 + u + 1)
                        if u == 0:
                            act.wait_ge(ey_full, e * 3)
                            act.wait_ge(eb1_made, e + 1)
                        nc.scalar.activation(hid_e[f][:, lo:lo + n], bank[2 + u % 4][:, 0:n], ACT.Relu,
                                             bias=b1_e[:, f:f + 1]).then_inc(eh_free, 1)

            with act.Fori(0, B) as b:
                for k in range(2):
                    act.wait_ge(fin_full[k], b + 1)
                    act.wait_ge(fin_out[k], b * 16)
                    to(fin_cm[k][:, 0:HN], bank[k][:, :]).then_inc(fin_made[k], 1)

        @block.vector
        def _(dve):
            v = nc.vector
            for i, (name, _, r) in enumerate(NAT):
                dve.wait_ge(weights_filled, i + 1)
                v.tensor_copy(TARGET[name], bank[i % 2][:, 0:r]).then_inc(weights_used, 1)
            n = len(NAT)
            for k, w in enumerate((fgT, flT)):
                dve.wait_ge(weights_filled, n + 1 + k)
                v.tensor_copy(w[:, :], bank[2 + k][:, 0:2 * C]).then_inc(weights_used, 1)
            dve.wait_ge(weights_used, n)
            v.tensor_scalar(hcols[:, 0:1], cols[:, COL["gq"]:COL["gq"] + 1], 0.25, None, ALU.mult)\
                .then_inc(weights_used, 1)
            v.tensor_scalar(hcols[:, 3:5], cols[:, COL["ffn0"]:COL["ffn0"] + 2], 0.5, None, ALU.mult)\
                .then_inc(weights_used, 1)
            dve.wait_ge(weights_filled, n + 3)
            v.tensor_tensor(hcols[:, 5:7], bank[4][:, 0:2], cols[:, COL["fus0"]:COL["fus0"] + 2], ALU.add)\
                .then_inc(const_dve, 1)
            dve.wait_ge(const_dve, 1)
            v.tensor_scalar(hcols[:, 1:3], hcols[:, 5:7], 0.5, None, ALU.mult).then_inc(weights_used, 1)
            dve.wait_ge(consts_made, 3)

            def split(b, w):
                r = slice(0, 2 * D if w == 0 else C)
                uses = [("conv_qk",), ("global_qk", 0), ("global_qk", 1)][w]
                head_done(dve, b, (*uses, 0), (*uses, 1))
                n = b * 9 + 3 * w
                v.tensor_tensor(split_x[r, :], split_x[r, :], parts[r, 0, :], ALU.subtract).then_inc(split_step, 1)
                after(dve, split_step, n + 1)
                v.tensor_copy(parts[r, 1, :], split_x[r, :]).then_inc(split_step, 1)
                after(dve, split_step, n + 2)
                v.tensor_tensor(parts[r, 2, :], split_x[r, :], parts[r, 1, :], ALU.subtract).then_inc(split_step, 1)

            def conv_v(b, h):
                ps, free = head_read(dve, b, ("conv_v", h))
                v.tensor_tensor(cv_tok[:, HT * h:HT * h + HT, 0:C], ps[:, :].rearrange("p (t c) -> p t c", c=C),
                                bc[:, BC["bv"], None, :].to_broadcast([P, HT, C]), ALU.add)\
                    .then_inc(free, 1)

            def conv_max(b, t):
                ps, free = head_read(dve, b, ("conv_max", t))
                v.tensor_reduce(cmax[:, t // 2, t % 2:t % 2 + 1], ps[:, :], AX.X, ALU.max)\
                    .then_inc(free, 1)

            def neg_parts(maxima, neg, rest, parts_, step, n):
                v.tensor_reduce(neg, maxima, AX.X, ALU.max, negate=True).then_inc(step, 1)
                after(dve, step, n + 1)
                v.tensor_copy(parts_[:, 0, :], neg).then_inc(step, 1)
                after(dve, step, n + 2)
                v.tensor_tensor(rest, neg, parts_[:, 0, :], ALU.subtract).then_inc(step, 1)
                after(dve, step, n + 3)
                v.tensor_copy(parts_[:, 1, :], rest).then_inc(step, 1)
                after(dve, step, n + 4)
                v.tensor_tensor(rest, rest, parts_[:, 1, :], ALU.subtract).then_inc(step, 1)
                after(dve, step, n + 5)
                v.tensor_copy(parts_[:, 2, :], rest).then_inc(step, 1)

            def conv_guard(b):
                head_done(dve, b, ("conv_max", 2 * NT - 2), ("conv_max", 2 * NT - 1))
                neg_parts(cmax[:, :, :], cneg[:, :], crest[:, :], cneg_parts, cguard_step, b * 6)

            def conv_pv(b, i):
                ps, free = head_read(dve, b, ("conv_pv", i))
                v.reciprocal(crecip[:, i:i + 1], ps[:, C:C + 1]).then_inc(crecip_made, 1)
                after(dve, crecip_made, b * NT + i + 1)
                if i == 0:
                    head_done(dve, b, ("x_tokens", 0), ("x_tokens", 1))
                v.scalar_tensor_tensor(t_tok[:, i, :], ps[:, 0:C], crecip[:, i:i + 1], t_tok[:, i, :],
                                       ALU.mult, ALU.add).then_inc(free, 1)

            def statistics(src, st, mv_, step, n):
                for i in range(HT):
                    v.bn_stats(st[:, i, :], src[:, i, :]).then_inc(step, 1)
                after(dve, step, n + HT)
                v.tensor_tensor(mv_[:, :, 0], st[:, :, 1], st[:, :, 4], ALU.add)
                v.tensor_tensor(mv_[:, :, 2], st[:, :, 1], st[:, :, 4], ALU.subtract)
                v.tensor_tensor(mv_[:, :, 1], st[:, :, 2], st[:, :, 5], ALU.add).then_inc(step, 1)
                after(dve, step, n + HT + 1)
                v.tensor_scalar(mv_[:, :, 0], mv_[:, :, 0], 0.5, None, ALU.mult)
                v.tensor_scalar(mv_[:, :, 1], mv_[:, :, 1], 1.0 / C, EPS, ALU.mult, ALU.add)
                v.tensor_tensor(mv_[:, :, 2], mv_[:, :, 2], mv_[:, :, 2], ALU.mult).then_inc(step, 1)
                after(dve, step, n + HT + 2)
                v.scalar_tensor_tensor(mv_[:, :, 1], mv_[:, :, 2], 0.25, mv_[:, :, 1], ALU.mult, ALU.add)\
                    .then_inc(step, 1)

            def normalise(dst, src, mv_, rstd_):
                for i in range(HT):
                    last = v.tensor_scalar(dst[:, i, 0:C], src[:, i, :], mv_[:, i, 0:1], rstd_[:, i:i + 1],
                                           ALU.subtract, ALU.mult)
                return last

            def stats_t(b, h):
                t = slice(HT * h, HT * h + HT)
                head_done(dve, b, ("conv_pv", HT * h + HT - 2), ("conv_pv", HT * h + HT - 1))
                if h == 1 or not (isinstance(b, int) and b == 0):
                    after(dve, a_made, b * 2 + h)
                statistics(t_tok[:, t, :], stats, mv, norm_step, b * 2 * NORM_STEPS + h * NORM_STEPS)

            def norm_t(b, h):
                t = slice(HT * h, HT * h + HT)
                if h == 0:
                    after(dve, kept, b * 32)
                after(dve, norm_rstd, b * 2 + h + 1)
                normalise(a_tok[:, t, :], t_tok[:, t, :], mv, rstd).then_inc(a_made, 1)

            def local_qkv(b, i):
                ps, free = head_read(dve, b, ("local_qkv", i))
                if not (isinstance(b, int) and b == 0 and i < 2):
                    after(dve, lqkv_out[i % 2], b * HT * 32 + i // 2 * 32)
                v.tensor_tensor(lqkv[:, i % 2, :], ps[:, 0:3 * C],
                                bc[:, BC["lq"]:BC["lv"] + 1, :].rearrange("p a c -> p (a c)"), ALU.add)\
                    .then_inc(free, 1)

            def global_v(b, h):
                after(dve, tail_full, tail_count(b, ("global_v", h)) + 1)
                if h == 0:
                    after(dve, pv_made, b * 2 * GROUPS)
                v.tensor_tensor(v_tok[:, HT * h:HT * h + HT, :, 0:D],
                                tail_ps[:, :].rearrange("p (t h d) -> p t h d", h=HEADS, d=D),
                                bc[:, BC["gv"], :].rearrange("p (h d) -> p h d", d=D)[:, None, :, :]
                                .to_broadcast([P, HT, HEADS, D]), ALU.add).then_inc(tail_free, 1)

            def max_tile(b, quad, n):
                after(dve, max_full, b * 2 * (TILES + 1) + quad * (TILES + 1) + n + 1)
                h, i, j = n // (2 * NT), n // 2 % NT, n % 2
                v.tensor_reduce(gmax[:, h, i, j:j + 1], max_ps[max_bank(quad, n)][:, :], AX.X, ALU.max)\
                    .then_inc(max_free, 1)

            def guard(b, quad):
                u = b * 2 * (TILES + 1) + quad * (TILES + 1)
                after(dve, max_free, u + TILES)
                neg_parts(gmax[:, :, :, :].rearrange("p h t j -> p (h t) j"), gneg[:, :], grest[:, :], gneg_parts,
                          guard_step, b * 12 + quad * 6)
                after(dve, max_full, u + TILES + 1)
                if quad == 0:
                    after(dve, guard_in[1], b * 48)
                else:
                    after(dve, guard_in[0], (b + 1) * 48)
                v.tensor_copy(gneg_rows[:, :], max_ps[max_bank(quad, TILES)][:, :].bitcast(BF16)[0:3 * QH * NT, 0:P])\
                    .then_inc(max_free, 1)

            def tail_wait(b, use):
                after(dve, tail_full, tail_count(b, use) + 1)

            def o_tokens(b, quad, h):
                tail_wait(b, ("o_tokens", quad, h))
                ps = tail_ps[:, :].rearrange("p (t h c) -> p t h c", h=QH, c=CG)
                n = b * 4 + quad * 2 + h
                v.reciprocal(grecip[:, :, :], ps[:, :, :, D]).then_inc(grecip_made, 1)
                after(dve, grecip_made, n + 1)
                v.tensor_tensor(og_tok[:, HT * h:HT * h + HT, quad, :, :], ps[:, :, :, 0:D],
                                grecip[:, :, :, None].to_broadcast([P, HT, QH, D]), ALU.mult)\
                    .then_inc(tail_free, 1)

            def local_max(b, g):
                n = b * 28 + 7 * g
                after(dve, lprod_made, b * 4 + g + 1)
                v.tensor_reduce(ls[:, :, :, :].rearrange("p i w h -> p (i w h)"),
                                lprod[:, :, :, :].rearrange("p i w (h d) -> p (i w h) d", d=LD), AX.X, ALU.add)\
                    .then_inc(local_step, 1)
                after(dve, local_step, n + 1)
                v.tensor_tensor(ls[:, :, :, :], ls[:, :, :, :], lmask[:, 2 * g:2 * g + 2, :, :], ALU.add)\
                    .then_inc(local_step, 1)
                after(dve, local_step, n + 2)
                v.tensor_reduce(lmx[:, :, :], ls[:, :, :, :].rearrange("p i w h -> p i h w"), AX.X, ALU.max)\
                    .then_inc(local_step, 1)
                after(dve, local_step, n + 3)
                v.tensor_tensor(ls[:, :, :, :], ls[:, :, :, :], lmx[:, :, None, :].to_broadcast([P, 2, WIN, LH]),
                                ALU.subtract).then_inc(local_step, 1)

            def local_sum(b, g):
                n = b * 28 + 7 * g
                after(dve, lexp_made, b * 4 + g + 1)
                v.tensor_reduce(lsum[:, :, :], ls[:, :, :, :].rearrange("p i w h -> p i h w"), AX.X, ALU.add)\
                    .then_inc(local_step, 1)
                after(dve, local_step, n + 5)
                v.reciprocal(lsum[:, :, :], lsum[:, :, :]).then_inc(local_step, 1)
                after(dve, local_step, n + 6)
                v.tensor_tensor(ls[:, :, :, :], ls[:, :, :, :], lsum[:, :, None, :].to_broadcast([P, 2, WIN, LH]),
                                ALU.mult).then_inc(local_step, 1)

            def local_out(b, g):
                after(dve, lpv_made, b * 4 + g + 1)
                if g == 0 and not (isinstance(b, int) and b == 0):
                    after(dve, tail_full, tail_count(b - 1, ("o_channels", 1, 1)) + 1)
                v.tensor_reduce(ol_tok[:, 2 * g:2 * g + 2, :],
                                lprod[:, :, :, :].rearrange("p i w c -> p i c w"), AX.X, ALU.add).then_inc(ol_made, 1)

            def silu(b, use, m, h):
                tail_done(dve, b, use)
                v.scalar_tensor_tensor(hid[:, m, h * HN:(h + 1) * HN], tanh_t[:, :], 1.0, half_t[:, :],
                                       ALU.add, ALU.mult).then_inc(hid_made, 1)

            def fuse1(b, m, h):
                silu(b, ("fuse1", m, h), m, h)

            def ffn1(b, m, h):
                silu(b, ("ffn1", m, h), m, h)

            def residual(b, use, h):
                tail_wait(b, use)
                t = slice(HT * h, HT * h + HT)
                v.tensor_tensor(x1[:, t, :], tail_ps[:, :].rearrange("p (t c) -> p t c", c=C), a_old[:, t, :],
                                ALU.add).then_inc(tail_free, 1)

            def fuse2(b, h):
                after(dve, bias_added, b + 1)
                if h == 0:
                    after(dve, t2_out, b * 16)
                residual(b, ("fuse2", h), h)

            def ffn2(b, h):
                after(dve, x1_bias, b * 2 + h + 1)
                if h == 0:
                    after(dve, x1_bias, b * 2 + 2)
                residual(b, ("ffn2", h), h)

            def tail_statistics(b, k, src):
                statistics(src, stats2, mv2, norm2_step, b * 6 * NORM_STEPS + k * NORM_STEPS)

            def tail_normalise(b, k, src, dst):
                after(dve, norm2_rstd, b * 6 + k + 1)
                return normalise(dst, src, mv2, rstd2)

            def half(h):
                return slice(HT * h, HT * h + HT)

            def stats_u(b, h):
                if not (isinstance(b, int) and b == 0 and h == 0):
                    after(dve, n2_made if h == 0 else u_normed, b * 2 if h == 0 else b * 4 + 1)
                tail_done(dve, b, ("fuse2", h))
                tail_statistics(b, h, x1[:, half(h), :])

            def norm_u(b, h):
                tail_normalise(b, h, x1[:, half(h), :], x1[:, half(h), :]).then_inc(u_normed, 1)

            def stats_v(b, h):
                after(dve, u_normed, b * 4 + 2 + h)
                tail_done(dve, b, ("ffn2", h))
                tail_statistics(b, 2 + h, x1[:, half(h), :])

            def norm_v(b, h):
                tail_normalise(b, 2 + h, x1[:, half(h), :], x1[:, half(h), :]).then_inc(u_normed, 1)

            def stats_t2(b, h):
                after(dve, u_normed if h == 0 else n2_made, b * 4 + 4 if h == 0 else b * 2 + 1)
                after(dve, t2_made, b * 2 + h + 1)
                tail_statistics(b, 4 + h, x1[:, half(h), :])

            def norm_t2(b, h):
                if h == 0 and not (isinstance(b, int) and b == 0):
                    after(dve, rows_out, b * NT * 16)
                if h == 0 and isinstance(b, int) and b == 0:
                    after(dve, scratch_zeroed, SCRATCH_LOADS * 16)
                tail_normalise(b, 4 + h, x1[:, half(h), :], rows[:, half(h), :]).then_inc(n2_made, 1)

            def logits(b):
                tail_wait(b, ("logits",))
                n = b * ROUTE_STEPS
                k = [0]

                def step(ins):
                    k[0] += 1
                    ins.then_inc(route_step, 1)
                    after(dve, route_step, n + k[0])

                v.tensor_tensor(lg[:, :, :], tail_ps[:, 0:NT * E].rearrange("p (t e) -> p t e", e=E),
                                gate_bc[:, None, :].to_broadcast([P, NT, E]), ALU.add)\
                    .then_inc(tail_free, 1)
                tail_done(dve, b, ("logits",))
                step(v.tensor_reduce(lgm[:, :], lg[:, :, :], AX.X, ALU.max))
                step(v.tensor_tensor(lg[:, :, :], lg[:, :, :], lgm[:, :, None].to_broadcast([P, NT, E]), ALU.subtract))
                step(v.tensor_scalar(cand[:, :, :], lg[:, :, :], 0.0, FAR, ALU.is_lt, ALU.mult))
                step(v.tensor_tensor(cand[:, :, :], cand[:, :, :], experts[:, None, :].to_broadcast([P, NT, E]),
                                     ALU.add))
                step(v.tensor_reduce(idx[:, :], cand[:, :, :], AX.X, ALU.min))
                step(v.tensor_tensor(onehot[:, :, :], experts[:, None, :].to_broadcast([P, NT, E]),
                                     idx[:, :, None].to_broadcast([P, NT, E]), ALU.is_equal))
                assert k[0] == ONEHOT_STEP

            def ranks(b):
                n = b * ROUTE_STEPS
                k = [ONEHOT_STEP]

                def step(ins):
                    k[0] += 1
                    ins.then_inc(route_step, 1)
                    after(dve, route_step, n + k[0])

                after(dve, lexpert, b + 1)
                step(v.tensor_reduce(lgm[:, :], lge[:, :, :], AX.X, ALU.add))
                step(v.reciprocal(rows[:, :, C], lgm[:, :]))
                step(v.tensor_copy(rows[:, :, C + 1], token_no[:, :]))
                step(v.tensor_scalar(token_no[:, :], token_no[:, :], float(N), None, ALU.add))
                tail_wait(b, ("ranks",))
                tot = tail_ps[:, NT * E:2 * NT * E].rearrange("p (t e) -> p t e", e=E)
                for t in range(NT):
                    step(v.tensor_tensor(cum[:, t + 1, :], cum[:, t, :], tot[:, t, :], ALU.add))
                step(v.tensor_tensor(cand[:, :, :], cum[:, 0:NT, :],
                                     tail_ps[:, 0:NT * E].rearrange("p (t e) -> p t e", e=E), ALU.add))
                v.tensor_copy(cum[:, 0, :], cum[:, NT, :]).then_inc(tail_free, 1)
                step(v.tensor_tensor(cand[:, :, :], cand[:, :, :], onehot[:, :, :], ALU.mult))
                step(v.tensor_reduce(rank[:, :], cand[:, :, :], AX.X, ALU.add))
                step(v.tensor_scalar(over[:, :], rank[:, :], float(CAP), STEP_UP, ALU.is_gt, ALU.mult))
                step(v.scalar_tensor_tensor(rank[:, :], idx[:, :], float(CAP), rank[:, :], ALU.mult, ALU.add))
                v.scalar_tensor_tensor(slot[:, :], rank[:, :], -1.0, over[:, :], ALU.add, ALU.add).then_inc(routed, 1)
                assert k[0] == ROUTE_STEPS, k[0]

            walk(dve, dict(split=split, conv_v=conv_v, conv_max=conv_max, conv_guard=conv_guard, conv_pv=conv_pv,
                           stats_t=stats_t, norm_t=norm_t, local_qkv=local_qkv, global_v=global_v,
                           max_tile=max_tile, guard=guard, o_tokens=o_tokens, local_max=local_max,
                           local_sum=local_sum, local_out=local_out, fuse1=fuse1, ffn1=ffn1, fuse2=fuse2,
                           ffn2=ffn2, stats_u=stats_u, norm_u=norm_u, stats_v=stats_v, norm_v=norm_v,
                           stats_t2=stats_t2, norm_t2=norm_t2, logits=logits, ranks=ranks))

            with dve.Fori(1, E + 1) as nth:
                e = nth - 1
                dve.wait_ge(erows_in, e * 16 + 16)
                dve.wait_ge(ey_out, e * CT * 16)
                v.tensor_copy(prob_e[:, :], rows_e[:, :, C])
                v.tensor_copy(token_e[:, :], rows_e[:, :, C + 1]).then_inc(etaken, 1)
                dve.wait_ge(eb2_in, e * 16 + 16)
                dve.wait_ge(etaken, nth)
                for c, (lo, n) in enumerate(XT_CHUNKS):
                    dve.wait_ge(ey_full, e * 3 + c + 1)
                    t0, nt = lo // P, n // P
                    y = y_e[:, t0:t0 + nt, :]
                    v.tensor_tensor(y, bank[6 + c % 2][:, 0:n].rearrange("p (t c) -> p t c", c=C),
                                    b2_e[:, 0:1, :].to_broadcast([P, nt, C]), ALU.add).then_inc(ey_free, 1)
                    dve.wait_ge(ey_free, e * 3 + c + 1)
                    v.tensor_tensor(y, y, prob_e[:, t0:t0 + nt, None].to_broadcast([P, nt, C]), ALU.mult)\
                        .then_inc(ey_step, 1)
                    dve.wait_ge(ey_step, e * 3 + c + 1)
                    odd = [odd_e[:, k, 0:n].rearrange("p (t c) -> p t c", c=C) for k in range(3)]
                    v.tensor_tensor(odd[0], y, y, ALU.not_equal)
                    v.tensor_scalar(odd[1], y, MAX_F32, None, ALU.is_gt)
                    v.tensor_scalar(odd[2], y, -MAX_F32, None, ALU.is_lt).then_inc(ey_odd[c], 1)
                    dve.wait_ge(consts_made, 3)
                    dve.wait_ge(ey_odd[c], nth)
                    for k in range(3):
                        v.copy_predicated(y, odd[k], huge[:, k:k + 1, None].to_broadcast([P, nt, C]))\
                            .then_inc(ey_made[c] if k == 2 else ey_pass[c][k], 1)
                        if k < 2:
                            dve.wait_ge(consts_made, 3)
                            dve.wait_ge(ey_pass[c][k], nth)


_INS = ["x", "L0_conv_wq", "L0_conv_bq", "L0_conv_wk", "L0_conv_bk", "L0_conv_wv", "L0_conv_bv",
        "L1_attn_g_in_w", "L1_attn_g_in_b", "L1_attn_g_out_w", "L1_attn_g_out_b",
        "L1_attn_t_in_w", "L1_attn_t_in_b", "L1_attn_t_out_w", "L1_attn_t_out_b",
        "L1_attn_fus_w1", "L1_attn_fus_b1", "L1_attn_fus_w2", "L1_attn_fus_b2",
        "L1_attn_ffn_w1", "L1_attn_ffn_b1", "L1_attn_ffn_w2", "L1_attn_ffn_b2",
        "L1_attn_gn_g", "L1_attn_gn_b", "L1_attn_fn_g", "L1_attn_fn_b",
        "L1_ffn_gate_w", "L1_ffn_gate_b", "L1_ffn_w1", "L1_ffn_b1", "L1_ffn_w2", "L1_ffn_b2"]
_OUTS = [((B, C, 32, 32), "float32")]


def kernel(**inputs):
    import numpy as _np
    import concourse.bacc as _bacc
    from concourse import mybir as _mybir
    from concourse.bass_utils import run_bass_kernel_spmd as _run

    nc = _bacc.Bacc("TRN2", target_bir_lowering=False, num_devices=1)
    arrays, args = {}, []
    for name in _INS:
        a = _np.ascontiguousarray(inputs[name])
        arrays[f"in_{name}_dram"] = a
        args.append(nc.dram_tensor(f"in_{name}_dram", a.shape, _mybir.dt.from_np(a.dtype), kind="ExternalInput").ap())
    for i, (shape, dtype) in enumerate(_OUTS):
        dt = _mybir.dt.from_np(_np.dtype(dtype))
        args.append(nc.dram_tensor(f"out_{i}_dram", shape, dt, kind="ExternalOutput").ap())
    hybrid_kernel(nc, *args)
    r = _run(nc, [arrays], core_ids=[0])
    return r.results[0]["out_0_dram"]
```

```python
from contextlib import ExitStack

import numpy as np

import concourse.bass as bass
from concourse import mybir

F32 = mybir.dt.float32
BF16 = mybir.dt.bfloat16
U32 = mybir.dt.uint32
ALU = mybir.AluOpType
ACT = mybir.ActivationFunctionType
AX = mybir.AxisListType

P = 128
B = 8
N = 1024
C = 128
NT = N // P
HT = NT // 2
HN = N // 2
D = 16
HEADS = C // D
QH = 4
CG = 32
QUADS = HEADS // QH
LH = 4
LD = C // LH
WIN = 5
PAD = WIN // 2
EPS = 1e-5
Q_PART = [0, 0, 1, 0, 2, 1]
K_PART = [0, 1, 0, 2, 0, 1]
TERMS = len(Q_PART)
KROWS = TERMS * D
KM = KROWS + 3
GROUPS = 2 * NT
TILES = GROUPS * QH
E = 8
CAP = (5 * B * N) // (4 * E)
CT = CAP // P
FF = 512
FC = FF // P
ROW = C + 4
NOWHERE = 1.0e6
STEP_UP = 20000.0
MAX_F32 = 3.4028234663852886e38
FAR = 64.0
ONEHOT_STEP = 6
ROUTE_STEPS = 23
NORM_STEPS = HT + 3
SCRATCH_LOADS = 2 * B + E * CT // NT
XT_CHUNKS = [(0, 512), (512, 512), (1024, 256)]
MASKED = -1.0e30

HEAD_USES = (
    [("x_tokens", h) for h in range(2)] + [("conv_qk", h) for h in range(2)]
    + [("conv_v", h) for h in range(2)] + [("conv_max", t) for t in range(2 * NT)] + [("conv_guard",)]
    + [u for h in range(2) for u in
       [("conv_exp", h, j) for j in range(NT)] + [("conv_pv", i) for i in range(HT * h, HT * h + HT)]]
    + [("a_channels", h) for h in range(2)]
    + [u for w in range(2) for u in
       [("global_qk", w, h) for h in range(2)] + [("local_qkv", i) for i in range(HT * w, HT * w + HT)]]
)
HEAD_BANK = {u: n % 2 for n, u in enumerate(HEAD_USES)}
HEAD_TURN = {u: n // 2 for n, u in enumerate(HEAD_USES)}
HEAD_TURNS = [(len(HEAD_USES) + 1) // 2, len(HEAD_USES) // 2]
TAIL_USES = (
    [("o_tokens", q, h) for q in range(QUADS) for h in range(2)]
    + [("o_channels", w, h) for w in range(2) for h in range(2)]
    + [("fuse1", m, h) for h in range(2) for m in range(2)] + [("fuse2", h) for h in range(2)]
    + [("x1_channels", h) for h in range(2)]
    + [("ffn1", m, h) for h in range(2) for m in range(2)] + [("ffn2", h) for h in range(2)]
    + [("n2_channels", h) for h in range(2)] + [("logits",), ("ranks",)]
)
TAIL_TURN = {u: n for n, u in enumerate(TAIL_USES)}
TAIL_TURNS = len(TAIL_USES)


PARTS = {
    "score_tile": [("pe", 0.24, 0.1), ("act", 0.48, 0.1)],
    "pv_group": [("pe", 1.0, 0.1)],
    "o_copy": [("act", 0.5, 0.1)],
    "max_tile": [("pe", 0.24, 0.1), ("dve", 0.6, 0.1)],
    "guard": [("dve", 0.8, 0.1), ("pe", 0.1, 0.2)],
    "guard_rows": [("dve", 0.1, 0.1), ("sp", 0.3, 2.5)],
    "load_x": [("sp", 0.1, 4.0)],
    "x_tokens": [("pe", 0.55, 0.1), ("act", 0.5, 0.1)],
    "conv_qk": [("pe", 0.9, 0.1), ("act", 0.95, 0.1)],
    "split": [("dve", 2.7, 0.1), ("sp", 0.1, 3.0)],
    "conv_stacks": [("sp", 1.0, 3.0)],
    "conv_v": [("pe", 1.0, 0.1), ("dve", 0.6, 0.1)],
    "conv_max": [("pe", 0.24, 0.1), ("dve", 0.6, 0.1)],
    "conv_guard": [("dve", 0.6, 0.1), ("pe", 0.1, 0.2), ("act", 0.2, 0.1), ("sp", 0.3, 2.5)],
    "conv_exp": [("pe", 0.24, 0.1), ("act", 0.48, 0.1)],
    "conv_pv": [("pe", 2.4, 0.1), ("dve", 0.4, 0.1)],
    "a_channels": [("pe", 0.55, 0.1), ("act", 0.5, 0.1)],
    "keep": [("sp", 0.2, 4.0)],
    "global_qk": [("pe", 0.9, 0.1), ("act", 0.95, 0.1)],
    "local_qkv": [("pe", 0.9, 0.1), ("dve", 0.5, 0.1), ("sp", 0.2, 3.0)],
    "global_stacks": [("sp", 1.0, 4.0)],
    "global_v": [("pe", 1.0, 0.1), ("dve", 0.6, 0.1)],
    "o_tokens": [("pe", 0.55, 0.1), ("dve", 0.4, 0.1)],
    "o_channels": [("pe", 0.55, 0.1), ("act", 0.5, 0.1)],
    "recall": [("sp", 0.2, 4.0)],
    "bias": [("pool", 2.4, 0.1)],
    "local_dot": [("sp", 0.2, 4.0), ("pool", 3.0, 0.1)],
    "local_max": [("dve", 1.8, 0.1), ("act", 0.2, 0.1)],
    "local_sum": [("dve", 0.5, 0.1), ("pool", 3.0, 0.1)],
    "local_out": [("dve", 1.4, 0.1)],
    "fuse1": [("pe", 1.8, 0.1), ("act", 0.95, 0.1), ("dve", 0.6, 0.1)],
    "ffn1": [("pe", 0.9, 0.1), ("act", 0.95, 0.1), ("dve", 0.6, 0.1)],
    "fuse2": [("pe", 1.9, 0.1), ("dve", 0.6, 0.1)],
    "ffn2": [("pe", 1.9, 0.1), ("dve", 0.6, 0.1)],
    "stats_t": [("dve", 1.3, 0.1), ("pool", 0.3, 0.1)],
    "stats_u": [("dve", 1.3, 0.1), ("pool", 0.3, 0.1)],
    "stats_v": [("dve", 1.3, 0.1), ("pool", 0.3, 0.1)],
    "stats_t2": [("dve", 1.3, 0.1), ("pool", 0.3, 0.1)],
    "norm_t": [("dve", 0.6, 0.1)],
    "norm_u": [("dve", 0.6, 0.1), ("pool", 3.8, 0.1)],
    "norm_v": [("dve", 0.6, 0.1), ("pool", 3.8, 0.1)],
    "norm_t2": [("dve", 0.6, 0.1)],
    "store_t2": [("sp", 0.1, 3.0)],
    "x1_channels": [("pe", 0.55, 0.1), ("act", 0.5, 0.1)],
    "n2_channels": [("pe", 0.55, 0.1), ("act", 0.5, 0.1)],
    "logits": [("pe", 0.4, 0.1), ("dve", 1.0, 0.1)],
    "ranks": [("pe", 0.4, 0.1), ("act", 0.1, 0.1), ("dve", 2.2, 0.1)],
    "route": [("pool", 7.0, 3.0)],
}


class Steps:

    def __init__(self):
        self.steps = []
        self.found = {}
        self.uses = {}

    def add(self, chain, ahead, step, *before, banks=None):
        n = len(self.steps)
        deps = [(self.found[x], None) for x in before if x in self.found]
        held = None
        if banks:
            name, count = banks
            uses = self.uses.setdefault(name, [])
            if len(uses) >= count:
                held = uses[-count]
            uses.append(n)
        self.steps.append((chain, ahead, step, deps, held))
        self.found[ahead, step] = n

    def plan(self):
        parts, before = [], []
        part_of, last_in = {}, {}
        for n, (chain, ahead, step, deps, held) in enumerate(self.steps):
            for k, (engine, time, arrives) in enumerate(PARTS[step[0]]):
                b = set()
                if k:
                    b.add(len(parts) - 1)
                else:
                    b |= {part_of[d, "end"] for d, _ in deps}
                if engine == "pe" and held is not None:
                    b.add(part_of[held, "read"])
                if (chain, engine) in last_in:
                    b.add(last_in[chain, engine])
                last_in[chain, engine] = len(parts)
                if engine == "pe":
                    part_of[n, "read"] = len(parts) + (1 if k + 1 < len(PARTS[step[0]]) else 0)
                part_of[n, "end"] = len(parts)
                parts.append((engine, time, arrives, (ahead, step)))
                before.append(b)
        way = [0.0] * len(parts)
        for k in reversed(range(len(parts))):
            way[k] += parts[k][1] + parts[k][2]
            for b in before[k]:
                way[b] = max(way[b], way[k])
        done, free, orders = {}, {}, {}
        todo = list(range(len(parts)))
        while todo:
            at = {}
            for k in todo[:400]:
                if all(b in done for b in before[k]):
                    at[k] = max([free.get(parts[k][0], 0.0)] + [done[b] for b in before[k]])
            first = min(at.values())
            k = min((k for k in at if at[k] <= first + 0.05), key=lambda k: (-way[k], k))
            engine, time, arrives, step = parts[k]
            free[engine] = at[k] + time
            done[k] = at[k] + time + arrives
            orders.setdefault(engine, []).append(step)
            todo.remove(k)
        return orders


HEAD_PS, TAIL_PS, MAX_PS, SCORE_PS = ("head", 2), ("tail", 1), ("max", 2), ("score", 2)


def head_a(s, a):
    for h in range(2):
        s.add("head", a, ("x_tokens", h), (a, ("load_x",)), (a - 1, ("keep",)), banks=HEAD_PS)
    for h in range(2):
        s.add("head", a, ("conv_qk", h), (a, ("load_x",)), (a - 1, ("split", 2)), banks=HEAD_PS)
    s.add("head", a, ("split", 0), (a, ("conv_qk", 1)))
    s.add("head", a, ("conv_stacks",), (a, ("split", 0)))
    for h in range(2):
        s.add("head", a, ("conv_v", h), banks=HEAD_PS)
    for t in range(2 * NT):
        s.add("head", a, ("conv_max", t), (a, ("conv_stacks",)), banks=HEAD_PS)
    s.add("head", a, ("conv_guard",), (a, ("conv_max", 2 * NT - 1)), banks=HEAD_PS)


def head_b(s, a):
    for h in range(2):
        for j in range(NT):
            s.add("head", a, ("conv_exp", h, j), (a, ("conv_guard",)), (a, ("conv_pv", HT - 1)), banks=HEAD_PS)
        for i in range(HT * h, HT * h + HT):
            s.add("head", a, ("conv_pv", i), (a, ("conv_exp", h, NT - 1)), banks=HEAD_PS)
        s.add("head", a, ("stats_t", h), (a, ("conv_pv", HT * h + HT - 1)))
        s.add("head", a, ("norm_t", h), (a, ("stats_t", h)))
    s.add("head", a, ("keep",), (a, ("norm_t", 1)))
    for h in range(2):
        s.add("head", a, ("a_channels", h), (a, ("norm_t", h)), banks=HEAD_PS)
    for w in range(2):
        for h in range(2):
            s.add("head", a, ("global_qk", w, h), (a, ("a_channels", h)), (a, ("split", w)), banks=HEAD_PS)
        s.add("head", a, ("split", 1 + w), (a, ("global_qk", w, 1)))
        for i in range(HT * w, HT * w + HT):
            s.add("head", a, ("local_qkv", i), (a, ("a_channels", w)), (a, ("local_qkv", i - 2)), banks=HEAD_PS)


def maxima(s, a, quad, *before):
    for t in range(TILES):
        s.add("maxima", a, ("max_tile", quad, t), *before, banks=MAX_PS)
    s.add("maxima", a, ("guard", quad), (a, ("max_tile", quad, TILES - 1)), banks=MAX_PS)
    s.add("maxima", a, ("guard_rows", quad), (a, ("guard", quad)))


def scores(s, quad):
    def product(g):
        s.add("scores", 0, ("pv_group", quad, g), (0, ("score_tile", quad, g * QH + QH - 1)),
              (0, ("o_copy", quad, 0) if quad == 0 else ("o_copy", 0, 1)), (0, ("o_copy", 1, 0)))
        if g % NT == NT - 1:
            s.add("scores", 0, ("o_copy", quad, g // NT), (0, ("pv_group", quad, g)),
                  (-1, ("o_tokens", quad, g // NT)))

    for n in range(TILES):
        s.add("scores", 0, ("score_tile", quad, n), (0, ("guard_rows", quad)), (0, ("pv_group", quad, n // QH - 2)),
              banks=SCORE_PS)
        if n % QH == QH - 1 and n >= QH:
            product(n // QH - 1)
    product(GROUPS - 1)


def local_attention(s):
    for g in range(NT // 2):
        s.add("local", 0, ("local_dot", g), (0, ("local_out", g - 1)))
        s.add("local", 0, ("local_max", g), (0, ("local_dot", g)))
        s.add("local", 0, ("local_sum", g), (0, ("local_max", g)))
        s.add("local", 0, ("local_out", g), (0, ("local_sum", g)), (-1, ("o_channels", 1, 1)))


def tail_a(s, a):
    for q in range(QUADS):
        for h in range(2):
            s.add("tail", a, ("o_tokens", q, h), banks=TAIL_PS)
    s.add("tail", a, ("recall",))
    for w in range(2):
        for h in range(2):
            s.add("tail", a, ("o_channels", w, h), (a, ("o_tokens", 1, 1)), banks=TAIL_PS)
    s.add("tail", a, ("bias",), (a, ("recall",)))


def tail_b(s, a):
    def hidden(name, *before):
        for h in range(2):
            for m in range(2):
                s.add("tail", a, (name, m, h), *before, (a, (name, 0, 0) if m else (name, 1, 0)), banks=TAIL_PS)

    def normed(name, after, number, last):
        s.add("tail", a, ("stats_" + name, number), (a, (after, number)), (a, last))
        s.add("tail", a, ("norm_" + name, number), (a, ("stats_" + name, number)))

    hidden("fuse1", (a, ("o_channels", 1, 1)))
    for h in range(2):
        s.add("tail", a, ("fuse2", h), (a, ("fuse1", 1, h)), (a, ("bias",)), banks=TAIL_PS)
    for h in range(2):
        normed("u", "fuse2", h, ("norm_u", 0))
    for h in range(2):
        s.add("tail", a, ("x1_channels", h), (a, ("norm_u", h)), banks=TAIL_PS)
    hidden("ffn1", (a, ("x1_channels", 1)))
    for h in range(2):
        s.add("tail", a, ("ffn2", h), (a, ("ffn1", 1, h)), (a, ("norm_u", 1)), banks=TAIL_PS)
    for h in range(2):
        normed("v", "ffn2", h, ("norm_v", 0))
    for h in range(2):
        normed("t2", "norm_v", h, ("norm_t2", 0))
    s.add("tail", a, ("store_t2",), (a, ("norm_v", 1)))
    for h in range(2):
        s.add("tail", a, ("n2_channels", h), (a, ("norm_t2", h)), banks=TAIL_PS)
    s.add("tail", a, ("logits",), (a, ("n2_channels", 1)), banks=TAIL_PS)
    s.add("tail", a, ("ranks",), (a, ("logits",)), banks=TAIL_PS)
    s.add("tail", a, ("route",), (a, ("ranks",)))


def stacks(s, a, quad):
    s.add("stacks", a, ("global_stacks", quad), (a, ("split", 2)), (a - 1, ("score_tile", quad, TILES - 1)))


def values(s, a):
    for h in range(2):
        s.add("tail", a, ("global_v", h), (a, ("a_channels", 1)), (a - 1, ("pv_group", 1, GROUPS - 1)), banks=TAIL_PS)


def first_steps():
    s = Steps()
    s.add("x", 0, ("load_x",))
    head_a(s, 0)
    s.add("x", 1, ("load_x",), (0, ("conv_v", 1)))
    head_b(s, 0)
    stacks(s, 0, 0)
    stacks(s, 0, 1)
    values(s, 0)
    head_a(s, 1)
    maxima(s, 0, 0, (0, ("global_stacks", 0)))
    return s.plan()


def iteration_steps(has_tail, has_a, has_b):
    s = Steps()
    if has_a:
        s.add("x", 2, ("load_x",))
    if has_tail:
        tail_a(s, -1)
        tail_b(s, -1)
    local_attention(s)
    maxima(s, 0, 1)
    if has_b:
        head_b(s, 1)
    scores(s, 0)
    scores(s, 1)
    if has_b:
        stacks(s, 1, 0)
        maxima(s, 1, 0, (1, ("global_stacks", 0)))
        stacks(s, 1, 1)
        values(s, 1)
    if has_a:
        head_a(s, 2)
    return s.plan()


def last_steps():
    s = Steps()
    tail_a(s, 0)
    tail_b(s, 0)
    return s.plan()


def hybrid_kernel(nc, x, wq, bq, wk, bk, wv, bv, g_in_w, g_in_b, g_out_w, g_out_b, t_in_w, t_in_b, t_out_w,
                  t_out_b, fus_w1, fus_b1, fus_w2, fus_b2, ffn_w1, ffn_b1, ffn_w2, ffn_b2, gn_g, gn_b, fn_g,
                  fn_b, gate_w, gate_b, w1, b1, w2, b2, out):
    x_b = x.rearrange("b c h w -> b c (h w)")
    out_b = out.rearrange("b c h w -> b c (h w)")

    parts_d = nc.dram_tensor("parts_d", [B, 3, 3, C, N], BF16).ap()
    kv_d = nc.dram_tensor("kv_d", [B, N + 2 * PAD, 2 * C], F32)
    kv_a = kv_d.ap()
    ql_d = nc.dram_tensor("ql_d", [B, N, C], F32).ap()
    kept_d = nc.dram_tensor("kept_d", [B, 2, P, NT, C], F32).ap()
    t2_d = nc.dram_tensor("t2_d", [B * N, C], F32).ap()
    rows_d = nc.dram_tensor("rows_d", [E * CAP, ROW], F32).ap()

    ctx = ExitStack()
    with ctx:
        def sb(name, shape, dt=F32):
            return ctx.enter_context(nc.sbuf_tensor(name, shape, dt))

        def sem(name):
            return ctx.enter_context(nc.semaphore(name))

        bank = [ctx.enter_context(nc.psum_tensor(f"bank{i}", [P, HN], F32)) for i in range(8)]
        head_ps = bank[0:2]
        max_ps = bank[2:4]
        score_ps = bank[4:6]
        o_ps = bank[6]
        tail_ps = bank[7]

        ident = sb("ident", [P, P])
        identb = sb("identb", [P, P], BF16)
        ones = sb("ones", [P, P])
        tri = sb("tri", [P, P])
        lmask = sb("lmask", [P, NT, WIN, LH])
        experts = sb("experts", [P, E])
        half_pow = sb("half_pow", [P, NT])
        cqkT = sb("cqkT", [P, 2 * D])
        cvw = sb("cvw", [P, C])
        gT = sb("gT", [P, 3, C])
        lT = sb("lT", [P, 3 * C])
        fgT = sb("fgT", [P, 2 * C])
        flT = sb("flT", [P, 2 * C])
        f2T = sb("f2T", [P, 2, C])
        n1T = sb("n1T", [P, 2 * C])
        n2wT = sb("n2wT", [P, 2, C])
        gate = sb("gate", [P, E])
        cols = sb("cols", [P, 16])
        hcols = sb("hcols", [P, 16])
        b1c = sb("b1c", [P, E * FC])
        bc = sb("bc", [P, 10, C])
        gate_bc = sb("gate_bc", [P, E])
        BC = {n: i for i, n in enumerate(["bv", "gv", "lq", "lk", "lv", "fus_b2", "gn_g", "gn_b", "ffn_b2", "fn_g"])}
        fnb_bc = sb("fnb_bc", [P, C])

        x_cm = sb("x_cm", [P, N])
        split_x = sb("split_x", [P, N])
        parts = sb("parts", [P, 3, N], BF16)
        cq_stack = sb("cq_stack", [P, N], BF16)
        ck_stack = sb("ck_stack", [P, N], BF16)
        cprob = sb("cprob", [P, NT, HN])
        cv_tok = sb("cv_tok", [P, NT, C + 1])
        t_tok = sb("t_tok", [P, NT, C])
        a_tok = sb("a_tok", [P, NT, C])
        a_cm = sb("a_cm", [P, N])
        cmax = sb("cmax", [P, NT, 2])
        cneg = sb("cneg", [P, NT])
        crest = sb("crest", [P, NT])
        cneg_parts = sb("cneg_parts", [P, 3, NT], BF16)
        cneg_rows = sb("cneg_rows", [3 * NT, P], BF16)
        crecip = sb("crecip", [P, NT])
        stats = sb("stats", [P, HT, 6])
        mv = sb("mv", [P, HT, 3])
        rstd = sb("rstd", [P, HT])
        lqkv = sb("lqkv", [P, 2, 3 * C])

        q_stack = [sb(f"q_stack{q}", [P, QH, N], BF16) for q in range(QUADS)]
        k_stack = [sb(f"k_stack{q}", [P, QH, N], BF16) for q in range(QUADS)]
        v_tok = sb("v_tok", [P, NT, HEADS, CG])
        prob = sb("prob", [P, 2, QH, HN])
        gmax = sb("gmax", [P, QH, NT, 2])
        gneg = sb("gneg", [P, QH * NT])
        grest = sb("grest", [P, QH * NT])
        gneg_parts = sb("gneg_parts", [P, 3, QH * NT], BF16)
        gneg_rows = sb("gneg_rows", [3 * QH * NT, P], BF16)
        o_raw = sb("o_raw", [P, QUADS, 2, HN])
        og_tok = sb("og_tok", [P, NT, QUADS, QH, D])
        grecip = sb("grecip", [P, HT, QH])
        kv_win = sb("kv_win", [P, 2, WIN, 2 * C])
        ql_tok = sb("ql_tok", [P, 2, C])
        lprod = sb("lprod", [P, 2, WIN, C])
        ls = sb("ls", [P, 2, WIN, LH])
        lmx = sb("lmx", [P, 2, LH])
        lsum = sb("lsum", [P, 2, LH])
        ol_tok = sb("ol_tok", [P, NT, C])

        t_old = sb("t_old", [P, NT, C])
        a_old = sb("a_old", [P, NT, C])
        y_cm = sb("y_cm", [P, 2, N])
        hid = sb("hid", [P, 2, N])
        tanh_t = sb("tanh_t", [P, HN])
        half_t = sb("half_t", [P, HN])
        x1 = sb("x1", [P, NT, C])
        stats2 = sb("stats2", [P, HT, 6])
        mv2 = sb("mv2", [P, HT, 3])
        rstd2 = sb("rstd2", [P, HT])
        rows = sb("rows", [P, NT, ROW])
        lg = sb("lg", [P, NT, E])
        lgm = sb("lgm", [P, NT])
        lge = sb("lge", [P, NT, E])
        cand = sb("cand", [P, NT, E])
        idx = sb("idx", [P, NT])
        onehot = sb("onehot", [P, NT, E])
        cum = sb("cum", [P, NT + 1, E])
        rank = sb("rank", [P, NT])
        over = sb("over", [P, NT])
        slot = sb("slot", [P, NT], U32)
        token_no = sb("token_no", [P, NT])

        rows_e = cprob[:, :, :].rearrange("p a b -> p (a b)")[:, 0:CT * ROW].rearrange("p (t r) -> p t r", r=ROW)
        stk = [q_stack[0], q_stack[1], k_stack[0], k_stack[1]]
        hid_e = [s[:, :, :].rearrange("p a b -> p (a b)").bitcast(F32)[:, 0:CAP] for s in stk]
        x_e = prob[:, :, :, :].rearrange("p a b c -> p (a b c)")[:, 0:CAP]
        y_e = v_tok[:, :, :, :].rearrange("p a b c -> p (a b c)")[:, 0:CAP].rearrange("p (t c) -> p t c", c=C)
        w1_e = x_cm[:, 0:FF]
        w2_e = x_cm[:, FF:2 * FF].rearrange("p (f c) -> p f c", c=C)
        b2_e = t_tok
        b1_e = sb("b1_e", [P, FC])
        prob_e = sb("prob_e", [P, CT])
        token_e = sb("token_e", [P, CT], U32)
        odd_e = hid[:, :, :].rearrange("p a b -> p (a b)")[:, 0:3 * HN].rearrange("p (k n) -> p k n", k=3).bitcast(U32)
        huge = sb("huge", [P, 3])
        zero_rows = lprod[0:PAD, 0, 0:2, :].rearrange("p a c -> p (a c)")
        nat = cprob[:, :, :].rearrange("p a b -> p (a b)")
        fin_tok = [a_tok, t_old]
        fin_cm = [hid[:, 0, :], hid[:, 1, :]]

        consts_made = sem("consts_made")
        const_step = sem("const_step")
        const_dve = sem("const_dve")
        weights_in = sem("weights_in")
        weights_filled = sem("weights_filled")
        weights_used = sem("weights_used")
        scratch_zeroed = sem("scratch_zeroed")
        x_in = sem("x_in")
        kept = sem("kept")
        recalled = sem("recalled")
        head_full = [sem(f"head_full{k}") for k in range(2)]
        head_free = [sem(f"head_free{k}") for k in range(2)]
        split_step = sem("split_step")
        split_out = sem("split_out")
        cstacks_in = sem("cstacks_in")
        cguard_step = sem("cguard_step")
        cguard_in = sem("cguard_in")
        cpv_made = sem("cpv_made")
        crecip_made = sem("crecip_made")
        norm_step = sem("norm_step")
        norm_rstd = sem("norm_rstd")
        a_made = sem("a_made")
        lqkv_out = [sem(f"lqkv_out{k}") for k in range(2)]
        gstacks_in = [sem(f"gstacks_in{q}") for q in range(QUADS)]
        max_full = sem("max_full")
        max_free = sem("max_free")
        guard_step = sem("guard_step")
        guard_in = [sem(f"guard_in{q}") for q in range(QUADS)]
        score_full = sem("score_full")
        exp_made = sem("exp_made")
        pv_made = sem("pv_made")
        o_copied = sem("o_copied")
        grecip_made = sem("grecip_made")
        kv_in = sem("kv_in")
        lprod_made = sem("lprod_made")
        local_step = sem("local_step")
        lexp_made = sem("lexp_made")
        lpv_made = sem("lpv_made")
        ol_made = sem("ol_made")
        tail_full = sem("tail_full")
        tail_free = sem("tail_free")
        hid_made = sem("hid_made")
        bias_added = sem("bias_added")
        norm2_step = sem("norm2_step")
        norm2_rstd = sem("norm2_rstd")
        u_normed = sem("u_normed")
        affine_step = sem("affine_step")
        x1_made = sem("x1_made")
        x1_bias = sem("x1_bias")
        t2_made = sem("t2_made")
        t2_out = sem("t2_out")
        n2_made = sem("n2_made")
        route_step = sem("route_step")
        lexpert = sem("lexpert")
        routed = sem("routed")
        rows_out = sem("rows_out")
        erows_in = sem("erows_in")
        ew1_in = sem("ew1_in")
        ew2_in = sem("ew2_in")
        eb2_in = sem("eb2_in")
        ext_full = sem("ext_full")
        ext_free = sem("ext_free")
        eh_full = sem("eh_full")
        eh_free = sem("eh_free")
        ey_full = sem("ey_full")
        ey_free = sem("ey_free")
        etaken = sem("etaken")
        ey_step = sem("ey_step")
        eb1_made = sem("eb1_made")
        ey_odd = [sem(f"ey_odd{c}") for c in range(3)]
        ey_pass = [[sem(f"ey_pass{c}{k}") for k in range(2)] for c in range(3)]
        ey_made = [sem(f"ey_made{c}") for c in range(3)]
        ey_out = sem("ey_out")
        fin_in = [sem(f"fin_in{k}") for k in range(2)]
        fin_full = [sem(f"fin_full{k}") for k in range(2)]
        fin_made = [sem(f"fin_made{k}") for k in range(2)]
        fin_out = [sem(f"fin_out{k}") for k in range(2)]

        def after(eng, s, count):
            if not isinstance(count, int) or count > 0:
                eng.wait_ge(s, count)

        def head_fill(pe, b, use):
            k = HEAD_BANK[use]
            after(pe, head_free[k], b * HEAD_TURNS[k] + HEAD_TURN[use])
            return head_ps[k], head_full[k]

        def head_read(eng, b, use):
            k = HEAD_BANK[use]
            after(eng, head_full[k], b * HEAD_TURNS[k] + HEAD_TURN[use] + 1)
            return head_ps[k], head_free[k]

        def head_done(eng, b, *uses):
            for use in uses:
                k = HEAD_BANK[use]
                after(eng, head_free[k], b * HEAD_TURNS[k] + HEAD_TURN[use] + 1)

        def tail_done(eng, b, use):
            after(eng, tail_free, tail_count(b, use) + 1)

        def tail_count(b, use):
            if use[0] == "global_v":
                return (0 if isinstance(b, int) and b == 0 else (b - 1) * (TAIL_TURNS + 2) + 2) + use[1]
            last = isinstance(b, int) and b == B - 1
            return b * (TAIL_TURNS + 2) + (2 if last else 4) + TAIL_TURN[use]

        def max_bank(quad, n):
            return (quad * (TILES + 1) + n) % 2

        def walk(name_, eng, steps):
            def take(orders, i):
                for ahead, (name, *args) in orders.get(name_, []):
                    steps[name](i + ahead if ahead else i, *args)
            take(first_steps(), 0)
            take(iteration_steps(False, True, True), 0)
            with eng.Fori(1, B - 2) as i:
                take(iteration_steps(True, True, True), i)
            take(iteration_steps(True, False, True), B - 2)
            take(iteration_steps(True, False, False), B - 1)
            take(last_steps(), B - 1)

        BIAS_ROWS = ["conv", "gq", "gk", "go", "to", "fus0", "fus1", "ffn0", "ffn1"]
        COL = {n: i for i, n in enumerate(BIAS_ROWS)}
        NAT = [("cqk", None, 2 * D), ("cv", wv, P)]
        NAT += [(f"g{i}", g_in_w[i * C:(i + 1) * C, :], P) for i in range(3)]
        NAT += [(f"l{i}", t_in_w[i * C:(i + 1) * C, :], P) for i in range(3)]
        NAT += [(f"f1{m}{k}", fus_w1[m * C:(m + 1) * C, k * C:(k + 1) * C], P) for m in range(2) for k in range(2)]
        NAT += [(f"f2{k}", fus_w2[:, k * C:(k + 1) * C], P) for k in range(2)]
        NAT += [(f"n1{m}", ffn_w1[m * C:(m + 1) * C, :], P) for m in range(2)]
        NAT += [(f"n2{k}", ffn_w2[:, k * C:(k + 1) * C], P) for k in range(2)]
        NAT += [("bias", None, len(BIAS_ROWS)), ("b1", b1.rearrange("e (f p) -> (e f) p", p=P), E * FC)]
        WO = {"g": len(NAT), "t": len(NAT) + 1}
        f1T = [hid[:, k, 0:2 * C] for k in range(2)]
        TARGET = {"cqk": cqkT[:, :], "cv": cvw[:, :]}
        for i in range(3):
            TARGET[f"g{i}"] = gT[:, i, :]
            TARGET[f"l{i}"] = lT[:, i * C:(i + 1) * C]
        for m in range(2):
            for k in range(2):
                TARGET[f"f1{m}{k}"] = f1T[k][:, m * C:(m + 1) * C]
            TARGET[f"f2{m}"] = f2T[:, m, :]
            TARGET[f"n1{m}"] = n1T[:, m * C:(m + 1) * C]
            TARGET[f"n2{m}"] = n2wT[:, m, :]
        TARGET["bias"] = cols[:, 0:len(BIAS_ROWS)]
        TARGET["b1"] = b1c[:, :]
        WEIGHT_LOADS = len(NAT) - 2 + 2 + 11 + 3 + len(BC) + 2

        block = ctx.enter_context(nc.Block())

        @block.sync
        def _(sp):
            def n_at(i, rows_=P, first=0):
                return nat[first:first + rows_, i * C:(i + 1) * C]

            loads = []
            for i, (name, src, r) in enumerate(NAT):
                if name == "cqk":
                    loads += [(n_at(i, D), wq), (n_at(i, D, D), wk)]
                elif name == "bias":
                    row = lambda k: nat[COL[k]:COL[k] + 1, i * C:(i + 1) * C]
                    one = lambda v, lo, hi: v[lo:hi].rearrange("(a n) -> a n", a=1)
                    loads += [(row("conv")[:, 0:D], one(bq, 0, D)), (row("conv")[:, D:2 * D], one(bk, 0, D))]
                    loads += [(row("conv")[:, 2 * D:C], one(g_in_b, 0, C - 2 * D))]
                    loads += [(row("gq"), one(g_in_b, 0, C)), (row("gk"), one(g_in_b, C, 2 * C))]
                    loads += [(row("go"), one(g_out_b, 0, C)), (row("to"), one(t_out_b, 0, C))]
                    loads += [(row(f"fus{m}"), one(fus_b1, m * C, (m + 1) * C)) for m in range(2)]
                    loads += [(row(f"ffn{m}"), one(ffn_b1, m * C, (m + 1) * C)) for m in range(2)]
                else:
                    loads.append((n_at(i, r), src))
            loads += [(n_at(WO["g"]), g_out_w), (n_at(WO["t"]), t_out_w), (gate[:, :], gate_w)]
            wide = {"bv": bv, "gv": g_in_b[2 * C:3 * C], "lq": t_in_b[0:C], "lk": t_in_b[C:2 * C],
                    "lv": t_in_b[2 * C:3 * C], "fus_b2": fus_b2, "gn_g": gn_g, "gn_b": gn_b, "ffn_b2": ffn_b2,
                    "fn_g": fn_g}
            loads += [(bc[:, BC[k], :], v.partition_broadcast(P)) for k, v in wide.items()]
            loads += [(fnb_bc[:, :], fn_b.partition_broadcast(P)), (gate_bc[:, :], gate_b.partition_broadcast(P))]
            assert len(loads) == WEIGHT_LOADS, len(loads)
            for dst, src in loads:
                sp.dma_start(dst, src).then_inc(weights_in, 16)

            sp.wait_ge(consts_made, 2)
            for b in range(B):
                sp.dma_start(kv_a[b, 0:PAD, :], zero_rows).then_inc(scratch_zeroed, 16)
                sp.dma_start(kv_a[b, N + PAD:N + 2 * PAD, :], zero_rows).then_inc(scratch_zeroed, 16)
            for e in range(E * CT // NT):
                sp.dma_start(rows_d[e * NT * P:(e + 1) * NT * P, :].rearrange("(t p) r -> p t r", p=P),
                             rows[:, :, :]).then_inc(scratch_zeroed, 16)

            def load_x(b):
                if not (isinstance(b, int) and b == 0):
                    k = HEAD_BANK["conv_v", 1]
                    after(sp, head_full[k], (b - 1) * HEAD_TURNS[k] + HEAD_TURN["conv_v", 1] + 1)
                sp.dma_start(x_cm[:, :], x_b[b]).then_inc(x_in, 16)

            def keep(b):
                after(sp, a_made, (b + 1) * 2)
                sp.dma_start(kept_d[b, 0], t_tok[:, :, :]).then_inc(kept, 16)
                sp.dma_start(kept_d[b, 1], a_tok[:, :, :]).then_inc(kept, 16)

            def recall(b):
                after(sp, kept, (b + 1) * 32)
                sp.dma_start(t_old[:, :, :], kept_d[b, 0]).then_inc(recalled, 16)
                sp.dma_start(a_old[:, :, :], kept_d[b, 1]).then_inc(recalled, 16)

            def split(b, w):
                rows_ = 2 * D if w == 0 else C
                after(sp, split_step, b * 9 + 3 * w + 3)
                sp.dma_start(parts_d[b, w].rearrange("s c n -> c s n")[0:rows_], parts[0:rows_, :, :])\
                  .then_inc(split_out, 16)

            def conv_stacks(b):
                if not (isinstance(b, int) and b == 0):
                    head_read(sp, b - 1, ("conv_exp", 1, NT - 1))
                after(sp, split_out, b * 48 + 16)
                for r in range(TERMS):
                    sp.dma_start(cq_stack[D * r:D * r + D, :], parts_d[b, 0, Q_PART[r], 0:D, :])\
                      .then_inc(cstacks_in, 16)
                    sp.dma_start(ck_stack[D * r:D * r + D, :], parts_d[b, 0, K_PART[r], D:2 * D, :])\
                      .then_inc(cstacks_in, 16)

            def conv_guard(b):
                head_done(sp, b, ("conv_guard",))
                for s in range(3):
                    dst = cq_stack[KROWS + s:KROWS + s + 1, :].rearrange("a (t p) -> a t p", p=P)
                    sp.dma_start(dst, cneg_rows[s * NT:s * NT + NT, :]).then_inc(cguard_in, 16)

            def local_qkv(b, i):
                head_done(sp, b, ("local_qkv", i))
                sp.dma_start(ql_d[b, i * P:(i + 1) * P, :], lqkv[:, i % 2, 0:C]).then_inc(lqkv_out[i % 2], 16)
                sp.dma_start(kv_a[b, PAD + i * P:PAD + (i + 1) * P, :], lqkv[:, i % 2, C:3 * C])\
                  .then_inc(lqkv_out[i % 2], 16)

            def global_stacks(b, quad):
                stored = b * 48 + 48 if isinstance(b, int) else sp.to_reg(b * 48 + 48)
                if not (isinstance(b, int) and b == 0):
                    after(sp, score_full, (b - 1) * 2 * TILES + (quad + 1) * TILES)
                after(sp, split_out, stored)
                for r in range(TERMS):
                    for w, st, part in ((1, q_stack[quad], Q_PART[r]), (2, k_stack[quad], K_PART[r])):
                        src = parts_d[b, w, part].rearrange("(h d) n -> d h n", d=D)
                        sp.dma_start(st[D * r:D * r + D, :, :], src[:, quad * QH:(quad + 1) * QH, :])\
                          .then_inc(gstacks_in[quad], 16)

            def guard_rows(b, quad):
                after(sp, max_free, b * 2 * (TILES + 1) + (quad + 1) * (TILES + 1))
                for s in range(3):
                    dst = q_stack[quad][KROWS + s:KROWS + s + 1, :, :].rearrange("a h (t p) -> a (h t) p", p=P)
                    sp.dma_start(dst, gneg_rows[s * QH * NT:(s + 1) * QH * NT, :]).then_inc(guard_in[quad], 16)

            def local_dot(b, g):
                if not (isinstance(b, int) and b == 0 and g == 0):
                    after(sp, lpv_made, b * 4 + g)
                for out_ in lqkv_out:
                    after(sp, out_, (b + 1) * HT * 32)
                after(sp, scratch_zeroed, SCRATCH_LOADS * 16)
                win = bass.AP(kv_d, (b * (N + 2 * PAD) + 2 * g * P) * 2 * C,
                              [[2 * C, P], [P * 2 * C, 2], [1, WIN * 2 * C]])
                sp.dma_start(kv_win[:, :, :, :].rearrange("p i w c -> p i (w c)"), win).then_inc(kv_in, 16)
                sp.dma_start(ql_tok[:, :, :],
                             ql_d[b, 2 * g * P:(2 * g + 2) * P, :].rearrange("(i p) c -> p i c", p=P))\
                  .then_inc(kv_in, 16)

            def store_t2(b):
                after(sp, t2_made, (b + 1) * 2)
                sp.dma_start(t2_d.rearrange("(b t p) c -> b p t c", t=NT, p=P)[b], x1[:, :, :]).then_inc(t2_out, 16)

            walk("sp", sp, dict(load_x=load_x, keep=keep, recall=recall, split=split, conv_stacks=conv_stacks,
                          conv_guard=conv_guard, local_qkv=local_qkv, global_stacks=global_stacks,
                          guard_rows=guard_rows,
                          local_dot=local_dot, store_t2=store_t2))

            sp.wait_ge(rows_out, B * NT * 16)
            rows_v = rows_d.rearrange("(e t p) r -> e p t r", t=CT, p=P)
            with sp.Fori(0, E) as e:
                sp.wait_ge(ext_full, e * 3)
                sp.wait_ge(etaken, e)
                sp.dma_start(rows_e, rows_v[e]).then_inc(erows_in, 16)
                sp.wait_ge(eh_full, e * FC * 3)
                sp.dma_start(w1_e, w1[e]).then_inc(ew1_in, 16)
                sp.wait_ge(ey_full, e * 3)
                sp.dma_start(w2_e, w2.rearrange("e (f p) c -> e p f c", p=P)[e]).then_inc(ew2_in, 16)
                sp.wait_ge(ey_free, e * 3)
                sp.dma_start(b2_e[:, 0, :], b2[e].partition_broadcast(P)).then_inc(eb2_in, 16)

            sp.wait_ge(ey_out, E * CT * 16)
            t2_v = t2_d.rearrange("(b k t p) c -> b k p t c", k=2, t=HT, p=P)
            with sp.Fori(0, B) as b:
                for k in range(2):
                    sp.wait_ge(fin_full[k], b)
                    sp.dma_start(fin_tok[k][:, 0:HT, :], t2_v[b, k]).then_inc(fin_in[k], 16)
                for k in range(2):
                    sp.wait_ge(fin_made[k], b + 1)
                    sp.dma_start(out_b[b, :, k * HN:(k + 1) * HN], fin_cm[k][:, 0:HN]).then_inc(fin_out[k], 16)
            for k in range(2):
                sp.wait_ge(fin_out[k], B * 16)

        @block.gpsimd
        def _(pool):
            last_slot = pool.to_reg(E * CAP - 1)
            last_token = pool.to_reg(B * N - 1)
            made = [0]

            def made_here(ins):
                made[0] += 1
                ins.then_inc(const_step, 1)
                pool.wait_ge(const_step, made[0])

            made_here(pool.memset(rows[:, :, :], 0.0))
            made_here(pool.memset(lprod[:, :, :, :], 0.0))
            pool.memset(rows[:, :, C + 1:C + 2], NOWHERE).then_inc(consts_made, 1)
            pool.memset(half_pow[:, :], -0.5).then_inc(consts_made, 1)
            for m in (ident, identb, tri):
                made_here(pool.memset(m[:, :], 1.0 if m is tri else 0.0))
            made_here(pool.memset(ones[:, :], 1.0))
            for m in (ident, identb):
                made_here(pool.affine_select(out=m[:, :], in_=m[:, :], compare_op=ALU.not_equal, fill=1.0,
                                             base=0, pattern=[[-1, P]], channel_multiplier=1))
            made_here(pool.affine_select(out=tri[:, :], in_=tri[:, :], compare_op=ALU.is_ge, fill=0.0,
                                         base=0, pattern=[[1, P]], channel_multiplier=-1))
            made_here(pool.memset(lmask[:, :, :, :], 0.0))
            made_here(pool.affine_select(out=lmask[:, 0, :, :], in_=lmask[:, 0, :, :], compare_op=ALU.is_ge,
                                         fill=MASKED, base=-PAD, pattern=[[1, WIN], [0, LH]], channel_multiplier=1))
            made_here(pool.affine_select(out=lmask[:, NT - 1, :, :], in_=lmask[:, NT - 1, :, :],
                                         compare_op=ALU.is_ge, fill=MASKED, base=P - 1 + PAD,
                                         pattern=[[-1, WIN], [0, LH]], channel_multiplier=-1))
            made_here(pool.iota(experts[:, :], pattern=[[1, E]], base=0, channel_multiplier=0,
                                allow_small_or_imprecise_dtypes=True))
            made_here(pool.iota(token_no[:, :], pattern=[[P, NT]], base=0, channel_multiplier=1,
                                allow_small_or_imprecise_dtypes=True))
            made_here(pool.memset(cum[:, :, :], 0.0))
            made_here(pool.memset(cv_tok[:, :, C:C + 1], 1.0))
            made_here(pool.memset(v_tok[:, :, :, :], 0.0))
            made_here(pool.memset(v_tok[:, :, :, D:D + 1], 1.0))
            made_here(pool.memset(huge[:, 0:1], 0.0))
            made_here(pool.memset(huge[:, 1:2], 10000.0))
            made_here(pool.memset(huge[:, 2:3], -10000.0))
            for s in (ck_stack[KROWS:KM, :], k_stack[0][KROWS:KM, :, :], k_stack[1][KROWS:KM, :, :]):
                made_here(pool.memset(s, 1.0))
            pool.memset(stats[:, 0, 0:1], 0.0).then_inc(consts_made, 1)

            def rms(b, in_, out_, step_sem, step, made_sem):
                after(pool, step_sem, step)
                pool.tensor_tensor(out_, in_, half_pow[:, 0:HT], ALU.pow).then_inc(made_sem, 1)

            def stats_t(b, h):
                rms(b, mv[:, :, 1], rstd[:, :], norm_step, b * 2 * NORM_STEPS + (h + 1) * NORM_STEPS, norm_rstd)

            def tail_rms(b, k):
                rms(b, mv2[:, :, 1], rstd2[:, :], norm2_step, b * 6 * NORM_STEPS + (k + 1) * NORM_STEPS, norm2_rstd)

            def wide(i, n=HT):
                return (bc[:, i, :] if isinstance(i, int) else i)[:, None, :].to_broadcast([P, n, C])

            def stats_u(b, h):
                tail_rms(b, h)

            def stats_v(b, h):
                tail_rms(b, 2 + h)

            def stats_t2(b, h):
                tail_rms(b, 4 + h)

            def local_dot(b, g):
                after(pool, kv_in, b * 128 + 32 * (g + 1))
                if not (isinstance(b, int) and b == 0 and g == 0):
                    after(pool, ol_made, b * 4 + g)
                for i in range(2):
                    m = pool.tensor_tensor(lprod[:, i, :, :], ql_tok[:, i, None, :].to_broadcast([P, WIN, C]),
                                           kv_win[:, i, :, 0:C], ALU.mult)
                m.then_inc(lprod_made, 1)

            def local_sum(b, g):
                after(pool, local_step, b * 28 + 7 * g + 7)
                for i in range(2):
                    m = pool.tensor_tensor(
                        lprod[:, i, :, :].rearrange("p w (h d) -> p w h d", d=LD),
                        ls[:, i, :, :, None].to_broadcast([P, WIN, LH, LD]),
                        kv_win[:, i, :, C:2 * C].rearrange("p w (h d) -> p w h d", d=LD), ALU.mult)
                m.then_inc(lpv_made, 1)

            def bias(b):
                after(pool, recalled, (b + 1) * 32)
                pool.tensor_tensor(a_old[:, :, :], a_old[:, :, :], wide(BC["fus_b2"], NT), ALU.add)\
                    .then_inc(bias_added, 1)

            def norm_u(b, h):
                t = slice(HT * h, HT * h + HT)
                after(pool, u_normed, b * 4 + h + 1)
                pool.tensor_tensor(x1[:, t, :], x1[:, t, :], wide(BC["gn_g"]), ALU.mult).then_inc(affine_step, 1)
                after(pool, affine_step, b * 6 + h * 1 + 1)
                pool.tensor_tensor(x1[:, t, :], x1[:, t, :], wide(BC["gn_b"]), ALU.add).then_inc(x1_made, 1)
                after(pool, x1_made, b * 2 + h + 1)
                tail_done(pool, b, ("fuse2", 1))
                pool.tensor_tensor(a_old[:, t, :], x1[:, t, :], wide(BC["ffn_b2"]), ALU.add).then_inc(x1_bias, 1)

            def norm_v(b, h):
                t = slice(HT * h, HT * h + HT)
                after(pool, u_normed, b * 4 + 2 + h + 1)
                pool.tensor_tensor(x1[:, t, :], x1[:, t, :], wide(BC["fn_g"]), ALU.mult).then_inc(affine_step, 1)
                after(pool, affine_step, b * 6 + 2 + 2 * h + 1)
                pool.tensor_tensor(x1[:, t, :], x1[:, t, :], wide(fnb_bc[:, :]), ALU.add).then_inc(affine_step, 1)
                after(pool, affine_step, b * 6 + 2 + 2 * h + 2)
                pool.tensor_tensor(x1[:, t, :], x1[:, t, :], t_old[:, t, :], ALU.add).then_inc(t2_made, 1)

            def route(b):
                pool.wait_ge(scratch_zeroed, SCRATCH_LOADS * 16)
                after(pool, routed, b + 1)
                for i in range(NT):
                    pool.indirect_dma_start(rows_d, bass.IndirectOffsetOnAxis(ap=slot[:, i:i + 1], axis=0),
                                            rows[:, i, :], None, bounds_check=last_slot, oob_is_err=False)\
                        .then_inc(rows_out, 16)

            walk("pool", pool, dict(stats_t=stats_t, local_dot=local_dot, local_sum=local_sum, bias=bias, stats_u=stats_u,
                            norm_u=norm_u, stats_v=stats_v, norm_v=norm_v, stats_t2=stats_t2, route=route))

            with pool.Fori(1, E + 1) as nth:
                for i in range(CT):
                    c = i * P // HN
                    if i * P % HN == 0:
                        pool.wait_ge(t2_out, B * 16)
                        pool.wait_ge(ey_made[c], nth)
                    pool.indirect_dma_start(t2_d, bass.IndirectOffsetOnAxis(ap=token_e[:, i:i + 1], axis=0),
                                            y_e[:, i, :], None, bounds_check=last_token, oob_is_err=False,
                                            compute_op=ALU.add).then_inc(ey_out, 16)

        @block.tensor
        def _(pe):
            mm = nc.tensor.matmul

            def turn(dst, src, n=P, identity=None):
                return nc.tensor.transpose(dst, src, ident[0:n, 0:n] if identity is None else identity)

            pe.wait_ge(consts_made, 3)
            pe.wait_ge(weights_in, WEIGHT_LOADS * 16)
            for i, (name, _, r) in enumerate(NAT):
                if i >= 2:
                    pe.wait_ge(weights_used, i - 1)
                turn(bank[i % 2][:, 0:r], nat[0:r, i * C:(i + 1) * C], r).then_inc(weights_filled, 1)
            n = len(NAT)
            pe.wait_ge(weights_used, n)
            for k, w in enumerate("gt"):
                mm(bank[2 + k][:, 0:2 * C], nat[:, WO[w] * C:(WO[w] + 1) * C], f1T[k], start=True, stop=True)\
                    .then_inc(weights_filled, 1)
            for m in range(2):
                for k, name in enumerate(("go", "to")):
                    last = mm(bank[4][:, m:m + 1], f1T[k][:, m * C:(m + 1) * C], cols[:, COL[name]:COL[name] + 1],
                              start=(k == 0), stop=(k == 1))
            last.then_inc(weights_filled, 1)
            pe.wait_ge(weights_used, n + 5)

            def x_tokens(b, h):
                ps, full = head_fill(pe, b, ("x_tokens", h))
                after(pe, x_in, (b + 1) * 16)
                for i in range(HT):
                    last = turn(ps[:, i * C:(i + 1) * C], x_cm[:, (HT * h + i) * P:(HT * h + i + 1) * P])
                last.then_inc(full, 1)

            def conv_qk(b, h):
                ps, full = head_fill(pe, b, ("conv_qk", h))
                mm(ps[0:2 * D, :], cqkT[:, :], x_cm[:, h * HN:(h + 1) * HN], start=True, stop=True).then_inc(full, 1)

            def conv_v(b, h):
                ps, full = head_fill(pe, b, ("conv_v", h))
                for i in range(HT):
                    last = mm(ps[:, i * C:(i + 1) * C], x_cm[:, (HT * h + i) * P:(HT * h + i + 1) * P], cvw[:, :],
                              start=True, stop=True)
                last.then_inc(full, 1)

            def conv_max(b, t):
                ps, full = head_fill(pe, b, ("conv_max", t))
                if t == 0:
                    after(pe, cstacks_in, (b + 1) * 12 * 16)
                i, j = t // 2, t % 2
                mm(ps[:, :], cq_stack[0:KROWS, i * P:(i + 1) * P], ck_stack[0:KROWS, j * HN:(j + 1) * HN],
                   start=True, stop=True).then_inc(full, 1)

            def conv_guard(b):
                ps, full = head_fill(pe, b, ("conv_guard",))
                after(pe, cguard_step, b * 6 + 6)
                turn(ps[:, :].bitcast(BF16)[0:3 * NT, 0:P], cneg_parts[:, :, :].rearrange("p s t -> p (s t)"),
                     identity=identb[:, :]).then_inc(full, 1)

            def conv_exp(b, h, j):
                ps, full = head_fill(pe, b, ("conv_exp", h, j))
                if h == 0 and j == 0:
                    after(pe, cguard_in, (b + 1) * 48)
                mm(ps[:, :], ck_stack[0:KM, j * P:(j + 1) * P], cq_stack[0:KM, h * HN:(h + 1) * HN],
                   start=True, stop=True).then_inc(full, 1)

            def conv_pv(b, i):
                ps, full = head_fill(pe, b, ("conv_pv", i))
                if i % HT == 0:
                    head_done(pe, b, ("conv_exp", i // HT, NT - 2), ("conv_exp", i // HT, NT - 1))
                if i == 0:
                    head_done(pe, b, ("conv_v", 0), ("conv_v", 1))
                for j in range(NT):
                    last = mm(ps[:, 0:C + 1], cprob[:, j, (i % HT) * P:(i % HT + 1) * P], cv_tok[:, j, :],
                              start=(j == 0), stop=(j == NT - 1))
                last.then_inc(full, 1)

            def a_channels(b, h):
                ps, full = head_fill(pe, b, ("a_channels", h))
                after(pe, a_made, b * 2 + h + 1)
                for i in range(HT):
                    last = turn(ps[:, i * P:(i + 1) * P], a_tok[:, HT * h + i, :])
                last.then_inc(full, 1)

            def global_qk(b, w, h):
                ps, full = head_fill(pe, b, ("global_qk", w, h))
                head_done(pe, b, ("a_channels", h))
                mm(ps[:, :], gT[:, w, :], a_cm[:, h * HN:(h + 1) * HN], start=True, stop=True).then_inc(full, 1)

            def local_qkv(b, i):
                ps, full = head_fill(pe, b, ("local_qkv", i))
                mm(ps[:, 0:3 * C], a_cm[:, i * P:(i + 1) * P], lT[:, :], start=True, stop=True).then_inc(full, 1)

            def global_v(b, h):
                tail_fill_at(b, ("global_v", h))
                for i in range(HT):
                    last = mm(tail_ps[:, i * C:(i + 1) * C], a_cm[:, (HT * h + i) * P:(HT * h + i + 1) * P],
                              gT[:, 2, :], start=True, stop=True)
                last.then_inc(tail_full, 1)

            def max_fill(b, quad, n):
                if not (isinstance(b, int) and b == 0 and quad == 0 and n < 2):
                    after(pe, max_free, b * 2 * (TILES + 1) + quad * (TILES + 1) + n - 1)

            def max_tile(b, quad, n):
                max_fill(b, quad, n)
                if n == 0:
                    after(pe, gstacks_in[quad], (b + 1) * 12 * 16)
                h, i, j = n // (2 * NT), n // 2 % NT, n % 2
                mm(max_ps[max_bank(quad, n)][:, :], q_stack[quad][0:KROWS, h, i * P:(i + 1) * P],
                   k_stack[quad][0:KROWS, h, j * HN:(j + 1) * HN], start=True, stop=True).then_inc(max_full, 1)

            def guard(b, quad):
                max_fill(b, quad, TILES)
                after(pe, guard_step, b * 12 + quad * 6 + 6)
                turn(max_ps[max_bank(quad, TILES)][:, :].bitcast(BF16)[0:3 * QH * NT, 0:P],
                     gneg_parts[:, :, :].rearrange("p s t -> p (s t)"), identity=identb[:, :]).then_inc(max_full, 1)

            def score_tile(b, quad, n):
                u = b * 2 * TILES + quad * TILES + n
                if not (isinstance(b, int) and b == 0 and quad == 0 and n < 2):
                    after(pe, exp_made, u - 1)
                if n == 0:
                    after(pe, guard_in[quad], (b + 1) * 48)
                g, h = n // QH, n % QH
                half, j = g // NT, g % NT
                mm(score_ps[n % 2][:, :], k_stack[quad][0:KM, h, j * P:(j + 1) * P],
                   q_stack[quad][0:KM, h, half * HN:(half + 1) * HN], start=True, stop=True).then_inc(score_full, 1)

            def pv_group(b, quad, g):
                half, j = g // NT, g % NT
                after(pe, exp_made, b * 2 * TILES + quad * TILES + g * QH + QH)
                if j == 0:
                    after(pe, o_copied, b * 4 + quad * 2 + half)
                if quad == 0 and g == 0:
                    tail_done(pe, b, ("global_v", 1))
                for h in range(QH):
                    last = mm(o_ps[CG * h:CG * (h + 1), :], v_tok[:, j, quad * QH + h, :], prob[:, g % 2, h, :],
                              start=(j == 0), stop=(j == NT - 1))
                last.then_inc(pv_made, 1)

            def o_tokens(b, quad, h):
                tail_fill_at(b, ("o_tokens", quad, h))
                after(pe, o_copied, b * 4 + quad * 2 + h + 1)
                for i in range(HT):
                    last = turn(tail_ps[:, i * P:(i + 1) * P], o_raw[:, quad, h, i * P:(i + 1) * P])
                last.then_inc(tail_full, 1)

            def tail_fill_at(b, use):
                after(pe, tail_free, tail_count(b, use))

            def o_channels(b, w, h):
                tail_fill_at(b, ("o_channels", w, h))
                if w == 1 and h == 0:
                    after(pe, ol_made, (b + 1) * 4)
                for i in range(HT):
                    t = HT * h + i
                    src = og_tok[:, t, :, :, :].rearrange("p q h d -> p (q h d)") if w == 0 else ol_tok[:, t, :]
                    last = turn(tail_ps[:, i * P:(i + 1) * P], src)
                last.then_inc(tail_full, 1)

            def fuse1(b, m, h):
                tail_fill_at(b, ("fuse1", m, h))
                for k, w in enumerate((fgT, flT)):
                    last = mm(tail_ps[:, :], w[:, m * C:(m + 1) * C], y_cm[:, k, h * HN:(h + 1) * HN],
                              start=(k == 0), stop=(k == 1))
                last.then_inc(tail_full, 1)

            def second(b, use, h, w, count):
                tail_fill_at(b, use)
                after(pe, hid_made, count)
                for i in range(HT):
                    t = HT * h + i
                    for k in range(2):
                        last = mm(tail_ps[:, i * C:(i + 1) * C], hid[:, k, t * P:(t + 1) * P], w[:, k, :],
                                  start=(k == 0), stop=(k == 1))
                last.then_inc(tail_full, 1)

            def fuse2(b, h):
                second(b, ("fuse2", h), h, f2T, b * 8 + 2 * h + 2)

            def ffn2(b, h):
                second(b, ("ffn2", h), h, n2wT, b * 8 + 4 + 2 * h + 2)

            def x1_channels(b, h):
                tail_fill_at(b, ("x1_channels", h))
                after(pe, x1_made, b * 2 + h + 1)
                for i in range(HT):
                    last = turn(tail_ps[:, i * P:(i + 1) * P], x1[:, HT * h + i, :])
                last.then_inc(tail_full, 1)

            def ffn1(b, m, h):
                tail_fill_at(b, ("ffn1", m, h))
                mm(tail_ps[:, :], n1T[:, m * C:(m + 1) * C], y_cm[:, 0, h * HN:(h + 1) * HN],
                   start=True, stop=True).then_inc(tail_full, 1)

            def n2_channels(b, h):
                tail_fill_at(b, ("n2_channels", h))
                after(pe, n2_made, b * 2 + h + 1)
                for i in range(HT):
                    last = turn(tail_ps[:, i * P:(i + 1) * P], rows[:, HT * h + i, 0:C])
                last.then_inc(tail_full, 1)

            def logits(b):
                tail_fill_at(b, ("logits",))
                for i in range(NT):
                    last = mm(tail_ps[:, i * E:(i + 1) * E], y_cm[:, 1, i * P:(i + 1) * P], gate[:, :],
                              start=True, stop=True)
                last.then_inc(tail_full, 1)

            def ranks(b):
                tail_fill_at(b, ("ranks",))
                after(pe, route_step, b * ROUTE_STEPS + ONEHOT_STEP)
                oh = onehot[:, :, :].rearrange("p t e -> p (t e)")
                mm(tail_ps[:, 0:NT * E], tri[:, :], oh, start=True, stop=True)
                mm(tail_ps[:, NT * E:2 * NT * E], ones[:, :], oh, start=True, stop=True).then_inc(tail_full, 1)

            walk("pe", pe, dict(x_tokens=x_tokens, conv_qk=conv_qk, conv_v=conv_v, conv_max=conv_max,
                          conv_guard=conv_guard, conv_exp=conv_exp, conv_pv=conv_pv, a_channels=a_channels,
                          global_qk=global_qk, local_qkv=local_qkv, global_v=global_v, max_tile=max_tile,
                          guard=guard, score_tile=score_tile, pv_group=pv_group, o_tokens=o_tokens,
                          o_channels=o_channels, fuse1=fuse1, fuse2=fuse2, x1_channels=x1_channels, ffn1=ffn1,
                          ffn2=ffn2, n2_channels=n2_channels, logits=logits, ranks=ranks))

            after(pe, tail_free, B * (TAIL_TURNS + 2))
            with pe.Fori(0, E) as e:
                pe.wait_ge(erows_in, e * 16 + 16)
                for c, (lo, n) in enumerate(XT_CHUNKS):
                    if c != 1:
                        pe.wait_ge(ext_free, e * 3 + c // 2)
                    for i in range(n // P):
                        last = turn(bank[c % 2][:, i * P:(i + 1) * P], rows_e[:, lo // P + i, 0:C])
                    last.then_inc(ext_full, 1)
                pe.wait_ge(ew1_in, e * 16 + 16)
                for f in range(FC):
                    for c, (lo, n) in enumerate(XT_CHUNKS):
                        u = f * 3 + c
                        if f == 0:
                            pe.wait_ge(ext_free, e * 3 + c + 1)
                        if u >= 4:
                            pe.wait_ge(eh_free, e * FC * 3 + u - 3)
                        elif u == 0:
                            pe.wait_ge(eh_free, e * FC * 3)
                        mm(bank[2 + u % 4][:, 0:n], w1_e[:, f * P:(f + 1) * P], x_e[:, lo:lo + n],
                           start=True, stop=True).then_inc(eh_full, 1)
                pe.wait_ge(ew2_in, e * 16 + 16)
                pe.wait_ge(eh_free, (e + 1) * FC * 3)
                for c, (lo, n) in enumerate(XT_CHUNKS):
                    if c == 2:
                        pe.wait_ge(ey_free, e * 3 + 1)
                    elif c == 0:
                        pe.wait_ge(ey_free, e * 3)
                    for i in range(n // P):
                        for f in range(FC):
                            last = mm(bank[6 + c % 2][:, i * C:(i + 1) * C], hid_e[f][:, lo + i * P:lo + (i + 1) * P],
                                      w2_e[:, f, :], start=(f == 0), stop=(f == FC - 1))
                    last.then_inc(ey_full, 1)

            pe.wait_ge(ey_free, E * 3)
            with pe.Fori(0, B) as b:
                for k in range(2):
                    pe.wait_ge(fin_in[k], b * 16 + 16)
                    pe.wait_ge(fin_made[k], b)
                    for i in range(HT):
                        last = turn(bank[k][:, i * P:(i + 1) * P], fin_tok[k][:, i, :])
                    last.then_inc(fin_full[k], 1)

        @block.scalar
        def _(act):
            def to(dst, src, **kw):
                return nc.scalar.activation(dst, src, ACT.Identity if kw else ACT.Copy, **kw)

            act.wait_ge(weights_used, len(NAT) + 5)

            def x_tokens(b, h):
                ps, free = head_read(act, b, ("x_tokens", h))
                if h == 0 and not (isinstance(b, int) and b == 0):
                    after(act, kept, b * 32)
                to(t_tok[:, HT * h:HT * h + HT, :], ps[:, :].rearrange("p (t c) -> p t c", c=C))\
                    .then_inc(free, 1)

            def split_load(b, use, w, h, rows_, bias, scale):
                ps, free = head_read(act, b, use)
                if h == 0:
                    after(act, split_out, b * 48 + 16 * w)
                n = slice(h * HN, (h + 1) * HN)
                to(parts[0:rows_, 0, n], ps[0:rows_, :], bias=bias, scale=scale)
                to(split_x[0:rows_, n], ps[0:rows_, :], bias=bias, scale=scale)\
                    .then_inc(free, 1)

            def conv_qk(b, h):
                split_load(b, ("conv_qk", h), 0, h, 2 * D, cols[0:2 * D, COL["conv"]:COL["conv"] + 1], 1.0)

            def global_qk(b, w, h):
                if w == 0:
                    split_load(b, ("global_qk", w, h), 1, h, C, hcols[:, 0:1], 0.25)
                else:
                    split_load(b, ("global_qk", w, h), 2, h, C, cols[:, COL["gk"]:COL["gk"] + 1], 1.0)

            def conv_guard(b):
                ps, free = head_read(act, b, ("conv_guard",))
                after(act, cguard_in, b * 48)
                to(cneg_rows[:, :], ps[:, :].bitcast(BF16)[0:3 * NT, 0:P]).then_inc(free, 1)

            def conv_exp(b, h, j):
                ps, free = head_read(act, b, ("conv_exp", h, j))
                if j == 0 and not (isinstance(b, int) and b == 0 and h == 0):
                    k = HEAD_BANK["conv_pv", NT - 1 if h == 0 else HT - 1]
                    n = HEAD_TURN["conv_pv", NT - 1 if h == 0 else HT - 1]
                    after(act, head_full[k], (b - 1 if h == 0 else b) * HEAD_TURNS[k] + n + 1)
                nc.scalar.activation(cprob[:, j, :], ps[:, :], ACT.Exp).then_inc(free, 1)

            def a_channels(b, h):
                ps, free = head_read(act, b, ("a_channels", h))
                if h == 0 and not (isinstance(b, int) and b == 0):
                    tail_done(act, b - 1, ("global_v", 1))
                to(a_cm[:, h * HN:(h + 1) * HN], ps[:, :]).then_inc(free, 1)

            def score_tile(b, quad, n):
                after(act, score_full, b * 2 * TILES + quad * TILES + n + 1)
                g, h = n // QH, n % QH
                if h == 0 and not (isinstance(b, int) and b == 0 and quad == 0 and g < 2):
                    after(act, pv_made, b * 2 * GROUPS + quad * GROUPS + g - 1)
                nc.scalar.activation(prob[:, g % 2, h, :], score_ps[n % 2][:, :], ACT.Exp).then_inc(exp_made, 1)

            def o_copy(b, quad, h):
                after(act, pv_made, b * 2 * GROUPS + quad * GROUPS + (h + 1) * NT)
                if not (isinstance(b, int) and b == 0):
                    tail_done(act, b - 1, ("o_tokens", quad, h))
                to(o_raw[:, quad, h, :], o_ps[:, :]).then_inc(o_copied, 1)

            def local_max(b, g):
                after(act, local_step, b * 28 + 7 * g + 4)
                nc.scalar.activation(ls[:, :, :, :], ls[:, :, :, :], ACT.Exp, scale=float(1.0 / np.sqrt(LD)))\
                    .then_inc(lexp_made, 1)

            def tail_wait(b, use):
                after(act, tail_full, tail_count(b, use) + 1)

            def o_channels(b, w, h):
                tail_wait(b, ("o_channels", w, h))
                to(y_cm[:, w, h * HN:(h + 1) * HN], tail_ps[:, :]).then_inc(tail_free, 1)

            def silu(b, use, count, bias):
                tail_wait(b, use)
                if not (isinstance(b, int) and b == 0 and count == 0):
                    after(act, hid_made, b * 8 + count)
                nc.scalar.activation(tanh_t[:, :], tail_ps[:, :], ACT.Tanh, bias=bias, scale=0.5)
                to(half_t[:, :], tail_ps[:, :], bias=bias, scale=0.5).then_inc(tail_free, 1)

            def fuse1(b, m, h):
                silu(b, ("fuse1", m, h), 2 * h + m, hcols[:, 1 + m:2 + m])

            def ffn1(b, m, h):
                silu(b, ("ffn1", m, h), 4 + 2 * h + m, hcols[:, 3 + m:4 + m])

            def x1_channels(b, h):
                tail_wait(b, ("x1_channels", h))
                to(y_cm[:, 0, h * HN:(h + 1) * HN], tail_ps[:, :]).then_inc(tail_free, 1)

            def n2_channels(b, h):
                tail_wait(b, ("n2_channels", h))
                to(y_cm[:, 1, h * HN:(h + 1) * HN], tail_ps[:, :]).then_inc(tail_free, 1)

            def ranks(b):
                after(act, route_step, b * ROUTE_STEPS + 2)
                nc.scalar.activation(lge[:, :, :], lg[:, :, :], ACT.Exp).then_inc(lexpert, 1)

            walk("act", act, dict(x_tokens=x_tokens, conv_qk=conv_qk, conv_guard=conv_guard, conv_exp=conv_exp,
                           a_channels=a_channels, global_qk=global_qk, score_tile=score_tile, o_copy=o_copy,
                           local_max=local_max, o_channels=o_channels, fuse1=fuse1, x1_channels=x1_channels, ffn1=ffn1,
                           n2_channels=n2_channels, ranks=ranks))

            with act.Fori(0, E) as e:
                act.wait_ge(eh_free, e * FC * 3)
                to(b1_e[:, :], b1c[:, bass.ds(e * FC, FC)]).then_inc(eb1_made, 1)
                for c, (lo, n) in enumerate(XT_CHUNKS):
                    act.wait_ge(ext_full, e * 3 + c + 1)
                    if c == 0:
                        act.wait_ge(eh_full, e * FC * 3)
                    to(x_e[:, lo:lo + n], bank[c % 2][:, 0:n]).then_inc(ext_free, 1)
                for f in range(FC):
                    for c, (lo, n) in enumerate(XT_CHUNKS):
                        u = f * 3 + c
                        act.wait_ge(eh_full, e * FC * 3 + u + 1)
                        if u == 0:
                            act.wait_ge(ey_full, e * 3)
                            act.wait_ge(eb1_made, e + 1)
                        nc.scalar.activation(hid_e[f][:, lo:lo + n], bank[2 + u % 4][:, 0:n], ACT.Relu,
                                             bias=b1_e[:, f:f + 1]).then_inc(eh_free, 1)

            with act.Fori(0, B) as b:
                for k in range(2):
                    act.wait_ge(fin_full[k], b + 1)
                    act.wait_ge(fin_out[k], b * 16)
                    to(fin_cm[k][:, 0:HN], bank[k][:, :]).then_inc(fin_made[k], 1)

        @block.vector
        def _(dve):
            v = nc.vector
            for i, (name, _, r) in enumerate(NAT):
                dve.wait_ge(weights_filled, i + 1)
                v.tensor_copy(TARGET[name], bank[i % 2][:, 0:r]).then_inc(weights_used, 1)
            n = len(NAT)
            for k, w in enumerate((fgT, flT)):
                dve.wait_ge(weights_filled, n + 1 + k)
                v.tensor_copy(w[:, :], bank[2 + k][:, 0:2 * C]).then_inc(weights_used, 1)
            dve.wait_ge(weights_used, n)
            v.tensor_scalar(hcols[:, 0:1], cols[:, COL["gq"]:COL["gq"] + 1], 0.25, None, ALU.mult)\
                .then_inc(weights_used, 1)
            v.tensor_scalar(hcols[:, 3:5], cols[:, COL["ffn0"]:COL["ffn0"] + 2], 0.5, None, ALU.mult)\
                .then_inc(weights_used, 1)
            dve.wait_ge(weights_filled, n + 3)
            v.tensor_tensor(hcols[:, 5:7], bank[4][:, 0:2], cols[:, COL["fus0"]:COL["fus0"] + 2], ALU.add)\
                .then_inc(const_dve, 1)
            dve.wait_ge(const_dve, 1)
            v.tensor_scalar(hcols[:, 1:3], hcols[:, 5:7], 0.5, None, ALU.mult).then_inc(weights_used, 1)
            dve.wait_ge(consts_made, 3)

            def split(b, w):
                r = slice(0, 2 * D if w == 0 else C)
                uses = [("conv_qk",), ("global_qk", 0), ("global_qk", 1)][w]
                head_done(dve, b, (*uses, 0), (*uses, 1))
                n = b * 9 + 3 * w
                v.tensor_tensor(split_x[r, :], split_x[r, :], parts[r, 0, :], ALU.subtract).then_inc(split_step, 1)
                after(dve, split_step, n + 1)
                v.tensor_copy(parts[r, 1, :], split_x[r, :]).then_inc(split_step, 1)
                after(dve, split_step, n + 2)
                v.tensor_tensor(parts[r, 2, :], split_x[r, :], parts[r, 1, :], ALU.subtract).then_inc(split_step, 1)

            def conv_v(b, h):
                ps, free = head_read(dve, b, ("conv_v", h))
                v.tensor_tensor(cv_tok[:, HT * h:HT * h + HT, 0:C], ps[:, :].rearrange("p (t c) -> p t c", c=C),
                                bc[:, BC["bv"], None, :].to_broadcast([P, HT, C]), ALU.add)\
                    .then_inc(free, 1)

            def conv_max(b, t):
                ps, free = head_read(dve, b, ("conv_max", t))
                v.tensor_reduce(cmax[:, t // 2, t % 2:t % 2 + 1], ps[:, :], AX.X, ALU.max)\
                    .then_inc(free, 1)

            def neg_parts(maxima, neg, rest, parts_, step, n):
                v.tensor_reduce(neg, maxima, AX.X, ALU.max, negate=True).then_inc(step, 1)
                after(dve, step, n + 1)
                v.tensor_copy(parts_[:, 0, :], neg).then_inc(step, 1)
                after(dve, step, n + 2)
                v.tensor_tensor(rest, neg, parts_[:, 0, :], ALU.subtract).then_inc(step, 1)
                after(dve, step, n + 3)
                v.tensor_copy(parts_[:, 1, :], rest).then_inc(step, 1)
                after(dve, step, n + 4)
                v.tensor_tensor(rest, rest, parts_[:, 1, :], ALU.subtract).then_inc(step, 1)
                after(dve, step, n + 5)
                v.tensor_copy(parts_[:, 2, :], rest).then_inc(step, 1)

            def conv_guard(b):
                head_done(dve, b, ("conv_max", 2 * NT - 2), ("conv_max", 2 * NT - 1))
                neg_parts(cmax[:, :, :], cneg[:, :], crest[:, :], cneg_parts, cguard_step, b * 6)

            def conv_pv(b, i):
                ps, free = head_read(dve, b, ("conv_pv", i))
                v.reciprocal(crecip[:, i:i + 1], ps[:, C:C + 1]).then_inc(crecip_made, 1)
                after(dve, crecip_made, b * NT + i + 1)
                if i == 0:
                    head_done(dve, b, ("x_tokens", 0), ("x_tokens", 1))
                v.scalar_tensor_tensor(t_tok[:, i, :], ps[:, 0:C], crecip[:, i:i + 1], t_tok[:, i, :],
                                       ALU.mult, ALU.add).then_inc(free, 1)

            def statistics(src, st, mv_, step, n):
                for i in range(HT):
                    v.bn_stats(st[:, i, :], src[:, i, :]).then_inc(step, 1)
                after(dve, step, n + HT)
                v.tensor_tensor(mv_[:, :, 0], st[:, :, 1], st[:, :, 4], ALU.add)
                v.tensor_tensor(mv_[:, :, 2], st[:, :, 1], st[:, :, 4], ALU.subtract)
                v.tensor_tensor(mv_[:, :, 1], st[:, :, 2], st[:, :, 5], ALU.add).then_inc(step, 1)
                after(dve, step, n + HT + 1)
                v.tensor_scalar(mv_[:, :, 0], mv_[:, :, 0], 0.5, None, ALU.mult)
                v.tensor_scalar(mv_[:, :, 1], mv_[:, :, 1], 1.0 / C, EPS, ALU.mult, ALU.add)
                v.tensor_tensor(mv_[:, :, 2], mv_[:, :, 2], mv_[:, :, 2], ALU.mult).then_inc(step, 1)
                after(dve, step, n + HT + 2)
                v.scalar_tensor_tensor(mv_[:, :, 1], mv_[:, :, 2], 0.25, mv_[:, :, 1], ALU.mult, ALU.add)\
                    .then_inc(step, 1)

            def normalise(dst, src, mv_, rstd_):
                for i in range(HT):
                    last = v.tensor_scalar(dst[:, i, 0:C], src[:, i, :], mv_[:, i, 0:1], rstd_[:, i:i + 1],
                                           ALU.subtract, ALU.mult)
                return last

            def stats_t(b, h):
                t = slice(HT * h, HT * h + HT)
                head_done(dve, b, ("conv_pv", HT * h + HT - 2), ("conv_pv", HT * h + HT - 1))
                if h == 1 or not (isinstance(b, int) and b == 0):
                    after(dve, a_made, b * 2 + h)
                statistics(t_tok[:, t, :], stats, mv, norm_step, b * 2 * NORM_STEPS + h * NORM_STEPS)

            def norm_t(b, h):
                t = slice(HT * h, HT * h + HT)
                if h == 0:
                    after(dve, kept, b * 32)
                after(dve, norm_rstd, b * 2 + h + 1)
                normalise(a_tok[:, t, :], t_tok[:, t, :], mv, rstd).then_inc(a_made, 1)

            def local_qkv(b, i):
                ps, free = head_read(dve, b, ("local_qkv", i))
                if not (isinstance(b, int) and b == 0 and i < 2):
                    after(dve, lqkv_out[i % 2], b * HT * 32 + i // 2 * 32)
                v.tensor_tensor(lqkv[:, i % 2, :], ps[:, 0:3 * C],
                                bc[:, BC["lq"]:BC["lv"] + 1, :].rearrange("p a c -> p (a c)"), ALU.add)\
                    .then_inc(free, 1)

            def global_v(b, h):
                after(dve, tail_full, tail_count(b, ("global_v", h)) + 1)
                if h == 0:
                    after(dve, pv_made, b * 2 * GROUPS)
                v.tensor_tensor(v_tok[:, HT * h:HT * h + HT, :, 0:D],
                                tail_ps[:, :].rearrange("p (t h d) -> p t h d", h=HEADS, d=D),
                                bc[:, BC["gv"], :].rearrange("p (h d) -> p h d", d=D)[:, None, :, :]
                                .to_broadcast([P, HT, HEADS, D]), ALU.add).then_inc(tail_free, 1)

            def max_tile(b, quad, n):
                after(dve, max_full, b * 2 * (TILES + 1) + quad * (TILES + 1) + n + 1)
                h, i, j = n // (2 * NT), n // 2 % NT, n % 2
                v.tensor_reduce(gmax[:, h, i, j:j + 1], max_ps[max_bank(quad, n)][:, :], AX.X, ALU.max)\
                    .then_inc(max_free, 1)

            def guard(b, quad):
                u = b * 2 * (TILES + 1) + quad * (TILES + 1)
                after(dve, max_free, u + TILES)
                neg_parts(gmax[:, :, :, :].rearrange("p h t j -> p (h t) j"), gneg[:, :], grest[:, :], gneg_parts,
                          guard_step, b * 12 + quad * 6)

            def guard_rows(b, quad):
                after(dve, max_full, (b * 2 + quad + 1) * (TILES + 1))
                if quad == 0:
                    after(dve, guard_in[1], b * 48)
                else:
                    after(dve, guard_in[0], (b + 1) * 48)
                v.tensor_copy(gneg_rows[:, :], max_ps[max_bank(quad, TILES)][:, :].bitcast(BF16)[0:3 * QH * NT, 0:P])\
                    .then_inc(max_free, 1)

            def tail_wait(b, use):
                after(dve, tail_full, tail_count(b, use) + 1)

            def o_tokens(b, quad, h):
                tail_wait(b, ("o_tokens", quad, h))
                ps = tail_ps[:, :].rearrange("p (t h c) -> p t h c", h=QH, c=CG)
                n = b * 4 + quad * 2 + h
                v.reciprocal(grecip[:, :, :], ps[:, :, :, D]).then_inc(grecip_made, 1)
                after(dve, grecip_made, n + 1)
                v.tensor_tensor(og_tok[:, HT * h:HT * h + HT, quad, :, :], ps[:, :, :, 0:D],
                                grecip[:, :, :, None].to_broadcast([P, HT, QH, D]), ALU.mult)\
                    .then_inc(tail_free, 1)

            def local_max(b, g):
                n = b * 28 + 7 * g
                after(dve, lprod_made, b * 4 + g + 1)
                v.tensor_reduce(ls[:, :, :, :].rearrange("p i w h -> p (i w h)"),
                                lprod[:, :, :, :].rearrange("p i w (h d) -> p (i w h) d", d=LD), AX.X, ALU.add)\
                    .then_inc(local_step, 1)
                after(dve, local_step, n + 1)
                v.tensor_tensor(ls[:, :, :, :], ls[:, :, :, :], lmask[:, 2 * g:2 * g + 2, :, :], ALU.add)\
                    .then_inc(local_step, 1)
                after(dve, local_step, n + 2)
                v.tensor_reduce(lmx[:, :, :], ls[:, :, :, :].rearrange("p i w h -> p i h w"), AX.X, ALU.max)\
                    .then_inc(local_step, 1)
                after(dve, local_step, n + 3)
                v.tensor_tensor(ls[:, :, :, :], ls[:, :, :, :], lmx[:, :, None, :].to_broadcast([P, 2, WIN, LH]),
                                ALU.subtract).then_inc(local_step, 1)

            def local_sum(b, g):
                n = b * 28 + 7 * g
                after(dve, lexp_made, b * 4 + g + 1)
                v.tensor_reduce(lsum[:, :, :], ls[:, :, :, :].rearrange("p i w h -> p i h w"), AX.X, ALU.add)\
                    .then_inc(local_step, 1)
                after(dve, local_step, n + 5)
                v.reciprocal(lsum[:, :, :], lsum[:, :, :]).then_inc(local_step, 1)
                after(dve, local_step, n + 6)
                v.tensor_tensor(ls[:, :, :, :], ls[:, :, :, :], lsum[:, :, None, :].to_broadcast([P, 2, WIN, LH]),
                                ALU.mult).then_inc(local_step, 1)

            def local_out(b, g):
                after(dve, lpv_made, b * 4 + g + 1)
                if g == 0 and not (isinstance(b, int) and b == 0):
                    after(dve, tail_full, tail_count(b - 1, ("o_channels", 1, 1)) + 1)
                v.tensor_reduce(ol_tok[:, 2 * g:2 * g + 2, :],
                                lprod[:, :, :, :].rearrange("p i w c -> p i c w"), AX.X, ALU.add).then_inc(ol_made, 1)

            def silu(b, use, m, h):
                tail_done(dve, b, use)
                v.scalar_tensor_tensor(hid[:, m, h * HN:(h + 1) * HN], tanh_t[:, :], 1.0, half_t[:, :],
                                       ALU.add, ALU.mult).then_inc(hid_made, 1)

            def fuse1(b, m, h):
                silu(b, ("fuse1", m, h), m, h)

            def ffn1(b, m, h):
                silu(b, ("ffn1", m, h), m, h)

            def residual(b, use, h):
                tail_wait(b, use)
                t = slice(HT * h, HT * h + HT)
                v.tensor_tensor(x1[:, t, :], tail_ps[:, :].rearrange("p (t c) -> p t c", c=C), a_old[:, t, :],
                                ALU.add).then_inc(tail_free, 1)

            def fuse2(b, h):
                after(dve, bias_added, b + 1)
                if h == 0:
                    after(dve, t2_out, b * 16)
                residual(b, ("fuse2", h), h)

            def ffn2(b, h):
                after(dve, x1_bias, b * 2 + h + 1)
                if h == 0:
                    after(dve, x1_bias, b * 2 + 2)
                residual(b, ("ffn2", h), h)

            def tail_statistics(b, k, src):
                statistics(src, stats2, mv2, norm2_step, b * 6 * NORM_STEPS + k * NORM_STEPS)

            def tail_normalise(b, k, src, dst):
                after(dve, norm2_rstd, b * 6 + k + 1)
                return normalise(dst, src, mv2, rstd2)

            def half(h):
                return slice(HT * h, HT * h + HT)

            def stats_u(b, h):
                if not (isinstance(b, int) and b == 0 and h == 0):
                    after(dve, n2_made if h == 0 else u_normed, b * 2 if h == 0 else b * 4 + 1)
                tail_done(dve, b, ("fuse2", h))
                tail_statistics(b, h, x1[:, half(h), :])

            def norm_u(b, h):
                tail_normalise(b, h, x1[:, half(h), :], x1[:, half(h), :]).then_inc(u_normed, 1)

            def stats_v(b, h):
                after(dve, u_normed, b * 4 + 2 + h)
                tail_done(dve, b, ("ffn2", h))
                tail_statistics(b, 2 + h, x1[:, half(h), :])

            def norm_v(b, h):
                tail_normalise(b, 2 + h, x1[:, half(h), :], x1[:, half(h), :]).then_inc(u_normed, 1)

            def stats_t2(b, h):
                after(dve, u_normed if h == 0 else n2_made, b * 4 + 4 if h == 0 else b * 2 + 1)
                after(dve, t2_made, b * 2 + h + 1)
                tail_statistics(b, 4 + h, x1[:, half(h), :])

            def norm_t2(b, h):
                if h == 0 and not (isinstance(b, int) and b == 0):
                    after(dve, rows_out, b * NT * 16)
                if h == 0 and isinstance(b, int) and b == 0:
                    after(dve, scratch_zeroed, SCRATCH_LOADS * 16)
                tail_normalise(b, 4 + h, x1[:, half(h), :], rows[:, half(h), :]).then_inc(n2_made, 1)

            def logits(b):
                tail_wait(b, ("logits",))
                n = b * ROUTE_STEPS
                k = [0]

                def step(ins):
                    k[0] += 1
                    ins.then_inc(route_step, 1)
                    after(dve, route_step, n + k[0])

                v.tensor_tensor(lg[:, :, :], tail_ps[:, 0:NT * E].rearrange("p (t e) -> p t e", e=E),
                                gate_bc[:, None, :].to_broadcast([P, NT, E]), ALU.add)\
                    .then_inc(tail_free, 1)
                tail_done(dve, b, ("logits",))
                step(v.tensor_reduce(lgm[:, :], lg[:, :, :], AX.X, ALU.max))
                step(v.tensor_tensor(lg[:, :, :], lg[:, :, :], lgm[:, :, None].to_broadcast([P, NT, E]), ALU.subtract))
                step(v.tensor_scalar(cand[:, :, :], lg[:, :, :], 0.0, FAR, ALU.is_lt, ALU.mult))
                step(v.tensor_tensor(cand[:, :, :], cand[:, :, :], experts[:, None, :].to_broadcast([P, NT, E]),
                                     ALU.add))
                step(v.tensor_reduce(idx[:, :], cand[:, :, :], AX.X, ALU.min))
                step(v.tensor_tensor(onehot[:, :, :], experts[:, None, :].to_broadcast([P, NT, E]),
                                     idx[:, :, None].to_broadcast([P, NT, E]), ALU.is_equal))
                assert k[0] == ONEHOT_STEP

            def ranks(b):
                n = b * ROUTE_STEPS
                k = [ONEHOT_STEP]

                def step(ins):
                    k[0] += 1
                    ins.then_inc(route_step, 1)
                    after(dve, route_step, n + k[0])

                after(dve, lexpert, b + 1)
                step(v.tensor_reduce(lgm[:, :], lge[:, :, :], AX.X, ALU.add))
                step(v.reciprocal(rows[:, :, C], lgm[:, :]))
                step(v.tensor_copy(rows[:, :, C + 1], token_no[:, :]))
                step(v.tensor_scalar(token_no[:, :], token_no[:, :], float(N), None, ALU.add))
                tail_wait(b, ("ranks",))
                tot = tail_ps[:, NT * E:2 * NT * E].rearrange("p (t e) -> p t e", e=E)
                for t in range(NT):
                    step(v.tensor_tensor(cum[:, t + 1, :], cum[:, t, :], tot[:, t, :], ALU.add))
                step(v.tensor_tensor(cand[:, :, :], cum[:, 0:NT, :],
                                     tail_ps[:, 0:NT * E].rearrange("p (t e) -> p t e", e=E), ALU.add))
                v.tensor_copy(cum[:, 0, :], cum[:, NT, :]).then_inc(tail_free, 1)
                step(v.tensor_tensor(cand[:, :, :], cand[:, :, :], onehot[:, :, :], ALU.mult))
                step(v.tensor_reduce(rank[:, :], cand[:, :, :], AX.X, ALU.add))
                step(v.tensor_scalar(over[:, :], rank[:, :], float(CAP), STEP_UP, ALU.is_gt, ALU.mult))
                step(v.scalar_tensor_tensor(rank[:, :], idx[:, :], float(CAP), rank[:, :], ALU.mult, ALU.add))
                v.scalar_tensor_tensor(slot[:, :], rank[:, :], -1.0, over[:, :], ALU.add, ALU.add).then_inc(routed, 1)
                assert k[0] == ROUTE_STEPS, k[0]

            walk("dve", dve, dict(split=split, conv_v=conv_v, conv_max=conv_max, conv_guard=conv_guard, conv_pv=conv_pv,
                           stats_t=stats_t, norm_t=norm_t, local_qkv=local_qkv, global_v=global_v,
                           max_tile=max_tile, guard=guard, guard_rows=guard_rows, o_tokens=o_tokens, local_max=local_max,
                           local_sum=local_sum, local_out=local_out, fuse1=fuse1, ffn1=ffn1, fuse2=fuse2,
                           ffn2=ffn2, stats_u=stats_u, norm_u=norm_u, stats_v=stats_v, norm_v=norm_v,
                           stats_t2=stats_t2, norm_t2=norm_t2, logits=logits, ranks=ranks))

            with dve.Fori(1, E + 1) as nth:
                e = nth - 1
                dve.wait_ge(erows_in, e * 16 + 16)
                dve.wait_ge(ey_out, e * CT * 16)
                v.tensor_copy(prob_e[:, :], rows_e[:, :, C])
                v.tensor_copy(token_e[:, :], rows_e[:, :, C + 1]).then_inc(etaken, 1)
                dve.wait_ge(eb2_in, e * 16 + 16)
                dve.wait_ge(etaken, nth)
                for c, (lo, n) in enumerate(XT_CHUNKS):
                    dve.wait_ge(ey_full, e * 3 + c + 1)
                    t0, nt = lo // P, n // P
                    y = y_e[:, t0:t0 + nt, :]
                    v.tensor_tensor(y, bank[6 + c % 2][:, 0:n].rearrange("p (t c) -> p t c", c=C),
                                    b2_e[:, 0:1, :].to_broadcast([P, nt, C]), ALU.add).then_inc(ey_free, 1)
                    dve.wait_ge(ey_free, e * 3 + c + 1)
                    v.tensor_tensor(y, y, prob_e[:, t0:t0 + nt, None].to_broadcast([P, nt, C]), ALU.mult)\
                        .then_inc(ey_step, 1)
                    dve.wait_ge(ey_step, e * 3 + c + 1)
                    odd = [odd_e[:, k, 0:n].rearrange("p (t c) -> p t c", c=C) for k in range(3)]
                    v.tensor_tensor(odd[0], y, y, ALU.not_equal)
                    v.tensor_scalar(odd[1], y, MAX_F32, None, ALU.is_gt)
                    v.tensor_scalar(odd[2], y, -MAX_F32, None, ALU.is_lt).then_inc(ey_odd[c], 1)
                    dve.wait_ge(consts_made, 3)
                    dve.wait_ge(ey_odd[c], nth)
                    for k in range(3):
                        v.copy_predicated(y, odd[k], huge[:, k:k + 1, None].to_broadcast([P, nt, C]))\
                            .then_inc(ey_made[c] if k == 2 else ey_pass[c][k], 1)
                        if k < 2:
                            dve.wait_ge(consts_made, 3)
                            dve.wait_ge(ey_pass[c][k], nth)


_INS = ["x", "L0_conv_wq", "L0_conv_bq", "L0_conv_wk", "L0_conv_bk", "L0_conv_wv", "L0_conv_bv",
        "L1_attn_g_in_w", "L1_attn_g_in_b", "L1_attn_g_out_w", "L1_attn_g_out_b",
        "L1_attn_t_in_w", "L1_attn_t_in_b", "L1_attn_t_out_w", "L1_attn_t_out_b",
        "L1_attn_fus_w1", "L1_attn_fus_b1", "L1_attn_fus_w2", "L1_attn_fus_b2",
        "L1_attn_ffn_w1", "L1_attn_ffn_b1", "L1_attn_ffn_w2", "L1_attn_ffn_b2",
        "L1_attn_gn_g", "L1_attn_gn_b", "L1_attn_fn_g", "L1_attn_fn_b",
        "L1_ffn_gate_w", "L1_ffn_gate_b", "L1_ffn_w1", "L1_ffn_b1", "L1_ffn_w2", "L1_ffn_b2"]
_OUTS = [((B, C, 32, 32), "float32")]


def kernel(**inputs):
    import numpy as _np
    import concourse.bacc as _bacc
    from concourse import mybir as _mybir
    from concourse.bass_utils import run_bass_kernel_spmd as _run

    nc = _bacc.Bacc("TRN2", target_bir_lowering=False, num_devices=1)
    arrays, args = {}, []
    for name in _INS:
        a = _np.ascontiguousarray(inputs[name])
        arrays[f"in_{name}_dram"] = a
        args.append(nc.dram_tensor(f"in_{name}_dram", a.shape, _mybir.dt.from_np(a.dtype), kind="ExternalInput").ap())
    for i, (shape, dtype) in enumerate(_OUTS):
        dt = _mybir.dt.from_np(_np.dtype(dtype))
        args.append(nc.dram_tensor(f"out_{i}_dram", shape, dt, kind="ExternalOutput").ap())
    hybrid_kernel(nc, *args)
    r = _run(nc, [arrays], core_ids=[0])
    return r.results[0]["out_0_dram"]
```

```python
from contextlib import ExitStack

import numpy as np

import concourse.bass as bass
from concourse import mybir

F32 = mybir.dt.float32
BF16 = mybir.dt.bfloat16
U32 = mybir.dt.uint32
ALU = mybir.AluOpType
ACT = mybir.ActivationFunctionType
AX = mybir.AxisListType

P = 128
B = 8
N = 1024
C = 128
NT = N // P
HT = NT // 2
HN = N // 2
D = 16
HEADS = C // D
QH = 4
CG = 32
QUADS = HEADS // QH
LH = 4
LD = C // LH
WIN = 5
PAD = WIN // 2
EPS = 1e-5
Q_PART = [0, 0, 1, 0, 2, 1]
K_PART = [0, 1, 0, 2, 0, 1]
TERMS = len(Q_PART)
KROWS = TERMS * D
KM = KROWS + 3
GROUPS = 2 * NT
TILES = GROUPS * QH
E = 8
CAP = (5 * B * N) // (4 * E)
CT = CAP // P
FF = 512
FC = FF // P
ROW = C + 4
NOWHERE = 1.0e6
STEP_UP = 20000.0
MAX_F32 = 3.4028234663852886e38
FAR = 64.0
ONEHOT_STEP = 6
ROUTE_STEPS = 23
NORM_STEPS = 5
SCRATCH_LOADS = 2 * B + E * CT // NT
XT_CHUNKS = [(0, 512), (512, 512), (1024, 256)]
MASKED = -1.0e30

LOCAL_AFTER = [range(0, 2), range(2, NT)]
HEAD_USES = (
    [("x_tokens", h) for h in range(2)] + [("conv_qk", h) for h in range(2)]
    + [("conv_v", h) for h in range(2)] + [("conv_max", t) for t in range(2 * NT)] + [("conv_guard",)]
    + [u for h in range(2) for u in
       [("conv_exp", h, j) for j in range(NT)] + [("conv_pv", i) for i in range(HT * h, HT * h + HT)]]
    + [("a_channels", h) for h in range(2)]
    + [u for w in range(2) for u in
       [("global_qk", w, h) for h in range(2)] + [("local_qkv", i) for i in LOCAL_AFTER[w]]]
)
HEAD_TURN = {u: n for n, u in enumerate(HEAD_USES)}
HEAD_TURNS = len(HEAD_USES)
ENDS = 4
MAX_BANKS = 3
TAIL_USES = (
    [("o_tokens", q, h) for q in range(QUADS) for h in range(2)]
    + [("o_channels", w, h) for w in range(2) for h in range(2)]
    + [u for h in range(2) for u in [("fuse1", 0, h), ("fuse1", 1, h), ("fuse2", h)]]
    + [u for h in range(2) for u in [("x1_channels", h), ("ffn1", 0, h), ("ffn1", 1, h), ("ffn2", h)]]
    + [("n2_channels", h) for h in range(2)] + [("logits",), ("ranks",)]
)
TAIL_TURN = {u: n for n, u in enumerate(TAIL_USES)}
TAIL_TURNS = len(TAIL_USES)


PARTS = {
    "score_tile": [("pe", 0.24, 0.2), ("act", 0.43, 0.2)],
    "pv_group": [("pe", 0.99, 0.2)],
    "weights": [("sp", 3.0, 15.0), ("pe", 8.0, 0.2), ("dve", 8.0, 0.2), ("act", 0.1, 0.2)],
    "o_copy": [("act", 0.48, 0.2)],
    "max_tile": [("pe", 0.22, 0.2), ("dve", 0.61, 0.2)],
    "guard": [("dve", 1.2, 0.2), ("pe", 0.11, 0.2)],
    "guard_rows": [("dve", 0.13, 0.2), ("sp", 0.3, 2.5)],
    "load_x": [("sp", 0.1, 4.0)],
    "x_tokens": [("pe", 0.55, 0.2), ("act", 0.48, 0.2)],
    "conv_qk": [("pe", 0.9, 0.2), ("act", 1.0, 0.2)],
    "split": [("dve", 1.15, 0.2), ("act", 0.94, 0.2)],
    "split_low": [("dve", 1.15, 0.2), ("sp", 0.1, 3.0)],
    "conv_stacks": [("sp", 1.0, 3.0)],
    "conv_v": [("pe", 0.87, 0.2), ("dve", 0.6, 0.2)],
    "conv_max": [("pe", 0.25, 0.2), ("dve", 0.6, 0.2)],
    "conv_guard": [("dve", 1.17, 0.2), ("pe", 0.1, 0.2), ("act", 0.2, 0.2), ("sp", 0.3, 2.5)],
    "conv_exp": [("pe", 0.25, 0.2), ("act", 0.48, 0.2)],
    "conv_pv": [("pe", 1.76, 0.2), ("dve", 0.45, 0.2)],
    "a_channels": [("pe", 0.43, 0.2), ("act", 0.48, 0.2)],
    "keep": [("sp", 0.2, 4.0)],
    "global_qk": [("pe", 0.86, 0.2), ("act", 1.0, 0.2)],
    "local_qkv": [("pe", 0.64, 0.2), ("dve", 0.47, 0.2), ("sp", 0.2, 3.0)],
    "global_stacks": [("sp", 1.0, 4.0)],
    "global_v": [("pe", 0.88, 0.2), ("dve", 0.6, 0.2)],
    "o_tokens": [("pe", 0.54, 0.2), ("dve", 0.63, 0.2)],
    "o_channels": [("pe", 0.43, 0.2), ("act", 0.48, 0.2)],
    "recall": [("sp", 0.2, 4.0)],
    "bias": [("pool", 2.3, 0.2)],
    "local_dot": [("sp", 0.2, 4.0), ("pool", 3.0, 0.2)],
    "local_max": [("dve", 2.1, 0.2), ("act", 0.21, 0.2)],
    "local_sum": [("dve", 0.55, 0.2), ("pool", 2.89, 0.2)],
    "local_out": [("dve", 1.4, 0.2)],
    "fuse1": [("pe", 1.71, 0.2), ("act", 1.0, 0.2), ("dve", 0.6, 0.2)],
    "ffn1": [("pe", 0.88, 0.2), ("act", 1.0, 0.2), ("dve", 0.6, 0.2)],
    "fuse2": [("pe", 1.74, 0.2), ("dve", 0.58, 0.2)],
    "ffn2": [("pe", 1.74, 0.2), ("dve", 0.6, 0.2)],
    "stats_t": [("dve", 0.9, 0.2), ("pool", 2.67, 0.2)],
    "stats_u": [("dve", 0.9, 0.2), ("pool", 2.8, 0.2)],
    "stats_v": [("dve", 0.86, 0.2), ("pool", 2.8, 0.2)],
    "stats_t2": [("dve", 0.9, 0.2), ("pool", 2.8, 0.2)],
    "norm_t": [("act", 0.90, 0.2)],
    "norm_u": [("act", 0.90, 0.2), ("pool", 3.9, 0.2)],
    "norm_v": [("act", 0.9, 0.2), ("pool", 3.9, 0.2)],
    "norm_t2": [("act", 0.99, 0.2)],
    "store_t2": [("sp", 0.1, 3.0)],
    "x1_channels": [("pe", 0.43, 0.2), ("act", 0.48, 0.2)],
    "n2_channels": [("pe", 0.44, 0.2), ("act", 0.47, 0.2)],
    "logits": [("pe", 1.4, 0.2), ("dve", 1.67, 0.2)],
    "ranks": [("pe", 0.37, 0.2), ("act", 0.1, 0.2), ("dve", 3.75, 0.2)],
    "route": [("pool", 8.42, 3.0)],
}


BESIDES = {"pe": 0.0, "act": 0.0, "dve": 0.0, "pool": 0.0, "sp": 0.0}
EARLIER = {"head": 0.0, "maxima": 5.0, "scores": 0.0, "tail": 0.0, "local": 1.0}
TOGETHER = 0.05


class Steps:

    def __init__(self):
        self.steps = []
        self.found = {}
        self.uses = {}

    def add(self, chain, ahead, step, *before, banks=None):
        n = len(self.steps)
        deps = [(self.found[x], None) for x in before if x in self.found]
        held = None
        if banks:
            name, count = banks
            uses = self.uses.setdefault(name, [])
            if len(uses) >= count:
                held = uses[-count]
            uses.append(n)
        self.steps.append((chain, ahead, step, deps, held))
        self.found[ahead, step] = n

    def plan(self):
        parts, before = [], []
        part_of, last_in, early = {}, {}, []
        for n, (chain, ahead, step, deps, held) in enumerate(self.steps):
            for k, (engine, time, arrives) in enumerate(PARTS[step[0]]):
                b = set()
                if k:
                    b.add(len(parts) - 1)
                else:
                    b |= {part_of[d, "end"] for d, _ in deps}
                if engine == "pe" and held is not None:
                    b.add(part_of[held, "read"])
                if (chain, engine) in last_in:
                    b.add(last_in[chain, engine])
                last_in[chain, engine] = len(parts)
                if engine == "pe":
                    part_of[n, "read"] = len(parts) + (1 if k + 1 < len(PARTS[step[0]]) else 0)
                part_of[n, "end"] = len(parts)
                parts.append((engine, time + BESIDES[engine], arrives, (ahead, step)))
                early.append(EARLIER.get(chain, 0.0))
                before.append(b)
        way = [0.0] * len(parts)
        for k in reversed(range(len(parts))):
            way[k] += parts[k][1] + parts[k][2]
            for b in before[k]:
                way[b] = max(way[b], way[k])
        done, free, orders = {}, {}, {}
        todo = list(range(len(parts)))
        while todo:
            at = {}
            for k in todo[:400]:
                if all(b in done for b in before[k]):
                    at[k] = max([free.get(parts[k][0], 0.0)] + [done[b] for b in before[k]])
            first = min(at.values())
            k = min((k for k in at if at[k] <= first + TOGETHER), key=lambda k: (-way[k] - early[k], k))
            engine, time, arrives, step = parts[k]
            free[engine] = at[k] + time
            done[k] = at[k] + time + arrives
            orders.setdefault(engine, []).append(step)
            todo.remove(k)
        return orders


HEAD_PS, TAIL_PS, MAX_PS, SCORE_PS = ("head", 1), ("tail", 1), ("max", 3), ("score", 2)


def head_a(s, a):
    for h in range(2):
        s.add("head", a, ("x_tokens", h), (a, ("load_x",)), (a - 1, ("keep",)), banks=HEAD_PS)
    for h in range(2):
        s.add("head", a, ("conv_qk", h), (a, ("load_x",)), (a - 1, ("split_low", 2)), banks=HEAD_PS)
    s.add("head", a, ("split", 0), (a, ("conv_qk", 1)))
    s.add("head", a, ("split_low", 0), (a, ("split", 0)))
    s.add("head", a, ("conv_stacks",), (a, ("split_low", 0)))
    for h in range(2):
        s.add("head", a, ("conv_v", h), banks=HEAD_PS)
    for t in range(2 * NT):
        s.add("head", a, ("conv_max", t), (a, ("conv_stacks",)), banks=HEAD_PS)
    s.add("head", a, ("conv_guard",), (a, ("conv_max", 2 * NT - 1)), banks=HEAD_PS)
    conv_half(s, a, 0)


def conv_half(s, a, h):
    for j in range(NT):
        s.add("head", a, ("conv_exp", h, j), (a, ("conv_guard",)), (a, ("conv_pv", HT - 1)),
              (a, ("weights",)), banks=HEAD_PS)
    for i in range(HT * h, HT * h + HT):
        s.add("head", a, ("conv_pv", i), (a, ("conv_exp", h, NT - 1)), banks=HEAD_PS)
    s.add("head", a, ("stats_t", h), (a, ("conv_pv", HT * h + HT - 1)))
    s.add("head", a, ("norm_t", h), (a, ("stats_t", h)))


def head_b(s, a):
    conv_half(s, a, 1)
    s.add("head", a, ("keep",), (a, ("norm_t", 1)))
    for h in range(2):
        s.add("head", a, ("a_channels", h), (a, ("norm_t", h)), banks=HEAD_PS)
    for w in range(2):
        for h in range(2):
            s.add("head", a, ("global_qk", w, h), (a, ("a_channels", h)), (a, ("split_low", w)), banks=HEAD_PS)
        s.add("head", a, ("split", 1 + w), (a, ("global_qk", w, 1)))
        s.add("head", a, ("split_low", 1 + w), (a, ("split", 1 + w)))
        for i in LOCAL_AFTER[w]:
            s.add("head", a, ("local_qkv", i), (a, ("a_channels", 1)), (a, ("local_qkv", i - 2)), banks=HEAD_PS)


def maxima(s, a, quad, *before):
    for t in range(TILES):
        s.add("maxima", a, ("max_tile", quad, t), *before, banks=MAX_PS)
    s.add("maxima", a, ("guard", quad), (a, ("max_tile", quad, TILES - 1)), banks=MAX_PS)
    s.add("maxima", a, ("guard_rows", quad), (a, ("guard", quad)))


def scores(s, quad):
    def product(g):
        s.add("scores", 0, ("pv_group", quad, g), (0, ("score_tile", quad, g * QH + QH - 1)),
              (0, ("o_copy", quad, 0) if quad == 0 else ("o_copy", 0, 1)), (0, ("o_copy", 1, 0)))
        if g % NT == NT - 1:
            s.add("scores", 0, ("o_copy", quad, g // NT), (0, ("pv_group", quad, g)),
                  (-1, ("o_tokens", quad, g // NT)))

    for n in range(TILES):
        s.add("scores", 0, ("score_tile", quad, n), (0, ("guard_rows", quad)), (0, ("pv_group", quad, n // QH - 2)),
              banks=SCORE_PS)
        if n % QH == QH - 1 and n >= QH:
            product(n // QH - 1)
    product(GROUPS - 1)


def local_attention(s):
    for g in range(NT // 2):
        s.add("local", 0, ("local_dot", g), (0, ("local_out", g - 1)))
        s.add("local", 0, ("local_max", g), (0, ("local_dot", g)))
        s.add("local", 0, ("local_sum", g), (0, ("local_max", g)))
        s.add("local", 0, ("local_out", g), (0, ("local_sum", g)), (-1, ("o_channels", 1, 1)))


def tail_a(s, a):
    for q in range(QUADS):
        for h in range(2):
            s.add("tail", a, ("o_tokens", q, h), banks=TAIL_PS)
    s.add("tail", a, ("recall",))
    for w in range(2):
        for h in range(2):
            s.add("tail", a, ("o_channels", w, h), (a, ("o_tokens", 1, 1)), banks=TAIL_PS)
    s.add("tail", a, ("bias",), (a, ("recall",)))


def tail_b(s, a):
    def hidden(name, h, *before):
        for m in range(2):
            s.add("tail", a, (name, m, h), *before, (a, (name, 0, 0) if m else (name, 1, 0)), banks=TAIL_PS)

    def normed(name, after):
        for h in range(2):
            s.add("tail", a, ("stats_" + name, h), (a, (after, h)))
        for h in range(2):
            s.add("tail", a, ("norm_" + name, h), (a, ("stats_" + name, h)))

    for h in range(2):
        hidden("fuse1", h, (a, ("o_channels", 1, 1)))
        s.add("tail", a, ("fuse2", h), (a, ("fuse1", 1, h)), (a, ("bias",)), banks=TAIL_PS)
    normed("u", "fuse2")
    for h in range(2):
        s.add("tail", a, ("x1_channels", h), (a, ("norm_u", h)), banks=TAIL_PS)
        hidden("ffn1", h, (a, ("x1_channels", h)))
        s.add("tail", a, ("ffn2", h), (a, ("ffn1", 1, h)), banks=TAIL_PS)
    normed("v", "ffn2")
    normed("t2", "norm_v")
    s.add("tail", a, ("store_t2",), (a, ("norm_v", 1)))
    for h in range(2):
        s.add("tail", a, ("n2_channels", h), (a, ("norm_t2", h)), banks=TAIL_PS)
    s.add("tail", a, ("logits",), (a, ("n2_channels", 1)), banks=TAIL_PS)
    s.add("tail", a, ("ranks",), (a, ("logits",)), banks=TAIL_PS)
    s.add("tail", a, ("route",), (a, ("ranks",)))


def stacks(s, a, quad):
    s.add("stacks", a, ("global_stacks", quad), (a, ("split_low", 2)), (a - 1, ("score_tile", quad, TILES - 1)))


def values(s, a):
    for h in range(2):
        s.add("tail", a, ("global_v", h), (a, ("a_channels", 1)), (a - 1, ("pv_group", 1, GROUPS - 1)), banks=TAIL_PS)


def first_steps():
    s = Steps()
    s.add("x", 0, ("load_x",))
    s.add("x", 0, ("weights",))
    head_a(s, 0)
    s.add("x", 1, ("load_x",), (0, ("conv_v", 1)))
    head_b(s, 0)
    stacks(s, 0, 0)
    stacks(s, 0, 1)
    values(s, 0)
    head_a(s, 1)
    maxima(s, 0, 0, (0, ("global_stacks", 0)))
    return s.plan()


def iteration_steps(has_tail, has_a, has_b):
    s = Steps()
    if has_a:
        s.add("x", 2, ("load_x",))
    if has_tail:
        tail_a(s, -1)
        tail_b(s, -1)
    local_attention(s)
    maxima(s, 0, 1)
    if has_b:
        head_b(s, 1)
    scores(s, 0)
    scores(s, 1)
    if has_b:
        stacks(s, 1, 0)
        maxima(s, 1, 0, (1, ("global_stacks", 0)))
        stacks(s, 1, 1)
        values(s, 1)
    if has_a:
        head_a(s, 2)
    return s.plan()


def last_steps():
    s = Steps()
    tail_a(s, 0)
    tail_b(s, 0)
    return s.plan()


def hybrid_kernel(nc, x, wq, bq, wk, bk, wv, bv, g_in_w, g_in_b, g_out_w, g_out_b, t_in_w, t_in_b, t_out_w,
                  t_out_b, fus_w1, fus_b1, fus_w2, fus_b2, ffn_w1, ffn_b1, ffn_w2, ffn_b2, gn_g, gn_b, fn_g,
                  fn_b, gate_w, gate_b, w1, b1, w2, b2, out):
    x_b = x.rearrange("b c h w -> b c (h w)")
    out_b = out.rearrange("b c h w -> b c (h w)")

    parts_d = nc.dram_tensor("parts_d", [B, 3, 3, C, N], BF16).ap()
    kv_d = nc.dram_tensor("kv_d", [B, N + 2 * PAD, 2 * C], F32)
    kv_a = kv_d.ap()
    ql_d = nc.dram_tensor("ql_d", [B, N, C], F32).ap()
    kept_d = nc.dram_tensor("kept_d", [B, 2, P, NT, C], F32).ap()
    t2_d = nc.dram_tensor("t2_d", [B * N, C], F32).ap()
    rows_d = nc.dram_tensor("rows_d", [E * CAP, ROW], F32).ap()

    ctx = ExitStack()
    with ctx:
        def sb(name, shape, dt=F32):
            return ctx.enter_context(nc.sbuf_tensor(name, shape, dt))

        def sem(name):
            return ctx.enter_context(nc.semaphore(name))

        bank = [ctx.enter_context(nc.psum_tensor(f"bank{i}", [P, HN], F32)) for i in range(8)]
        head_ps = bank[0]
        max_ps = bank[1:1 + MAX_BANKS]
        score_ps = bank[4:6]
        o_ps = bank[6]
        tail_ps = bank[7]

        ident = sb("ident", [P, P])
        identb = sb("identb", [P, P], BF16)
        ones = sb("ones", [P, P])
        tri = sb("tri", [P, P])
        lmask = sb("lmask", [P, NT, WIN, LH])
        experts = sb("experts", [P, E])
        half_pow = sb("half_pow", [P, HT])
        of_all = sb("of_all", [P, HT])
        eps = sb("eps", [P, HT])
        cqkT = sb("cqkT", [P, 2 * D])
        cvw = sb("cvw", [P, C])
        gT = sb("gT", [P, 3, C])
        lT = sb("lT", [P, 3 * C])
        fgT = sb("fgT", [P, 2 * C])
        flT = sb("flT", [P, 2 * C])
        f2T = sb("f2T", [P, 2, C])
        n1T = sb("n1T", [P, 2 * C])
        n2wT = sb("n2wT", [P, 2, C])
        gate = sb("gate", [P, E])
        cols = sb("cols", [P, 16])
        hcols = sb("hcols", [P, 16])
        b1c = sb("b1c", [P, E * FC])
        bc = sb("bc", [P, 10, C])
        gate_bc = sb("gate_bc", [P, E])
        BC = {n: i for i, n in enumerate(["bv", "gv", "lq", "lk", "lv", "fus_b2", "gn_g", "gn_b", "ffn_b2", "fn_g"])}
        fnb_bc = sb("fnb_bc", [P, C])

        x_cm = sb("x_cm", [P, N])
        split_x = sb("split_x", [P, N])
        parts = sb("parts", [P, 3, N], BF16)
        cq_stack = sb("cq_stack", [P, N], BF16)
        ck_stack = sb("ck_stack", [P, N], BF16)
        cprob = sb("cprob", [P, NT, HN])
        cv_tok = sb("cv_tok", [P, NT, C + 1])
        t_tok = sb("t_tok", [P, NT, C])
        a_tok = sb("a_tok", [P, NT, C])
        a_cm = sb("a_cm", [P, N])
        cmax = sb("cmax", [P, NT, 2])
        cneg = sb("cneg", [P, NT])
        crest = sb("crest", [P, NT])
        cneg_parts = sb("cneg_parts", [P, 3, NT], BF16)
        cneg_rows = sb("cneg_rows", [3 * NT, P], BF16)
        crecip = sb("crecip", [P, NT])
        stats = sb("stats", [P, HT, 6])
        mv = sb("mv", [P, 3, HT])
        rstd = sb("rstd", [P, HT])
        shift = sb("shift", [P, HT])
        lqkv = sb("lqkv", [P, 2, 3 * C])

        q_stack = [sb(f"q_stack{q}", [P, QH, N], BF16) for q in range(QUADS)]
        k_stack = [sb(f"k_stack{q}", [P, QH, N], BF16) for q in range(QUADS)]
        v_tok = sb("v_tok", [P, NT, HEADS, CG])
        prob = sb("prob", [P, 2, QH, HN])
        gmax = sb("gmax", [P, QH, NT, 2])
        gneg = sb("gneg", [P, QH * NT])
        grest = sb("grest", [P, QH * NT])
        gneg_parts = sb("gneg_parts", [P, 3, QH * NT], BF16)
        gneg_rows = sb("gneg_rows", [3 * QH * NT, P], BF16)
        o_raw = sb("o_raw", [P, QUADS, 2, HN])
        og_tok = sb("og_tok", [P, NT, QUADS, QH, D])
        grecip = sb("grecip", [P, HT, QH])
        kv_win = sb("kv_win", [P, 2, WIN, 2 * C])
        ql_tok = sb("ql_tok", [P, 2, C])
        lprod = sb("lprod", [P, 2, WIN, C])
        ls = sb("ls", [P, 2, WIN, LH])
        lmx = sb("lmx", [P, 2, LH])
        lsum = sb("lsum", [P, 2, LH])
        ol_tok = sb("ol_tok", [P, NT, C])

        t_old = sb("t_old", [P, NT, C])
        a_old = sb("a_old", [P, NT, C])
        y_cm = sb("y_cm", [P, 2, N])
        hid = sb("hid", [P, 2, N])
        tanh_t = sb("tanh_t", [P, HN])
        half_t = sb("half_t", [P, HN])
        x1 = sb("x1", [P, NT, C])
        stats2 = sb("stats2", [P, 2, HT, 6])
        mv2 = sb("mv2", [P, 2, 3, HT])
        rstd2 = sb("rstd2", [P, 2, HT])
        shift2 = sb("shift2", [P, 2, HT])
        rows = sb("rows", [P, NT, ROW])
        lg = sb("lg", [P, NT, E])
        lgm = sb("lgm", [P, NT])
        lge = sb("lge", [P, NT, E])
        cand = sb("cand", [P, NT, E])
        idx = sb("idx", [P, NT])
        onehot = sb("onehot", [P, NT, E])
        cum = sb("cum", [P, NT + 1, E])
        rank = sb("rank", [P, NT])
        over = sb("over", [P, NT])
        slot = sb("slot", [P, NT], U32)
        token_no = sb("token_no", [P, NT])

        rows_e = cprob[:, :, :].rearrange("p a b -> p (a b)")[:, 0:CT * ROW].rearrange("p (t r) -> p t r", r=ROW)
        stk = [q_stack[0], q_stack[1], k_stack[0], k_stack[1]]
        hid_e = [s[:, :, :].rearrange("p a b -> p (a b)").bitcast(F32)[:, 0:CAP] for s in stk]
        x_e = prob[:, :, :, :].rearrange("p a b c -> p (a b c)")[:, 0:CAP]
        y_e = v_tok[:, :, :, :].rearrange("p a b c -> p (a b c)")[:, 0:CAP].rearrange("p (t c) -> p t c", c=C)
        w1_e = x_cm[:, 0:FF]
        w2_e = x_cm[:, FF:2 * FF].rearrange("p (f c) -> p f c", c=C)
        b2_e = t_tok
        b1_e = sb("b1_e", [P, FC])
        prob_e = sb("prob_e", [P, CT])
        token_e = sb("token_e", [P, CT], U32)
        odd_e = hid[:, :, :].rearrange("p a b -> p (a b)")[:, 0:3 * HN].rearrange("p (k n) -> p k n", k=3).bitcast(U32)
        huge = sb("huge", [P, 3])
        zero_rows = lprod[0:PAD, 0, 0:2, :].rearrange("p a c -> p (a c)")
        nat = cprob[:, :, :].rearrange("p a b -> p (a b)")
        fin_tok = [m[:, HT * h:HT * h + HT, :] for m in (a_tok, t_old) for h in range(2)]
        fin_cm = [hid[:, k, h * HN:(h + 1) * HN] for k in range(2) for h in range(2)]

        consts_made = sem("consts_made")
        const_step = sem("const_step")
        const_dve = sem("const_dve")
        first_in = sem("first_in")
        weights_in = sem("weights_in")
        weights_filled = sem("weights_filled")
        weights_used = sem("weights_used")
        scratch_zeroed = sem("scratch_zeroed")
        x_in = sem("x_in")
        kept = sem("kept")
        recalled = sem("recalled")
        head_full = sem("head_full")
        head_free = sem("head_free")
        split_step = sem("split_step")
        split_out = sem("split_out")
        cstacks_in = sem("cstacks_in")
        cguard_step = sem("cguard_step")
        cguard_in = sem("cguard_in")
        cpv_made = sem("cpv_made")
        crecip_made = sem("crecip_made")
        stats_made = sem("stats_made")
        norm_step = sem("norm_step")
        norm_rstd = sem("norm_rstd")
        a_made = sem("a_made")
        lqkv_out = [sem(f"lqkv_out{k}") for k in range(2)]
        gstacks_in = [sem(f"gstacks_in{q}") for q in range(QUADS)]
        max_full = sem("max_full")
        max_free = sem("max_free")
        guard_step = sem("guard_step")
        guard_in = [sem(f"guard_in{q}") for q in range(QUADS)]
        score_full = sem("score_full")
        exp_made = sem("exp_made")
        pv_made = sem("pv_made")
        o_copied = sem("o_copied")
        grecip_made = sem("grecip_made")
        kv_in = sem("kv_in")
        lprod_made = sem("lprod_made")
        local_step = sem("local_step")
        lexp_made = sem("lexp_made")
        lpv_made = sem("lpv_made")
        ol_made = sem("ol_made")
        tail_full = sem("tail_full")
        tail_free = sem("tail_free")
        hid_made = sem("hid_made")
        bias_added = sem("bias_added")
        stats2_made = sem("stats2_made")
        norm2_step = sem("norm2_step")
        norm2_rstd = sem("norm2_rstd")
        normed = sem("normed")
        affine_step = sem("affine_step")
        x1_made = sem("x1_made")
        x1_bias = sem("x1_bias")
        t2_made = sem("t2_made")
        t2_out = sem("t2_out")
        route_step = sem("route_step")
        lexpert = sem("lexpert")
        routed = sem("routed")
        rows_out = sem("rows_out")
        erows_in = sem("erows_in")
        ew1_in = sem("ew1_in")
        ew2_in = sem("ew2_in")
        eb2_in = sem("eb2_in")
        ext_full = sem("ext_full")
        ext_free = sem("ext_free")
        eh_full = sem("eh_full")
        eh_free = sem("eh_free")
        ey_full = sem("ey_full")
        ey_free = sem("ey_free")
        etaken = sem("etaken")
        ey_step = sem("ey_step")
        eb1_made = sem("eb1_made")
        ey_odd = [sem(f"ey_odd{c}") for c in range(3)]
        ey_pass = [[sem(f"ey_pass{c}{k}") for k in range(2)] for c in range(3)]
        ey_made = [sem(f"ey_made{c}") for c in range(3)]
        ey_out = sem("ey_out")
        fin_in = [sem(f"fin_in{k}") for k in range(ENDS)]
        fin_full = [sem(f"fin_full{k}") for k in range(ENDS)]
        fin_made = [sem(f"fin_made{k}") for k in range(ENDS)]
        fin_out = [sem(f"fin_out{k}") for k in range(ENDS)]

        def after(eng, s, count):
            if not isinstance(count, int) or count > 0:
                eng.wait_ge(s, count)

        def head_fill(pe, b, use):
            after(pe, head_free, b * HEAD_TURNS + HEAD_TURN[use])
            return head_ps, head_full

        def head_filled(eng, b, use):
            after(eng, head_full, b * HEAD_TURNS + HEAD_TURN[use] + 1)

        def head_read(eng, b, use):
            head_filled(eng, b, use)
            return head_ps, head_free

        def head_done(eng, b, use):
            after(eng, head_free, b * HEAD_TURNS + HEAD_TURN[use] + 1)

        def tail_done(eng, b, use):
            after(eng, tail_free, tail_count(b, use) + 1)

        def tail_count(b, use):
            if use[0] == "global_v":
                return (0 if isinstance(b, int) and b == 0 else (b - 1) * (TAIL_TURNS + 2) + 2) + use[1]
            last = isinstance(b, int) and b == B - 1
            return b * (TAIL_TURNS + 2) + (2 if last else 4) + TAIL_TURN[use]

        def max_bank(n):
            return n % MAX_BANKS

        def walk(name_, eng, steps):
            def take(orders, i):
                for ahead, (name, *args) in orders.get(name_, []):
                    steps[name](i + ahead if ahead else i, *args)
            take(first_steps(), 0)
            take(iteration_steps(False, True, True), 0)
            with eng.Fori(1, B - 2) as i:
                take(iteration_steps(True, True, True), i)
            take(iteration_steps(True, False, True), B - 2)
            take(iteration_steps(True, False, False), B - 1)
            take(last_steps(), B - 1)

        BIAS_ROWS = ["conv", "gq", "gk", "go", "to", "fus0", "fus1", "ffn0", "ffn1"]
        COL = {n: i for i, n in enumerate(BIAS_ROWS)}
        NAT = [("cqk", None, 2 * D), ("cv", wv, P), ("bias", None, len(BIAS_ROWS))]
        FIRST = len(NAT)
        NAT += [(f"g{i}", g_in_w[i * C:(i + 1) * C, :], P) for i in range(3)]
        NAT += [(f"l{i}", t_in_w[i * C:(i + 1) * C, :], P) for i in range(3)]
        NAT += [(f"f1{m}{k}", fus_w1[m * C:(m + 1) * C, k * C:(k + 1) * C], P) for m in range(2) for k in range(2)]
        NAT += [(f"f2{k}", fus_w2[:, k * C:(k + 1) * C], P) for k in range(2)]
        NAT += [(f"n1{m}", ffn_w1[m * C:(m + 1) * C, :], P) for m in range(2)]
        NAT += [(f"n2{k}", ffn_w2[:, k * C:(k + 1) * C], P) for k in range(2)]
        NAT += [("b1", b1.rearrange("e (f p) -> (e f) p", p=P), E * FC)]
        WO = {"g": len(NAT), "t": len(NAT) + 1}
        f1T = [hid[:, k, 0:2 * C] for k in range(2)]
        TARGET = {"cqk": cqkT[:, :], "cv": cvw[:, :]}
        for i in range(3):
            TARGET[f"g{i}"] = gT[:, i, :]
            TARGET[f"l{i}"] = lT[:, i * C:(i + 1) * C]
        for m in range(2):
            for k in range(2):
                TARGET[f"f1{m}{k}"] = f1T[k][:, m * C:(m + 1) * C]
            TARGET[f"f2{m}"] = f2T[:, m, :]
            TARGET[f"n1{m}"] = n1T[:, m * C:(m + 1) * C]
            TARGET[f"n2{m}"] = n2wT[:, m, :]
        TARGET["bias"] = cols[:, 0:len(BIAS_ROWS)]
        TARGET["b1"] = b1c[:, :]
        FIRST_LOADS = 2 + 1 + 11 + 1
        WEIGHT_LOADS = FIRST_LOADS + len(NAT) - FIRST + 3 + len(BC) - 1 + 2

        block = ctx.enter_context(nc.Block())

        @block.sync
        def _(sp):
            def n_at(i, rows_=P, first=0):
                return nat[first:first + rows_, i * C:(i + 1) * C]

            loads = []
            for i, (name, src, r) in enumerate(NAT):
                if i == FIRST:
                    loads.append((bc[:, BC["bv"], :], bv.partition_broadcast(P)))
                    first_loads = len(loads)
                if name == "cqk":
                    loads += [(n_at(i, D), wq), (n_at(i, D, D), wk)]
                elif name == "bias":
                    row = lambda k: nat[COL[k]:COL[k] + 1, i * C:(i + 1) * C]
                    one = lambda v, lo, hi: v[lo:hi].rearrange("(a n) -> a n", a=1)
                    loads += [(row("conv")[:, 0:D], one(bq, 0, D)), (row("conv")[:, D:2 * D], one(bk, 0, D))]
                    loads += [(row("conv")[:, 2 * D:C], one(g_in_b, 0, C - 2 * D))]
                    loads += [(row("gq"), one(g_in_b, 0, C)), (row("gk"), one(g_in_b, C, 2 * C))]
                    loads += [(row("go"), one(g_out_b, 0, C)), (row("to"), one(t_out_b, 0, C))]
                    loads += [(row(f"fus{m}"), one(fus_b1, m * C, (m + 1) * C)) for m in range(2)]
                    loads += [(row(f"ffn{m}"), one(ffn_b1, m * C, (m + 1) * C)) for m in range(2)]
                else:
                    loads.append((n_at(i, r), src))
            loads += [(n_at(WO["g"]), g_out_w), (n_at(WO["t"]), t_out_w), (gate[:, :], gate_w)]
            wide = {"gv": g_in_b[2 * C:3 * C], "lq": t_in_b[0:C], "lk": t_in_b[C:2 * C],
                    "lv": t_in_b[2 * C:3 * C], "fus_b2": fus_b2, "gn_g": gn_g, "gn_b": gn_b, "ffn_b2": ffn_b2,
                    "fn_g": fn_g}
            loads += [(bc[:, BC[k], :], v.partition_broadcast(P)) for k, v in wide.items()]
            loads += [(fnb_bc[:, :], fn_b.partition_broadcast(P)), (gate_bc[:, :], gate_b.partition_broadcast(P))]
            assert len(loads) == WEIGHT_LOADS, len(loads)
            assert first_loads == FIRST_LOADS, first_loads
            for dst, src in loads[:FIRST_LOADS]:
                sp.dma_start(dst, src).then_inc(first_in, 16)

            def weights(b):
                for dst, src in loads[FIRST_LOADS:]:
                    sp.dma_start(dst, src).then_inc(weights_in, 16)
                sp.wait_ge(consts_made, 2)
                for n in range(B):
                    sp.dma_start(kv_a[n, 0:PAD, :], zero_rows).then_inc(scratch_zeroed, 16)
                    sp.dma_start(kv_a[n, N + PAD:N + 2 * PAD, :], zero_rows).then_inc(scratch_zeroed, 16)
                for e in range(E * CT // NT):
                    sp.dma_start(rows_d[e * NT * P:(e + 1) * NT * P, :].rearrange("(t p) r -> p t r", p=P),
                                 rows[:, :, :]).then_inc(scratch_zeroed, 16)

            def load_x(b):
                if not (isinstance(b, int) and b == 0):
                    head_filled(sp, b - 1, ("conv_v", 1))
                sp.dma_start(x_cm[:, :], x_b[b]).then_inc(x_in, 16)

            def keep(b):
                after(sp, a_made, (b + 1) * 2)
                sp.dma_start(kept_d[b, 0], t_tok[:, :, :]).then_inc(kept, 16)
                sp.dma_start(kept_d[b, 1], a_tok[:, :, :]).then_inc(kept, 16)

            def recall(b):
                after(sp, kept, (b + 1) * 32)
                sp.dma_start(t_old[:, :, :], kept_d[b, 0]).then_inc(recalled, 16)
                sp.dma_start(a_old[:, :, :], kept_d[b, 1]).then_inc(recalled, 16)

            def split_low(b, w):
                rows_ = 2 * D if w == 0 else C
                after(sp, split_step, b * 9 + 3 * w + 3)
                sp.dma_start(parts_d[b, w].rearrange("s c n -> c s n")[0:rows_], parts[0:rows_, :, :])\
                  .then_inc(split_out, 16)

            def conv_stacks(b):
                if not (isinstance(b, int) and b == 0):
                    head_filled(sp, b - 1, ("conv_exp", 1, NT - 1))
                after(sp, split_out, b * 48 + 16)
                for r in range(TERMS):
                    sp.dma_start(cq_stack[D * r:D * r + D, :], parts_d[b, 0, Q_PART[r], 0:D, :])\
                      .then_inc(cstacks_in, 16)
                    sp.dma_start(ck_stack[D * r:D * r + D, :], parts_d[b, 0, K_PART[r], D:2 * D, :])\
                      .then_inc(cstacks_in, 16)

            def conv_guard(b):
                head_done(sp, b, ("conv_guard",))
                for s in range(3):
                    dst = cq_stack[KROWS + s:KROWS + s + 1, :].rearrange("a (t p) -> a t p", p=P)
                    sp.dma_start(dst, cneg_rows[s * NT:s * NT + NT, :]).then_inc(cguard_in, 16)

            def local_qkv(b, i):
                head_done(sp, b, ("local_qkv", i))
                sp.dma_start(ql_d[b, i * P:(i + 1) * P, :], lqkv[:, i % 2, 0:C]).then_inc(lqkv_out[i % 2], 16)
                sp.dma_start(kv_a[b, PAD + i * P:PAD + (i + 1) * P, :], lqkv[:, i % 2, C:3 * C])\
                  .then_inc(lqkv_out[i % 2], 16)

            def global_stacks(b, quad):
                stored = b * 48 + 48 if isinstance(b, int) else sp.to_reg(b * 48 + 48)
                if not (isinstance(b, int) and b == 0):
                    after(sp, score_full, (b - 1) * 2 * TILES + (quad + 1) * TILES)
                after(sp, split_out, stored)
                for r in range(TERMS):
                    for w, st, part in ((1, q_stack[quad], Q_PART[r]), (2, k_stack[quad], K_PART[r])):
                        src = parts_d[b, w, part].rearrange("(h d) n -> d h n", d=D)
                        sp.dma_start(st[D * r:D * r + D, :, :], src[:, quad * QH:(quad + 1) * QH, :])\
                          .then_inc(gstacks_in[quad], 16)

            def guard_rows(b, quad):
                after(sp, max_free, b * 2 * (TILES + 1) + (quad + 1) * (TILES + 1))
                for s in range(3):
                    dst = q_stack[quad][KROWS + s:KROWS + s + 1, :, :].rearrange("a h (t p) -> a (h t) p", p=P)
                    sp.dma_start(dst, gneg_rows[s * QH * NT:(s + 1) * QH * NT, :]).then_inc(guard_in[quad], 16)

            def local_dot(b, g):
                if not (isinstance(b, int) and b == 0 and g == 0):
                    after(sp, lpv_made, b * 4 + g)
                for out_ in lqkv_out:
                    after(sp, out_, (b + 1) * HT * 32)
                after(sp, scratch_zeroed, SCRATCH_LOADS * 16)
                win = bass.AP(kv_d, (b * (N + 2 * PAD) + 2 * g * P) * 2 * C,
                              [[2 * C, P], [P * 2 * C, 2], [1, WIN * 2 * C]])
                sp.dma_start(kv_win[:, :, :, :].rearrange("p i w c -> p i (w c)"), win).then_inc(kv_in, 16)
                sp.dma_start(ql_tok[:, :, :],
                             ql_d[b, 2 * g * P:(2 * g + 2) * P, :].rearrange("(i p) c -> p i c", p=P))\
                  .then_inc(kv_in, 16)

            def store_t2(b):
                after(sp, t2_made, (b + 1) * 2)
                sp.dma_start(t2_d.rearrange("(b t p) c -> b p t c", t=NT, p=P)[b], x1[:, :, :]).then_inc(t2_out, 16)

            walk("sp", sp, dict(load_x=load_x, weights=weights, keep=keep, recall=recall, split_low=split_low, conv_stacks=conv_stacks,
                          conv_guard=conv_guard, local_qkv=local_qkv, global_stacks=global_stacks,
                          guard_rows=guard_rows,
                          local_dot=local_dot, store_t2=store_t2))

            sp.wait_ge(rows_out, B * NT * 16)
            rows_v = rows_d.rearrange("(e t p) r -> e p t r", t=CT, p=P)
            with sp.Fori(0, E) as e:
                sp.wait_ge(ext_full, e * 3)
                sp.wait_ge(etaken, e)
                sp.dma_start(rows_e, rows_v[e]).then_inc(erows_in, 16)
                sp.wait_ge(eh_full, e * FC * 3)
                sp.dma_start(w1_e, w1[e]).then_inc(ew1_in, 16)
                sp.wait_ge(ey_full, e * 3)
                sp.dma_start(w2_e, w2.rearrange("e (f p) c -> e p f c", p=P)[e]).then_inc(ew2_in, 16)
                sp.wait_ge(ey_free, e * 3)
                sp.dma_start(b2_e[:, 0, :], b2[e].partition_broadcast(P)).then_inc(eb2_in, 16)

            sp.wait_ge(ey_out, E * CT * 16)
            t2_v = t2_d.rearrange("(b k t p) c -> b k p t c", k=ENDS, t=HT, p=P)
            with sp.Fori(0, 2 * B // ENDS) as r:
                for k in range(ENDS):
                    sp.wait_ge(fin_full[k], r)
                    sp.dma_start(fin_tok[k], t2_v[r, k]).then_inc(fin_in[k], 16)

        @block.gpsimd
        def _(pool):
            last_slot = pool.to_reg(E * CAP - 1)
            last_token = pool.to_reg(B * N - 1)
            made = [0]

            def made_here(ins):
                made[0] += 1
                ins.then_inc(const_step, 1)
                pool.wait_ge(const_step, made[0])

            made_here(pool.memset(rows[:, :, :], 0.0))
            made_here(pool.memset(lprod[:, :, :, :], 0.0))
            pool.memset(rows[:, :, C + 1:C + 2], NOWHERE).then_inc(consts_made, 1)
            pool.memset(half_pow[:, :], -0.5).then_inc(consts_made, 1)
            made_here(pool.memset(of_all[:, :], 1.0 / C))
            made_here(pool.memset(eps[:, :], EPS))
            for m in (ident, identb, tri):
                made_here(pool.memset(m[:, :], 1.0 if m is tri else 0.0))
            made_here(pool.memset(ones[:, :], 1.0))
            for m in (ident, identb):
                made_here(pool.affine_select(out=m[:, :], in_=m[:, :], compare_op=ALU.not_equal, fill=1.0,
                                             base=0, pattern=[[-1, P]], channel_multiplier=1))
            made_here(pool.affine_select(out=tri[:, :], in_=tri[:, :], compare_op=ALU.is_ge, fill=0.0,
                                         base=0, pattern=[[1, P]], channel_multiplier=-1))
            made_here(pool.memset(lmask[:, :, :, :], 0.0))
            made_here(pool.affine_select(out=lmask[:, 0, :, :], in_=lmask[:, 0, :, :], compare_op=ALU.is_ge,
                                         fill=MASKED, base=-PAD, pattern=[[1, WIN], [0, LH]], channel_multiplier=1))
            made_here(pool.affine_select(out=lmask[:, NT - 1, :, :], in_=lmask[:, NT - 1, :, :],
                                         compare_op=ALU.is_ge, fill=MASKED, base=P - 1 + PAD,
                                         pattern=[[-1, WIN], [0, LH]], channel_multiplier=-1))
            made_here(pool.iota(experts[:, :], pattern=[[1, E]], base=0, channel_multiplier=0,
                                allow_small_or_imprecise_dtypes=True))
            made_here(pool.iota(token_no[:, :], pattern=[[P, NT]], base=0, channel_multiplier=1,
                                allow_small_or_imprecise_dtypes=True))
            made_here(pool.memset(cum[:, :, :], 0.0))
            made_here(pool.memset(cv_tok[:, :, C:C + 1], 1.0))
            made_here(pool.memset(v_tok[:, :, :, :], 0.0))
            made_here(pool.memset(v_tok[:, :, :, D:D + 1], 1.0))
            made_here(pool.memset(huge[:, 0:1], 0.0))
            made_here(pool.memset(huge[:, 1:2], 10000.0))
            made_here(pool.memset(huge[:, 2:3], -10000.0))
            for s in (ck_stack[KROWS:KM, :], k_stack[0][KROWS:KM, :, :], k_stack[1][KROWS:KM, :, :]):
                made_here(pool.memset(s, 1.0))
            pool.memset(stats[:, 0, 0:1], 0.0).then_inc(consts_made, 1)

            def wide(i, n=HT):
                return (bc[:, i, :] if isinstance(i, int) else i)[:, None, :].to_broadcast([P, n, C])

            def factors(st, m, scale, shift, stats_sem, free_sem, step_sem, made_sem, n, used):
                k = [n * NORM_STEPS]

                def step(ins):
                    k[0] += 1
                    ins.then_inc(step_sem, 1)
                    pool.wait_ge(step_sem, k[0])

                tt = pool.tensor_tensor
                after(pool, stats_sem, n + 1)
                after(pool, free_sem, used)
                tt(m[:, 0, :], st[:, :, 1], st[:, :, 4], ALU.add)
                tt(m[:, 2, :], st[:, :, 1], st[:, :, 4], ALU.subtract)
                step(tt(m[:, 1, :], st[:, :, 2], st[:, :, 5], ALU.add))
                tt(m[:, 0, :], m[:, 0, :], half_pow[:, :], ALU.mult)
                tt(m[:, 2, :], m[:, 2, :], half_pow[:, :], ALU.mult)
                step(tt(m[:, 1, :], m[:, 1, :], of_all[:, :], ALU.mult))
                tt(m[:, 2, :], m[:, 2, :], m[:, 2, :], ALU.mult)
                step(tt(m[:, 1, :], m[:, 1, :], eps[:, :], ALU.add))
                step(tt(m[:, 1, :], m[:, 1, :], m[:, 2, :], ALU.add))
                step(tt(scale, m[:, 1, :], half_pow[:, :], ALU.pow))
                tt(shift, m[:, 0, :], scale, ALU.mult).then_inc(made_sem, 1)

            def stats_t(b, h):
                factors(stats, mv, rstd[:, :], shift[:, :], stats_made, a_made, norm_step, norm_rstd, b * 2 + h,
                        b * 2 + h)

            def tail_rms(b, k):
                h = k % 2
                factors(stats2[:, h], mv2[:, h], rstd2[:, h, :], shift2[:, h, :], stats2_made, normed, norm2_step,
                        norm2_rstd, b * 6 + k, b * 6 + max(k - 1, 0))

            def stats_u(b, h):
                tail_rms(b, h)

            def stats_v(b, h):
                tail_rms(b, 2 + h)

            def stats_t2(b, h):
                tail_rms(b, 4 + h)

            def local_dot(b, g):
                after(pool, kv_in, b * 128 + 32 * (g + 1))
                if not (isinstance(b, int) and b == 0 and g == 0):
                    after(pool, ol_made, b * 4 + g)
                for i in range(2):
                    m = pool.tensor_tensor(lprod[:, i, :, :], ql_tok[:, i, None, :].to_broadcast([P, WIN, C]),
                                           kv_win[:, i, :, 0:C], ALU.mult)
                m.then_inc(lprod_made, 1)

            def local_sum(b, g):
                after(pool, local_step, b * 28 + 7 * g + 7)
                for i in range(2):
                    m = pool.tensor_tensor(
                        lprod[:, i, :, :].rearrange("p w (h d) -> p w h d", d=LD),
                        ls[:, i, :, :, None].to_broadcast([P, WIN, LH, LD]),
                        kv_win[:, i, :, C:2 * C].rearrange("p w (h d) -> p w h d", d=LD), ALU.mult)
                m.then_inc(lpv_made, 1)

            def bias(b):
                after(pool, recalled, (b + 1) * 32)
                pool.tensor_tensor(a_old[:, :, :], a_old[:, :, :], wide(BC["fus_b2"], NT), ALU.add)\
                    .then_inc(bias_added, 1)

            def norm_u(b, h):
                t = slice(HT * h, HT * h + HT)
                after(pool, normed, b * 6 + h + 1)
                pool.tensor_tensor(x1[:, t, :], x1[:, t, :], wide(BC["gn_g"]), ALU.mult).then_inc(affine_step, 1)
                after(pool, affine_step, b * 6 + h * 1 + 1)
                pool.tensor_tensor(x1[:, t, :], x1[:, t, :], wide(BC["gn_b"]), ALU.add).then_inc(x1_made, 1)
                after(pool, x1_made, b * 2 + h + 1)
                tail_done(pool, b, ("fuse2", h))
                pool.tensor_tensor(a_old[:, t, :], x1[:, t, :], wide(BC["ffn_b2"]), ALU.add).then_inc(x1_bias, 1)

            def norm_v(b, h):
                t = slice(HT * h, HT * h + HT)
                after(pool, normed, b * 6 + 2 + h + 1)
                pool.tensor_tensor(x1[:, t, :], x1[:, t, :], wide(BC["fn_g"]), ALU.mult).then_inc(affine_step, 1)
                after(pool, affine_step, b * 6 + 2 + 2 * h + 1)
                pool.tensor_tensor(x1[:, t, :], x1[:, t, :], wide(fnb_bc[:, :]), ALU.add).then_inc(affine_step, 1)
                after(pool, affine_step, b * 6 + 2 + 2 * h + 2)
                pool.tensor_tensor(x1[:, t, :], x1[:, t, :], t_old[:, t, :], ALU.add).then_inc(t2_made, 1)

            def route(b):
                pool.wait_ge(scratch_zeroed, SCRATCH_LOADS * 16)
                after(pool, routed, b + 1)
                for i in range(NT):
                    pool.indirect_dma_start(rows_d, bass.IndirectOffsetOnAxis(ap=slot[:, i:i + 1], axis=0),
                                            rows[:, i, :], None, bounds_check=last_slot, oob_is_err=False)\
                        .then_inc(rows_out, 16)

            walk("pool", pool, dict(stats_t=stats_t, local_dot=local_dot, local_sum=local_sum, bias=bias, stats_u=stats_u,
                            norm_u=norm_u, stats_v=stats_v, norm_v=norm_v, stats_t2=stats_t2, route=route))

            with pool.Fori(1, E + 1) as nth:
                for i in range(CT):
                    c = i * P // HN
                    if i * P % HN == 0:
                        pool.wait_ge(t2_out, B * 16)
                        pool.wait_ge(ey_made[c], nth)
                    pool.indirect_dma_start(t2_d, bass.IndirectOffsetOnAxis(ap=token_e[:, i:i + 1], axis=0),
                                            y_e[:, i, :], None, bounds_check=last_token, oob_is_err=False,
                                            compute_op=ALU.add).then_inc(ey_out, 16)

        @block.tensor
        def _(pe):
            mm = nc.tensor.matmul

            def turn(dst, src, n=P, identity=None):
                return nc.tensor.transpose(dst, src, ident[0:n, 0:n] if identity is None else identity)

            def transpose_weight(i):
                if i >= 2:
                    pe.wait_ge(weights_used, i - 1)
                _, _, r = NAT[i]
                turn(score_ps[i % 2][:, 0:r], nat[0:r, i * C:(i + 1) * C], r).then_inc(weights_filled, 1)

            pe.wait_ge(consts_made, 3)
            pe.wait_ge(first_in, FIRST_LOADS * 16)
            for i in range(FIRST):
                transpose_weight(i)
            pe.wait_ge(weights_used, FIRST)

            def weights(b):
                pe.wait_ge(weights_in, (WEIGHT_LOADS - FIRST_LOADS) * 16)
                for i in range(FIRST, len(NAT)):
                    transpose_weight(i)
                n = len(NAT)
                pe.wait_ge(weights_used, n)
                for k, w in enumerate("gt"):
                    mm(bank[6 + k][:, 0:2 * C], nat[:, WO[w] * C:(WO[w] + 1) * C], f1T[k], start=True, stop=True)\
                        .then_inc(weights_filled, 1)
                for m in range(2):
                    for k, name in enumerate(("go", "to")):
                        last = mm(bank[2][:, m:m + 1], f1T[k][:, m * C:(m + 1) * C],
                                  cols[:, COL[name]:COL[name] + 1], start=(k == 0), stop=(k == 1))
                last.then_inc(weights_filled, 1)
                pe.wait_ge(weights_used, n + 5)

            def x_tokens(b, h):
                ps, full = head_fill(pe, b, ("x_tokens", h))
                after(pe, x_in, (b + 1) * 16)
                for i in range(HT):
                    last = turn(ps[:, i * C:(i + 1) * C], x_cm[:, (HT * h + i) * P:(HT * h + i + 1) * P])
                last.then_inc(full, 1)

            def conv_qk(b, h):
                ps, full = head_fill(pe, b, ("conv_qk", h))
                mm(ps[0:2 * D, :], cqkT[:, :], x_cm[:, h * HN:(h + 1) * HN], start=True, stop=True).then_inc(full, 1)

            def conv_v(b, h):
                ps, full = head_fill(pe, b, ("conv_v", h))
                for i in range(HT):
                    last = mm(ps[:, i * C:(i + 1) * C], x_cm[:, (HT * h + i) * P:(HT * h + i + 1) * P], cvw[:, :],
                              start=True, stop=True)
                last.then_inc(full, 1)

            def conv_max(b, t):
                ps, full = head_fill(pe, b, ("conv_max", t))
                if t == 0:
                    after(pe, cstacks_in, (b + 1) * 12 * 16)
                i, j = t // 2, t % 2
                mm(ps[:, :], cq_stack[0:KROWS, i * P:(i + 1) * P], ck_stack[0:KROWS, j * HN:(j + 1) * HN],
                   start=True, stop=True).then_inc(full, 1)

            def conv_guard(b):
                ps, full = head_fill(pe, b, ("conv_guard",))
                after(pe, cguard_step, b * 6 + 6)
                turn(ps[:, :].bitcast(BF16)[0:3 * NT, 0:P], cneg_parts[:, :, :].rearrange("p s t -> p (s t)"),
                     identity=identb[:, :]).then_inc(full, 1)

            def conv_exp(b, h, j):
                ps, full = head_fill(pe, b, ("conv_exp", h, j))
                if h == 0 and j == 0:
                    after(pe, cguard_in, (b + 1) * 48)
                mm(ps[:, :], ck_stack[0:KM, j * P:(j + 1) * P], cq_stack[0:KM, h * HN:(h + 1) * HN],
                   start=True, stop=True).then_inc(full, 1)

            def conv_pv(b, i):
                ps, full = head_fill(pe, b, ("conv_pv", i))
                for j in range(NT):
                    last = mm(ps[:, 0:C + 1], cprob[:, j, (i % HT) * P:(i % HT + 1) * P], cv_tok[:, j, :],
                              start=(j == 0), stop=(j == NT - 1))
                last.then_inc(full, 1)

            def a_channels(b, h):
                ps, full = head_fill(pe, b, ("a_channels", h))
                after(pe, a_made, b * 2 + h + 1)
                for i in range(HT):
                    last = turn(ps[:, i * P:(i + 1) * P], a_tok[:, HT * h + i, :])
                last.then_inc(full, 1)

            def global_qk(b, w, h):
                ps, full = head_fill(pe, b, ("global_qk", w, h))
                mm(ps[:, :], gT[:, w, :], a_cm[:, h * HN:(h + 1) * HN], start=True, stop=True).then_inc(full, 1)

            def local_qkv(b, i):
                ps, full = head_fill(pe, b, ("local_qkv", i))
                mm(ps[:, 0:3 * C], a_cm[:, i * P:(i + 1) * P], lT[:, :], start=True, stop=True).then_inc(full, 1)

            def global_v(b, h):
                tail_fill_at(b, ("global_v", h))
                for i in range(HT):
                    last = mm(tail_ps[:, i * C:(i + 1) * C], a_cm[:, (HT * h + i) * P:(HT * h + i + 1) * P],
                              gT[:, 2, :], start=True, stop=True)
                last.then_inc(tail_full, 1)

            def max_fill(b, quad, n):
                used = b * 2 * (TILES + 1) + quad * (TILES + 1)
                if n >= MAX_BANKS:
                    after(pe, max_free, used + n - MAX_BANKS + 1)
                elif not (isinstance(b, int) and b == 0 and quad == 0):
                    last = [k for k in range(TILES + 1) if max_bank(k) == max_bank(n)][-1]
                    after(pe, max_free, used - TILES + last)

            def max_tile(b, quad, n):
                max_fill(b, quad, n)
                if n == 0:
                    after(pe, gstacks_in[quad], (b + 1) * 12 * 16)
                h, i, j = n // (2 * NT), n // 2 % NT, n % 2
                mm(max_ps[max_bank(n)][:, :], q_stack[quad][0:KROWS, h, i * P:(i + 1) * P],
                   k_stack[quad][0:KROWS, h, j * HN:(j + 1) * HN], start=True, stop=True).then_inc(max_full, 1)

            def guard(b, quad):
                max_fill(b, quad, TILES)
                after(pe, guard_step, b * 12 + quad * 6 + 6)
                turn(max_ps[max_bank(TILES)][:, :].bitcast(BF16)[0:3 * QH * NT, 0:P],
                     gneg_parts[:, :, :].rearrange("p s t -> p (s t)"), identity=identb[:, :]).then_inc(max_full, 1)

            def score_tile(b, quad, n):
                u = b * 2 * TILES + quad * TILES + n
                if not (isinstance(b, int) and b == 0 and quad == 0 and n < 2):
                    after(pe, exp_made, u - 1)
                if n == 0:
                    after(pe, guard_in[quad], (b + 1) * 48)
                g, h = n // QH, n % QH
                half, j = g // NT, g % NT
                mm(score_ps[n % 2][:, :], k_stack[quad][0:KM, h, j * P:(j + 1) * P],
                   q_stack[quad][0:KM, h, half * HN:(half + 1) * HN], start=True, stop=True).then_inc(score_full, 1)

            def pv_group(b, quad, g):
                half, j = g // NT, g % NT
                after(pe, exp_made, b * 2 * TILES + quad * TILES + g * QH + QH)
                if j == 0:
                    after(pe, o_copied, b * 4 + quad * 2 + half)
                if quad == 0 and g == 0:
                    tail_done(pe, b, ("global_v", 1))
                for h in range(QH):
                    last = mm(o_ps[CG * h:CG * (h + 1), :], v_tok[:, j, quad * QH + h, :], prob[:, g % 2, h, :],
                              start=(j == 0), stop=(j == NT - 1))
                last.then_inc(pv_made, 1)

            def o_tokens(b, quad, h):
                tail_fill_at(b, ("o_tokens", quad, h))
                after(pe, o_copied, b * 4 + quad * 2 + h + 1)
                for i in range(HT):
                    last = turn(tail_ps[:, i * P:(i + 1) * P], o_raw[:, quad, h, i * P:(i + 1) * P])
                last.then_inc(tail_full, 1)

            def tail_fill_at(b, use):
                after(pe, tail_free, tail_count(b, use))

            def o_channels(b, w, h):
                tail_fill_at(b, ("o_channels", w, h))
                if w == 1 and h == 0:
                    after(pe, ol_made, (b + 1) * 4)
                for i in range(HT):
                    t = HT * h + i
                    src = og_tok[:, t, :, :, :].rearrange("p q h d -> p (q h d)") if w == 0 else ol_tok[:, t, :]
                    last = turn(tail_ps[:, i * P:(i + 1) * P], src)
                last.then_inc(tail_full, 1)

            def fuse1(b, m, h):
                tail_fill_at(b, ("fuse1", m, h))
                for k, w in enumerate((fgT, flT)):
                    last = mm(tail_ps[:, :], w[:, m * C:(m + 1) * C], y_cm[:, k, h * HN:(h + 1) * HN],
                              start=(k == 0), stop=(k == 1))
                last.then_inc(tail_full, 1)

            def second(b, use, h, w, count):
                tail_fill_at(b, use)
                after(pe, hid_made, count)
                for i in range(HT):
                    t = HT * h + i
                    for k in range(2):
                        last = mm(tail_ps[:, i * C:(i + 1) * C], hid[:, k, t * P:(t + 1) * P], w[:, k, :],
                                  start=(k == 0), stop=(k == 1))
                last.then_inc(tail_full, 1)

            def fuse2(b, h):
                second(b, ("fuse2", h), h, f2T, b * 8 + 2 * h + 2)

            def ffn2(b, h):
                second(b, ("ffn2", h), h, n2wT, b * 8 + 4 + 2 * h + 2)

            def x1_channels(b, h):
                tail_fill_at(b, ("x1_channels", h))
                after(pe, x1_made, b * 2 + h + 1)
                for i in range(HT):
                    last = turn(tail_ps[:, i * P:(i + 1) * P], x1[:, HT * h + i, :])
                last.then_inc(tail_full, 1)

            def ffn1(b, m, h):
                tail_fill_at(b, ("ffn1", m, h))
                mm(tail_ps[:, :], n1T[:, m * C:(m + 1) * C], y_cm[:, 0, h * HN:(h + 1) * HN],
                   start=True, stop=True).then_inc(tail_full, 1)

            def n2_channels(b, h):
                tail_fill_at(b, ("n2_channels", h))
                after(pe, normed, b * 6 + 4 + h + 1)
                for i in range(HT):
                    last = turn(tail_ps[:, i * P:(i + 1) * P], rows[:, HT * h + i, 0:C])
                last.then_inc(tail_full, 1)

            def logits(b):
                tail_fill_at(b, ("logits",))
                for i in range(NT):
                    last = mm(tail_ps[:, i * E:(i + 1) * E], y_cm[:, 1, i * P:(i + 1) * P], gate[:, :],
                              start=True, stop=True)
                last.then_inc(tail_full, 1)

            def ranks(b):
                tail_fill_at(b, ("ranks",))
                after(pe, route_step, b * ROUTE_STEPS + ONEHOT_STEP)
                oh = onehot[:, :, :].rearrange("p t e -> p (t e)")
                mm(tail_ps[:, 0:NT * E], tri[:, :], oh, start=True, stop=True)
                mm(tail_ps[:, NT * E:2 * NT * E], ones[:, :], oh, start=True, stop=True).then_inc(tail_full, 1)

            walk("pe", pe, dict(weights=weights, x_tokens=x_tokens, conv_qk=conv_qk, conv_v=conv_v, conv_max=conv_max,
                          conv_guard=conv_guard, conv_exp=conv_exp, conv_pv=conv_pv, a_channels=a_channels,
                          global_qk=global_qk, local_qkv=local_qkv, global_v=global_v, max_tile=max_tile,
                          guard=guard, score_tile=score_tile, pv_group=pv_group, o_tokens=o_tokens,
                          o_channels=o_channels, fuse1=fuse1, fuse2=fuse2, x1_channels=x1_channels, ffn1=ffn1,
                          ffn2=ffn2, n2_channels=n2_channels, logits=logits, ranks=ranks))

            after(pe, tail_free, B * (TAIL_TURNS + 2))
            with pe.Fori(0, E) as e:
                pe.wait_ge(erows_in, e * 16 + 16)
                for c, (lo, n) in enumerate(XT_CHUNKS):
                    if c != 1:
                        pe.wait_ge(ext_free, e * 3 + c // 2)
                    for i in range(n // P):
                        last = turn(bank[c % 2][:, i * P:(i + 1) * P], rows_e[:, lo // P + i, 0:C])
                    last.then_inc(ext_full, 1)
                pe.wait_ge(ew1_in, e * 16 + 16)
                for f in range(FC):
                    for c, (lo, n) in enumerate(XT_CHUNKS):
                        u = f * 3 + c
                        if f == 0:
                            pe.wait_ge(ext_free, e * 3 + c + 1)
                        if u >= 4:
                            pe.wait_ge(eh_free, e * FC * 3 + u - 3)
                        elif u == 0:
                            pe.wait_ge(eh_free, e * FC * 3)
                        mm(bank[2 + u % 4][:, 0:n], w1_e[:, f * P:(f + 1) * P], x_e[:, lo:lo + n],
                           start=True, stop=True).then_inc(eh_full, 1)
                pe.wait_ge(ew2_in, e * 16 + 16)
                pe.wait_ge(eh_free, (e + 1) * FC * 3)
                for c, (lo, n) in enumerate(XT_CHUNKS):
                    if c == 2:
                        pe.wait_ge(ey_free, e * 3 + 1)
                    elif c == 0:
                        pe.wait_ge(ey_free, e * 3)
                    for i in range(n // P):
                        for f in range(FC):
                            last = mm(bank[6 + c % 2][:, i * C:(i + 1) * C], hid_e[f][:, lo + i * P:lo + (i + 1) * P],
                                      w2_e[:, f, :], start=(f == 0), stop=(f == FC - 1))
                    last.then_inc(ey_full, 1)

            pe.wait_ge(ey_free, E * 3)
            with pe.Fori(0, 2 * B // ENDS) as r:
                for k in range(ENDS):
                    pe.wait_ge(fin_in[k], r * 16 + 16)
                    pe.wait_ge(fin_made[k], r)
                    for i in range(HT):
                        last = turn(bank[k][:, i * P:(i + 1) * P], fin_tok[k][:, i, :])
                    last.then_inc(fin_full[k], 1)

        @block.scalar
        def _(act):
            def to(dst, src, **kw):
                return nc.scalar.activation(dst, src, ACT.Identity if kw else ACT.Copy, **kw)

            act.wait_ge(weights_used, FIRST)

            def weights(b):
                act.wait_ge(weights_used, len(NAT) + 5)

            def x_tokens(b, h):
                ps, free = head_read(act, b, ("x_tokens", h))
                if h == 0 and not (isinstance(b, int) and b == 0):
                    after(act, kept, b * 32)
                to(t_tok[:, HT * h:HT * h + HT, :], ps[:, :].rearrange("p (t c) -> p t c", c=C))\
                    .then_inc(free, 1)

            def split_load(b, use, w, h, rows_, bias, scale):
                ps, free = head_read(act, b, use)
                if h == 0:
                    after(act, split_out, b * 48 + 16 * w)
                n = slice(h * HN, (h + 1) * HN)
                to(parts[0:rows_, 0, n], ps[0:rows_, :], bias=bias, scale=scale)
                to(split_x[0:rows_, n], ps[0:rows_, :], bias=bias, scale=scale)\
                    .then_inc(free, 1)

            def conv_qk(b, h):
                split_load(b, ("conv_qk", h), 0, h, 2 * D, cols[0:2 * D, COL["conv"]:COL["conv"] + 1], 1.0)

            def global_qk(b, w, h):
                if w == 0:
                    split_load(b, ("global_qk", w, h), 1, h, C, hcols[:, 0:1], 0.25)
                else:
                    split_load(b, ("global_qk", w, h), 2, h, C, cols[:, COL["gk"]:COL["gk"] + 1], 1.0)

            def conv_guard(b):
                ps, free = head_read(act, b, ("conv_guard",))
                after(act, cguard_in, b * 48)
                to(cneg_rows[:, :], ps[:, :].bitcast(BF16)[0:3 * NT, 0:P]).then_inc(free, 1)

            def conv_exp(b, h, j):
                ps, free = head_read(act, b, ("conv_exp", h, j))
                if j == 0 and not (isinstance(b, int) and b == 0 and h == 0):
                    head_filled(act, b - 1 if h == 0 else b, ("conv_pv", NT - 1 if h == 0 else HT - 1))
                nc.scalar.activation(cprob[:, j, :], ps[:, :], ACT.Exp).then_inc(free, 1)

            def a_channels(b, h):
                ps, free = head_read(act, b, ("a_channels", h))
                if h == 0 and not (isinstance(b, int) and b == 0):
                    tail_done(act, b - 1, ("global_v", 1))
                to(a_cm[:, h * HN:(h + 1) * HN], ps[:, :]).then_inc(free, 1)

            def split(b, w):
                r = slice(0, 2 * D if w == 0 else C)
                after(act, split_step, b * 9 + 3 * w + 1)
                to(parts[r, 1, :], split_x[r, :]).then_inc(split_step, 1)

            def normalise(dst, src, scale, shift_):
                for i in range(HT):
                    last = to(dst[:, i, 0:C], src[:, i, :], scale=scale[:, i:i + 1], bias=shift_[:, i:i + 1])
                return last

            def half(h):
                return slice(HT * h, HT * h + HT)

            def norm_t(b, h):
                if h == 0:
                    after(act, kept, b * 32)
                after(act, norm_rstd, b * 2 + h + 1)
                normalise(a_tok[:, half(h), :], t_tok[:, half(h), :], rstd, shift).then_inc(a_made, 1)

            def tail_normalise(b, k, src, dst):
                after(act, norm2_rstd, b * 6 + k + 1)
                normalise(dst, src, rstd2[:, k % 2], shift2[:, k % 2]).then_inc(normed, 1)

            def norm_u(b, h):
                tail_normalise(b, h, x1[:, half(h), :], x1[:, half(h), :])

            def norm_v(b, h):
                tail_normalise(b, 2 + h, x1[:, half(h), :], x1[:, half(h), :])

            def norm_t2(b, h):
                if h == 0 and not (isinstance(b, int) and b == 0):
                    after(act, rows_out, b * NT * 16)
                tail_normalise(b, 4 + h, x1[:, half(h), :], rows[:, half(h), :])

            def score_tile(b, quad, n):
                after(act, score_full, b * 2 * TILES + quad * TILES + n + 1)
                g, h = n // QH, n % QH
                if h == 0 and not (isinstance(b, int) and b == 0 and quad == 0 and g < 2):
                    after(act, pv_made, b * 2 * GROUPS + quad * GROUPS + g - 1)
                nc.scalar.activation(prob[:, g % 2, h, :], score_ps[n % 2][:, :], ACT.Exp).then_inc(exp_made, 1)

            def o_copy(b, quad, h):
                after(act, pv_made, b * 2 * GROUPS + quad * GROUPS + (h + 1) * NT)
                if not (isinstance(b, int) and b == 0):
                    tail_done(act, b - 1, ("o_tokens", quad, h))
                to(o_raw[:, quad, h, :], o_ps[:, :]).then_inc(o_copied, 1)

            def local_max(b, g):
                after(act, local_step, b * 28 + 7 * g + 4)
                nc.scalar.activation(ls[:, :, :, :], ls[:, :, :, :], ACT.Exp, scale=float(1.0 / np.sqrt(LD)))\
                    .then_inc(lexp_made, 1)

            def tail_wait(b, use):
                after(act, tail_full, tail_count(b, use) + 1)

            def o_channels(b, w, h):
                tail_wait(b, ("o_channels", w, h))
                to(y_cm[:, w, h * HN:(h + 1) * HN], tail_ps[:, :]).then_inc(tail_free, 1)

            def silu(b, use, count, bias):
                tail_wait(b, use)
                if not (isinstance(b, int) and b == 0 and count == 0):
                    after(act, hid_made, b * 8 + count)
                nc.scalar.activation(tanh_t[:, :], tail_ps[:, :], ACT.Tanh, bias=bias, scale=0.5)
                to(half_t[:, :], tail_ps[:, :], bias=bias, scale=0.5).then_inc(tail_free, 1)

            def fuse1(b, m, h):
                silu(b, ("fuse1", m, h), 2 * h + m, hcols[:, 1 + m:2 + m])

            def ffn1(b, m, h):
                silu(b, ("ffn1", m, h), 4 + 2 * h + m, hcols[:, 3 + m:4 + m])

            def x1_channels(b, h):
                tail_wait(b, ("x1_channels", h))
                to(y_cm[:, 0, h * HN:(h + 1) * HN], tail_ps[:, :]).then_inc(tail_free, 1)

            def n2_channels(b, h):
                tail_wait(b, ("n2_channels", h))
                to(y_cm[:, 1, h * HN:(h + 1) * HN], tail_ps[:, :]).then_inc(tail_free, 1)

            def ranks(b):
                after(act, route_step, b * ROUTE_STEPS + 2)
                nc.scalar.activation(lge[:, :, :], lg[:, :, :], ACT.Exp).then_inc(lexpert, 1)

            walk("act", act, dict(weights=weights, split=split, norm_t=norm_t, norm_u=norm_u, norm_v=norm_v, norm_t2=norm_t2,
                           x_tokens=x_tokens, conv_qk=conv_qk, conv_guard=conv_guard, conv_exp=conv_exp,
                           a_channels=a_channels, global_qk=global_qk, score_tile=score_tile, o_copy=o_copy,
                           local_max=local_max, o_channels=o_channels, fuse1=fuse1, x1_channels=x1_channels, ffn1=ffn1,
                           n2_channels=n2_channels, ranks=ranks))

            with act.Fori(0, E) as e:
                act.wait_ge(eh_free, e * FC * 3)
                to(b1_e[:, :], b1c[:, bass.ds(e * FC, FC)]).then_inc(eb1_made, 1)
                for c, (lo, n) in enumerate(XT_CHUNKS):
                    act.wait_ge(ext_full, e * 3 + c + 1)
                    if c == 0:
                        act.wait_ge(eh_full, e * FC * 3)
                    to(x_e[:, lo:lo + n], bank[c % 2][:, 0:n]).then_inc(ext_free, 1)
                for f in range(FC):
                    for c, (lo, n) in enumerate(XT_CHUNKS):
                        u = f * 3 + c
                        act.wait_ge(eh_full, e * FC * 3 + u + 1)
                        if u == 0:
                            act.wait_ge(ey_full, e * 3)
                            act.wait_ge(eb1_made, e + 1)
                        nc.scalar.activation(hid_e[f][:, lo:lo + n], bank[2 + u % 4][:, 0:n], ACT.Relu,
                                             bias=b1_e[:, f:f + 1]).then_inc(eh_free, 1)

            with act.Fori(0, 2 * B // ENDS) as r:
                for k in range(ENDS):
                    act.wait_ge(fin_full[k], r + 1)
                    act.wait_ge(fin_out[k], r * 16)
                    to(fin_cm[k], bank[k][:, :]).then_inc(fin_made[k], 1)
                    act.wait_ge(fin_made[k], r + 1)
                    act.dma_start(out_b[r * (ENDS // 2) + k // 2, :, k % 2 * HN:(k % 2 + 1) * HN], fin_cm[k])\
                       .then_inc(fin_out[k], 16)
            for k in range(ENDS):
                act.wait_ge(fin_out[k], 2 * B // ENDS * 16)

        @block.vector
        def _(dve):
            v = nc.vector
            def copy_weight(i):
                name, _, r = NAT[i]
                dve.wait_ge(weights_filled, i + 1)
                v.tensor_copy(TARGET[name], score_ps[i % 2][:, 0:r]).then_inc(weights_used, 1)

            for i in range(FIRST):
                copy_weight(i)
            dve.wait_ge(consts_made, 3)

            def weights(b):
                for i in range(FIRST, len(NAT)):
                    copy_weight(i)
                n = len(NAT)
                for k, w in enumerate((fgT, flT)):
                    dve.wait_ge(weights_filled, n + 1 + k)
                    v.tensor_copy(w[:, :], bank[6 + k][:, 0:2 * C]).then_inc(weights_used, 1)
                dve.wait_ge(weights_used, n)
                v.tensor_scalar(hcols[:, 0:1], cols[:, COL["gq"]:COL["gq"] + 1], 0.25, None, ALU.mult)\
                    .then_inc(weights_used, 1)
                v.tensor_scalar(hcols[:, 3:5], cols[:, COL["ffn0"]:COL["ffn0"] + 2], 0.5, None, ALU.mult)\
                    .then_inc(weights_used, 1)
                dve.wait_ge(weights_filled, n + 3)
                v.tensor_tensor(hcols[:, 5:7], bank[2][:, 0:2], cols[:, COL["fus0"]:COL["fus0"] + 2], ALU.add)\
                    .then_inc(const_dve, 1)
                dve.wait_ge(const_dve, 1)
                v.tensor_scalar(hcols[:, 1:3], hcols[:, 5:7], 0.5, None, ALU.mult).then_inc(weights_used, 1)

            def split(b, w):
                r = slice(0, 2 * D if w == 0 else C)
                uses = [("conv_qk",), ("global_qk", 0), ("global_qk", 1)][w]
                head_done(dve, b, (*uses, 1))
                n = b * 9 + 3 * w
                v.tensor_tensor(split_x[r, :], split_x[r, :], parts[r, 0, :], ALU.subtract).then_inc(split_step, 1)

            def split_low(b, w):
                r = slice(0, 2 * D if w == 0 else C)
                after(dve, split_step, b * 9 + 3 * w + 2)
                v.tensor_tensor(parts[r, 2, :], split_x[r, :], parts[r, 1, :], ALU.subtract).then_inc(split_step, 1)

            def conv_v(b, h):
                ps, free = head_read(dve, b, ("conv_v", h))
                v.tensor_tensor(cv_tok[:, HT * h:HT * h + HT, 0:C], ps[:, :].rearrange("p (t c) -> p t c", c=C),
                                bc[:, BC["bv"], None, :].to_broadcast([P, HT, C]), ALU.add)\
                    .then_inc(free, 1)

            def conv_max(b, t):
                ps, free = head_read(dve, b, ("conv_max", t))
                v.tensor_reduce(cmax[:, t // 2, t % 2:t % 2 + 1], ps[:, :], AX.X, ALU.max)\
                    .then_inc(free, 1)

            def neg_parts(maxima, neg, rest, parts_, step, n):
                v.tensor_reduce(neg, maxima, AX.X, ALU.max, negate=True).then_inc(step, 1)
                after(dve, step, n + 1)
                v.tensor_copy(parts_[:, 0, :], neg).then_inc(step, 1)
                after(dve, step, n + 2)
                v.tensor_tensor(rest, neg, parts_[:, 0, :], ALU.subtract).then_inc(step, 1)
                after(dve, step, n + 3)
                v.tensor_copy(parts_[:, 1, :], rest).then_inc(step, 1)
                after(dve, step, n + 4)
                v.tensor_tensor(rest, rest, parts_[:, 1, :], ALU.subtract).then_inc(step, 1)
                after(dve, step, n + 5)
                v.tensor_copy(parts_[:, 2, :], rest).then_inc(step, 1)

            def conv_guard(b):
                head_done(dve, b, ("conv_max", 2 * NT - 1))
                neg_parts(cmax[:, :, :], cneg[:, :], crest[:, :], cneg_parts, cguard_step, b * 6)

            def conv_pv(b, i):
                ps, free = head_read(dve, b, ("conv_pv", i))
                v.reciprocal(crecip[:, i:i + 1], ps[:, C:C + 1]).then_inc(crecip_made, 1)
                after(dve, crecip_made, b * NT + i + 1)
                if i == 0:
                    head_done(dve, b, ("x_tokens", 1))
                v.scalar_tensor_tensor(t_tok[:, i, :], ps[:, 0:C], crecip[:, i:i + 1], t_tok[:, i, :],
                                       ALU.mult, ALU.add).then_inc(free, 1)

            def statistics(src, st, made_sem):
                for i in range(HT):
                    last = v.bn_stats(st[:, i, :], src[:, i, :])
                last.then_inc(made_sem, 1)

            def stats_t(b, h):
                head_done(dve, b, ("conv_pv", HT * h + HT - 1))
                after(dve, norm_rstd, b * 2 + h)
                statistics(t_tok[:, HT * h:HT * h + HT, :], stats, stats_made)

            def local_qkv(b, i):
                ps, free = head_read(dve, b, ("local_qkv", i))
                if not (isinstance(b, int) and b == 0 and i < 2):
                    after(dve, lqkv_out[i % 2], b * HT * 32 + i // 2 * 32)
                v.tensor_tensor(lqkv[:, i % 2, :], ps[:, 0:3 * C],
                                bc[:, BC["lq"]:BC["lv"] + 1, :].rearrange("p a c -> p (a c)"), ALU.add)\
                    .then_inc(free, 1)

            def global_v(b, h):
                after(dve, tail_full, tail_count(b, ("global_v", h)) + 1)
                if h == 0:
                    after(dve, pv_made, b * 2 * GROUPS)
                v.tensor_tensor(v_tok[:, HT * h:HT * h + HT, :, 0:D],
                                tail_ps[:, :].rearrange("p (t h d) -> p t h d", h=HEADS, d=D),
                                bc[:, BC["gv"], :].rearrange("p (h d) -> p h d", d=D)[:, None, :, :]
                                .to_broadcast([P, HT, HEADS, D]), ALU.add).then_inc(tail_free, 1)

            def max_tile(b, quad, n):
                after(dve, max_full, b * 2 * (TILES + 1) + quad * (TILES + 1) + n + 1)
                h, i, j = n // (2 * NT), n // 2 % NT, n % 2
                v.tensor_reduce(gmax[:, h, i, j:j + 1], max_ps[max_bank(n)][:, :], AX.X, ALU.max)\
                    .then_inc(max_free, 1)

            def guard(b, quad):
                u = b * 2 * (TILES + 1) + quad * (TILES + 1)
                after(dve, max_free, u + TILES)
                neg_parts(gmax[:, :, :, :].rearrange("p h t j -> p (h t) j"), gneg[:, :], grest[:, :], gneg_parts,
                          guard_step, b * 12 + quad * 6)

            def guard_rows(b, quad):
                after(dve, max_full, (b * 2 + quad + 1) * (TILES + 1))
                if quad == 0:
                    after(dve, guard_in[1], b * 48)
                else:
                    after(dve, guard_in[0], (b + 1) * 48)
                v.tensor_copy(gneg_rows[:, :], max_ps[max_bank(TILES)][:, :].bitcast(BF16)[0:3 * QH * NT, 0:P])\
                    .then_inc(max_free, 1)

            def tail_wait(b, use):
                after(dve, tail_full, tail_count(b, use) + 1)

            def o_tokens(b, quad, h):
                tail_wait(b, ("o_tokens", quad, h))
                ps = tail_ps[:, :].rearrange("p (t h c) -> p t h c", h=QH, c=CG)
                n = b * 4 + quad * 2 + h
                v.reciprocal(grecip[:, :, :], ps[:, :, :, D]).then_inc(grecip_made, 1)
                after(dve, grecip_made, n + 1)
                v.tensor_tensor(og_tok[:, HT * h:HT * h + HT, quad, :, :], ps[:, :, :, 0:D],
                                grecip[:, :, :, None].to_broadcast([P, HT, QH, D]), ALU.mult)\
                    .then_inc(tail_free, 1)

            def local_max(b, g):
                n = b * 28 + 7 * g
                after(dve, lprod_made, b * 4 + g + 1)
                v.tensor_reduce(ls[:, :, :, :].rearrange("p i w h -> p (i w h)"),
                                lprod[:, :, :, :].rearrange("p i w (h d) -> p (i w h) d", d=LD), AX.X, ALU.add)\
                    .then_inc(local_step, 1)
                after(dve, local_step, n + 1)
                v.tensor_tensor(ls[:, :, :, :], ls[:, :, :, :], lmask[:, 2 * g:2 * g + 2, :, :], ALU.add)\
                    .then_inc(local_step, 1)
                after(dve, local_step, n + 2)
                v.tensor_reduce(lmx[:, :, :], ls[:, :, :, :].rearrange("p i w h -> p i h w"), AX.X, ALU.max)\
                    .then_inc(local_step, 1)
                after(dve, local_step, n + 3)
                v.tensor_tensor(ls[:, :, :, :], ls[:, :, :, :], lmx[:, :, None, :].to_broadcast([P, 2, WIN, LH]),
                                ALU.subtract).then_inc(local_step, 1)

            def local_sum(b, g):
                n = b * 28 + 7 * g
                after(dve, lexp_made, b * 4 + g + 1)
                v.tensor_reduce(lsum[:, :, :], ls[:, :, :, :].rearrange("p i w h -> p i h w"), AX.X, ALU.add)\
                    .then_inc(local_step, 1)
                after(dve, local_step, n + 5)
                v.reciprocal(lsum[:, :, :], lsum[:, :, :]).then_inc(local_step, 1)
                after(dve, local_step, n + 6)
                v.tensor_tensor(ls[:, :, :, :], ls[:, :, :, :], lsum[:, :, None, :].to_broadcast([P, 2, WIN, LH]),
                                ALU.mult).then_inc(local_step, 1)

            def local_out(b, g):
                after(dve, lpv_made, b * 4 + g + 1)
                if g == 0 and not (isinstance(b, int) and b == 0):
                    after(dve, tail_full, tail_count(b - 1, ("o_channels", 1, 1)) + 1)
                v.tensor_reduce(ol_tok[:, 2 * g:2 * g + 2, :],
                                lprod[:, :, :, :].rearrange("p i w c -> p i c w"), AX.X, ALU.add).then_inc(ol_made, 1)

            def silu(b, use, m, h):
                tail_done(dve, b, use)
                v.scalar_tensor_tensor(hid[:, m, h * HN:(h + 1) * HN], tanh_t[:, :], 1.0, half_t[:, :],
                                       ALU.add, ALU.mult).then_inc(hid_made, 1)

            def fuse1(b, m, h):
                silu(b, ("fuse1", m, h), m, h)

            def ffn1(b, m, h):
                silu(b, ("ffn1", m, h), m, h)

            def residual(b, use, h):
                tail_wait(b, use)
                t = slice(HT * h, HT * h + HT)
                v.tensor_tensor(x1[:, t, :], tail_ps[:, :].rearrange("p (t c) -> p t c", c=C), a_old[:, t, :],
                                ALU.add).then_inc(tail_free, 1)

            def fuse2(b, h):
                after(dve, bias_added, b + 1)
                if h == 0:
                    after(dve, t2_out, b * 16)
                    after(dve, normed, b * 6)
                residual(b, ("fuse2", h), h)

            def ffn2(b, h):
                after(dve, x1_bias, b * 2 + h + 1)
                residual(b, ("ffn2", h), h)

            def tail_statistics(b, k, h):
                after(dve, norm2_rstd, b * 6 + max(k - 1, 0))
                statistics(x1[:, HT * h:HT * h + HT, :], stats2[:, h], stats2_made)

            def stats_u(b, h):
                tail_done(dve, b, ("fuse2", h))
                tail_statistics(b, h, h)

            def stats_v(b, h):
                tail_done(dve, b, ("ffn2", h))
                tail_statistics(b, 2 + h, h)

            def stats_t2(b, h):
                after(dve, t2_made, b * 2 + h + 1)
                tail_statistics(b, 4 + h, h)

            def logits(b):
                tail_wait(b, ("logits",))
                n = b * ROUTE_STEPS
                k = [0]

                def step(ins):
                    k[0] += 1
                    ins.then_inc(route_step, 1)
                    after(dve, route_step, n + k[0])

                v.tensor_tensor(lg[:, :, :], tail_ps[:, 0:NT * E].rearrange("p (t e) -> p t e", e=E),
                                gate_bc[:, None, :].to_broadcast([P, NT, E]), ALU.add)\
                    .then_inc(tail_free, 1)
                tail_done(dve, b, ("logits",))
                step(v.tensor_reduce(lgm[:, :], lg[:, :, :], AX.X, ALU.max))
                step(v.tensor_tensor(lg[:, :, :], lg[:, :, :], lgm[:, :, None].to_broadcast([P, NT, E]), ALU.subtract))
                step(v.tensor_scalar(cand[:, :, :], lg[:, :, :], 0.0, FAR, ALU.is_lt, ALU.mult))
                step(v.tensor_tensor(cand[:, :, :], cand[:, :, :], experts[:, None, :].to_broadcast([P, NT, E]),
                                     ALU.add))
                step(v.tensor_reduce(idx[:, :], cand[:, :, :], AX.X, ALU.min))
                step(v.tensor_tensor(onehot[:, :, :], experts[:, None, :].to_broadcast([P, NT, E]),
                                     idx[:, :, None].to_broadcast([P, NT, E]), ALU.is_equal))
                assert k[0] == ONEHOT_STEP

            def ranks(b):
                n = b * ROUTE_STEPS
                k = [ONEHOT_STEP]

                def step(ins):
                    k[0] += 1
                    ins.then_inc(route_step, 1)
                    after(dve, route_step, n + k[0])

                after(dve, lexpert, b + 1)
                step(v.tensor_reduce(lgm[:, :], lge[:, :, :], AX.X, ALU.add))
                step(v.reciprocal(rows[:, :, C], lgm[:, :]))
                step(v.tensor_copy(rows[:, :, C + 1], token_no[:, :]))
                step(v.tensor_scalar(token_no[:, :], token_no[:, :], float(N), None, ALU.add))
                tail_wait(b, ("ranks",))
                tot = tail_ps[:, NT * E:2 * NT * E].rearrange("p (t e) -> p t e", e=E)
                for t in range(NT):
                    step(v.tensor_tensor(cum[:, t + 1, :], cum[:, t, :], tot[:, t, :], ALU.add))
                step(v.tensor_tensor(cand[:, :, :], cum[:, 0:NT, :],
                                     tail_ps[:, 0:NT * E].rearrange("p (t e) -> p t e", e=E), ALU.add))
                v.tensor_copy(cum[:, 0, :], cum[:, NT, :]).then_inc(tail_free, 1)
                step(v.tensor_tensor(cand[:, :, :], cand[:, :, :], onehot[:, :, :], ALU.mult))
                step(v.tensor_reduce(rank[:, :], cand[:, :, :], AX.X, ALU.add))
                step(v.tensor_scalar(over[:, :], rank[:, :], float(CAP), STEP_UP, ALU.is_gt, ALU.mult))
                step(v.scalar_tensor_tensor(rank[:, :], idx[:, :], float(CAP), rank[:, :], ALU.mult, ALU.add))
                v.scalar_tensor_tensor(slot[:, :], rank[:, :], -1.0, over[:, :], ALU.add, ALU.add).then_inc(routed, 1)
                assert k[0] == ROUTE_STEPS, k[0]

            walk("dve", dve, dict(weights=weights, split=split, split_low=split_low, conv_v=conv_v, conv_max=conv_max, conv_guard=conv_guard, conv_pv=conv_pv,
                           stats_t=stats_t, local_qkv=local_qkv, global_v=global_v,
                           max_tile=max_tile, guard=guard, guard_rows=guard_rows, o_tokens=o_tokens, local_max=local_max,
                           local_sum=local_sum, local_out=local_out, fuse1=fuse1, ffn1=ffn1, fuse2=fuse2,
                           ffn2=ffn2, stats_u=stats_u, stats_v=stats_v, 
                           stats_t2=stats_t2, logits=logits, ranks=ranks))

            with dve.Fori(1, E + 1) as nth:
                e = nth - 1
                dve.wait_ge(erows_in, e * 16 + 16)
                dve.wait_ge(ey_out, e * CT * 16)
                v.tensor_copy(prob_e[:, :], rows_e[:, :, C])
                v.tensor_copy(token_e[:, :], rows_e[:, :, C + 1]).then_inc(etaken, 1)
                dve.wait_ge(eb2_in, e * 16 + 16)
                dve.wait_ge(etaken, nth)
                for c, (lo, n) in enumerate(XT_CHUNKS):
                    dve.wait_ge(ey_full, e * 3 + c + 1)
                    t0, nt = lo // P, n // P
                    y = y_e[:, t0:t0 + nt, :]
                    v.tensor_tensor(y, bank[6 + c % 2][:, 0:n].rearrange("p (t c) -> p t c", c=C),
                                    b2_e[:, 0:1, :].to_broadcast([P, nt, C]), ALU.add).then_inc(ey_free, 1)
                    dve.wait_ge(ey_free, e * 3 + c + 1)
                    v.tensor_tensor(y, y, prob_e[:, t0:t0 + nt, None].to_broadcast([P, nt, C]), ALU.mult)\
                        .then_inc(ey_step, 1)
                    dve.wait_ge(ey_step, e * 3 + c + 1)
                    odd = [odd_e[:, k, 0:n].rearrange("p (t c) -> p t c", c=C) for k in range(3)]
                    v.tensor_tensor(odd[0], y, y, ALU.not_equal)
                    v.tensor_scalar(odd[1], y, MAX_F32, None, ALU.is_gt)
                    v.tensor_scalar(odd[2], y, -MAX_F32, None, ALU.is_lt).then_inc(ey_odd[c], 1)
                    dve.wait_ge(consts_made, 3)
                    dve.wait_ge(ey_odd[c], nth)
                    for k in range(3):
                        v.copy_predicated(y, odd[k], huge[:, k:k + 1, None].to_broadcast([P, nt, C]))\
                            .then_inc(ey_made[c] if k == 2 else ey_pass[c][k], 1)
                        if k < 2:
                            dve.wait_ge(consts_made, 3)
                            dve.wait_ge(ey_pass[c][k], nth)


_INS = ["x", "L0_conv_wq", "L0_conv_bq", "L0_conv_wk", "L0_conv_bk", "L0_conv_wv", "L0_conv_bv",
        "L1_attn_g_in_w", "L1_attn_g_in_b", "L1_attn_g_out_w", "L1_attn_g_out_b",
        "L1_attn_t_in_w", "L1_attn_t_in_b", "L1_attn_t_out_w", "L1_attn_t_out_b",
        "L1_attn_fus_w1", "L1_attn_fus_b1", "L1_attn_fus_w2", "L1_attn_fus_b2",
        "L1_attn_ffn_w1", "L1_attn_ffn_b1", "L1_attn_ffn_w2", "L1_attn_ffn_b2",
        "L1_attn_gn_g", "L1_attn_gn_b", "L1_attn_fn_g", "L1_attn_fn_b",
        "L1_ffn_gate_w", "L1_ffn_gate_b", "L1_ffn_w1", "L1_ffn_b1", "L1_ffn_w2", "L1_ffn_b2"]
_OUTS = [((B, C, 32, 32), "float32")]


def kernel(**inputs):
    import numpy as _np
    import concourse.bacc as _bacc
    from concourse import mybir as _mybir
    from concourse.bass_utils import run_bass_kernel_spmd as _run

    nc = _bacc.Bacc("TRN2", target_bir_lowering=False, num_devices=1)
    arrays, args = {}, []
    for name in _INS:
        a = _np.ascontiguousarray(inputs[name])
        arrays[f"in_{name}_dram"] = a
        args.append(nc.dram_tensor(f"in_{name}_dram", a.shape, _mybir.dt.from_np(a.dtype), kind="ExternalInput").ap())
    for i, (shape, dtype) in enumerate(_OUTS):
        dt = _mybir.dt.from_np(_np.dtype(dtype))
        args.append(nc.dram_tensor(f"out_{i}_dram", shape, dt, kind="ExternalOutput").ap())
    hybrid_kernel(nc, *args)
    r = _run(nc, [arrays], core_ids=[0])
    return r.results[0]["out_0_dram"]
```
